# Optimizing a Trainium2 kernel written in Bass

```python
import numpy as np
import jax
import jax.numpy as jnp

def _softmax(x, axis=-1):
    return jax.nn.softmax(x, axis=axis)

def _gelu(x):
    return jax.nn.gelu(x, approximate=True)

def _silu(x):
    return jax.nn.silu(x)

def _sigmoid(x):
    return jax.nn.sigmoid(x)

def _layernorm(x, axis=-1, eps=1e-05):
    m = jnp.mean(x, axis=axis, keepdims=True)
    v = jnp.var(x, axis=axis, keepdims=True)
    return (x - m) / jnp.sqrt(v + eps)

def _scatter_add(tgt, idx, src, axis=0):
    return tgt.at[idx].add(src)

def _segment_sum(src, seg, n):
    return jax.ops.segment_sum(src, seg, n)
kernel_name = 'mk_lm_tower_d1_tok_ids1024_r4_dd8af0'

def setup_inputs(seed: int=0):
    np.random.seed(seed)
    _w = jnp.asarray

    def _rec_inputs():
        import jax
        import jax.numpy as jnp
        _rk = jax.random.key(seed)
        x = jax.random.randint(jax.random.fold_in(_rk, 1), (4, 1024), 0, 250, jnp.int32)
        return x
    x = _rec_inputs()

    def _L0_tok_setup():
        import math
        import jax, jax.numpy as jnp
        import numpy as np
        PAD_IDX = 1
        SEP_ID = 4
        STARTPOS = 1025
        BSZ, SEQ_LEN, EMBED_DIM = (32, 1024, 256)

        def _build_table(num_cons, dim, padding_idx, startpos):
            half = dim // 2
            freqs = jnp.exp(jnp.arange(half, dtype=jnp.float32) * -(math.log(10000.0) / (half - 1)))
            ang = jnp.arange(startpos, startpos + num_cons, dtype=jnp.float32)[:, None] * freqs[None, :]
            tab = jnp.concatenate([jnp.sin(ang), jnp.cos(ang)], axis=1)
            return tab.at[padding_idx].set(0.0)

        def _positions(tokens):
            L = tokens.shape[1]
            valid = jnp.cumprod((tokens != PAD_IDX).astype(jnp.int32), axis=1).astype(bool)
            j = jnp.arange(L, dtype=jnp.int32)
            sep_j = jnp.where(tokens == SEP_ID, j, 0)
            last_sep = jax.lax.associative_scan(jnp.maximum, sep_j, axis=1)
            pos = j - last_sep + 2
            return jnp.where(valid, pos, 1)
        key = jax.random.key(seed)
        tokens = jax.random.randint(key, (BSZ, SEQ_LEN), 0, 250, dtype=jnp.int64)
        num_cons = PAD_IDX + 1 + SEQ_LEN
        weights = _build_table(num_cons, EMBED_DIM, PAD_IDX, STARTPOS)
        return {'input': tokens, 'weights': weights}
    _L0_tok_all = _L0_tok_setup()
    _L0_tok_in = {k: v for k, v in _L0_tok_all.items() if k in ('weights',)}
    del _L0_tok_all

    def _L0_attn_setup():
        import jax, jax.numpy as jnp
        import numpy as np
        B, T, C = (64, 64, 256)
        N_HEAD, HEAD_SIZE, KV_RANK = (16, 64, 128)
        BLOCK_SIZE = 64
        key = jax.random.key(seed)
        ks = jax.random.split(key, 5)
        HD = N_HEAD * HEAD_SIZE

        def init(k, shape):
            fan_in = shape[0]
            bound = 1.0 / np.sqrt(fan_in)
            return jax.random.uniform(k, shape, jnp.float32, -bound, bound)
        return {'x': jax.random.normal(ks[0], (B, T, C), jnp.float32), 'w_kv_down': init(ks[1], (C, KV_RANK)), 'w_kv_up': init(ks[2], (KV_RANK, 2 * HD)), 'w_q': init(ks[3], (C, HD)), 'w_out': init(ks[4], (HD, C))}
    _L0_attn_all = _L0_attn_setup()
    _L0_attn_in = {k: v for k, v in _L0_attn_all.items() if k in ('w_kv_down', 'w_kv_up', 'w_q', 'w_out')}
    del _L0_attn_all

    def _L0_ffn_setup():
        import jax, jax.numpy as jnp
        import numpy as np

        def _bitlinear(x, w_latent):
            scale = jax.lax.stop_gradient(jnp.clip(jnp.mean(jnp.abs(w_latent), axis=1, keepdims=True), 1e-05, None))
            tern = jnp.clip(jnp.round(w_latent / scale), -1.0, 1.0)
            w = w_latent + jax.lax.stop_gradient(tern - w_latent)
            return x @ (w * scale).T
        key = jax.random.key(seed)
        ks = jax.random.split(key, 6)
        dim, hidden, rank = (256, 1024, 16)
        B, S = (4, 1024)
        x = jax.random.normal(ks[0], (B, S, dim), dtype=jnp.float32)
        w_fc = 0.02 * jax.random.normal(ks[1], (hidden, dim), dtype=jnp.float32)
        w_proj = 0.02 * jax.random.normal(ks[2], (dim, hidden), dtype=jnp.float32)
        u = 0.02 * jax.random.normal(ks[3], (hidden, rank), dtype=jnp.float32)
        v = 0.02 * jax.random.normal(ks[4], (rank, dim), dtype=jnp.float32)
        fast_b = jax.random.normal(ks[5], (rank, rank), dtype=jnp.float32)
        gate = jnp.float32(0.05)
        return {'x': x, 'fast_b': fast_b, 'w_fc': w_fc, 'w_proj': w_proj, 'u': u, 'v': v, 'gate': gate}
    _L0_ffn_all = _L0_ffn_setup()
    _L0_ffn_in = {k: v for k, v in _L0_ffn_all.items() if k in ('fast_b', 'w_fc', 'w_proj', 'u', 'v', 'gate')}
    del _L0_ffn_all
    return {'x': x, 'L0_tok_weights': _L0_tok_in['weights'], 'L0_attn_w_kv_down': _L0_attn_in['w_kv_down'], 'L0_attn_w_kv_up': _L0_attn_in['w_kv_up'], 'L0_attn_w_q': _L0_attn_in['w_q'], 'L0_attn_w_out': _L0_attn_in['w_out'], 'L0_ffn_fast_b': _L0_ffn_in['fast_b'], 'L0_ffn_w_fc': _L0_ffn_in['w_fc'], 'L0_ffn_w_proj': _L0_ffn_in['w_proj'], 'L0_ffn_u': _L0_ffn_in['u'], 'L0_ffn_v': _L0_ffn_in['v'], 'L0_ffn_gate': _L0_ffn_in['gate']}

def reference(x, L0_tok_weights, L0_attn_w_kv_down, L0_attn_w_kv_up, L0_attn_w_q, L0_attn_w_out, L0_ffn_fast_b, L0_ffn_w_fc, L0_ffn_w_proj, L0_ffn_u, L0_ffn_v, L0_ffn_gate):
    import jax
    import jax.numpy as jnp

    def _L0_tok_ref(input, weights):
        import math
        import jax, jax.numpy as jnp
        import numpy as np
        PAD_IDX = 1
        SEP_ID = 4
        STARTPOS = 1025
        BSZ, SEQ_LEN, EMBED_DIM = (32, 1024, 256)

        def _build_table(num_cons, dim, padding_idx, startpos):
            half = dim // 2
            freqs = jnp.exp(jnp.arange(half, dtype=jnp.float32) * -(math.log(10000.0) / (half - 1)))
            ang = jnp.arange(startpos, startpos + num_cons, dtype=jnp.float32)[:, None] * freqs[None, :]
            tab = jnp.concatenate([jnp.sin(ang), jnp.cos(ang)], axis=1)
            return tab.at[padding_idx].set(0.0)

        def _positions(tokens):
            L = tokens.shape[1]
            valid = jnp.cumprod((tokens != PAD_IDX).astype(jnp.int32), axis=1).astype(bool)
            j = jnp.arange(L, dtype=jnp.int32)
            sep_j = jnp.where(tokens == SEP_ID, j, 0)
            last_sep = jax.lax.associative_scan(jnp.maximum, sep_j, axis=1)
            pos = j - last_sep + 2
            return jnp.where(valid, pos, 1)
        pos = _positions(input)
        return jnp.take(weights, pos, axis=0)

    def _L0_attn_ref(x, w_kv_down, w_kv_up, w_q, w_out):
        import jax, jax.numpy as jnp
        import numpy as np
        B, T, C = (64, 64, 256)
        N_HEAD, HEAD_SIZE, KV_RANK = (16, 64, 128)
        BLOCK_SIZE = 64
        Bx, Tx, Cx = x.shape
        HD = N_HEAD * HEAD_SIZE
        latent_kv = x @ w_kv_down
        kv = latent_kv @ w_kv_up
        k, v = (kv[..., :HD], kv[..., HD:])
        k = k.reshape(Bx, Tx, N_HEAD, HEAD_SIZE)
        v = v.reshape(Bx, Tx, N_HEAD, HEAD_SIZE)
        q = (x @ w_q).reshape(Bx, Tx, N_HEAD, HEAD_SIZE)
        scale = HEAD_SIZE ** (-0.5)
        att = jnp.einsum('bqhd,bkhd->bhqk', q, k) * scale
        causal = jnp.tril(jnp.ones((Tx, Tx), dtype=bool))
        att = jnp.where(causal, att, -jnp.inf)
        att = jax.nn.softmax(att, axis=-1)
        y = jnp.einsum('bhqk,bkhd->bqhd', att, v)
        y = y.reshape(Bx, Tx, HD)
        return y @ w_out

    def _L0_ffn_ref(x, fast_b, w_fc, w_proj, u, v, gate):
        import jax, jax.numpy as jnp
        import numpy as np

        def _bitlinear(x, w_latent):
            scale = jax.lax.stop_gradient(jnp.clip(jnp.mean(jnp.abs(w_latent), axis=1, keepdims=True), 1e-05, None))
            tern = jnp.clip(jnp.round(w_latent / scale), -1.0, 1.0)
            w = w_latent + jax.lax.stop_gradient(tern - w_latent)
            return x @ (w * scale).T
        h = _bitlinear(x, w_fc) + gate * (x @ v.T @ fast_b.T @ u.T)
        r = jnp.maximum(h, 0.0)
        return _bitlinear(r * r, w_proj)
    h = _L0_tok_ref(x, L0_tok_weights)
    h = h + _L0_attn_ref(_layernorm(h, axis=-1), L0_attn_w_kv_down, L0_attn_w_kv_up, L0_attn_w_q, L0_attn_w_out)
    h = h + _L0_ffn_ref(_layernorm(h, axis=-1), L0_ffn_fast_b, L0_ffn_w_fc, L0_ffn_w_proj, L0_ffn_u, L0_ffn_v, L0_ffn_gate)
    return h

_drawn_inputs = setup_inputs


def setup_inputs(seed=0):
    import zlib

    import numpy as np

    out = dict(_drawn_inputs(seed))
    spreads = {}
    factors = {'L0_attn_w_q': 25.92, 'L0_ffn_fast_b': 8.0, 'L0_ffn_u': 8.0, 'L0_ffn_v': 8.0}
    for name, (base, spread) in spreads.items():
        noise = np.random.default_rng([zlib.crc32(name.encode()), seed]).standard_normal(out[name].shape)
        drawn = base * np.exp(spread * noise) if base else spread * noise
        out[name] = jnp.asarray(drawn.astype(out[name].dtype))
    for name, factor in factors.items():
        out[name] = (out[name] * factor).astype(out[name].dtype)
    return out
```

```python
from contextlib import ExitStack

import concourse.bass as bass
from concourse import mybir

F32 = mybir.dt.float32
F16 = mybir.dt.float16
BF16 = mybir.dt.bfloat16
I32 = mybir.dt.int32
U32 = mybir.dt.uint32
ALU = mybir.AluOpType
ACT = mybir.ActivationFunctionType
AX_X = mybir.AxisListType.X

P = 128
BANK = 512
PAD_TOKEN, SEP_TOKEN = 1, 4
EPS = 1e-5
X_SCALE = 64.0
W_TOP = 64.0
LAT_SHIFT = 2.0 ** -6
Q_SHIFT = 2.0 ** -9
KV_SHIFT = 2.0 ** -17
ONE_ROW = 2.0 ** 15
P_BIAS = 6.931471805599453
H_SHIFT = 2.0 ** -14
EXP_BITS = 0x7F800000


def layer_kernel(nc, tokens, table, w_kvd, w_kvu, w_q, w_out, fast_b, w_fc, w_proj, u, v, gate, out):
    B, T = tokens.shape
    C = table.shape[1]
    R = w_kvd.shape[1]
    HID = w_fc.shape[0]
    RANK = fast_b.shape[0]
    HD = 64
    NH = w_q.shape[1] // HD
    KC = C // P
    TT = T // P
    NT = B * TT
    KH = HID // P
    NP = NH // 2
    TOK = B * T
    GROUPS = TOK // BANK
    assert R == P and T == 2 * BANK and C == 256 and NH * HD == HID

    embed_scr = nc.dram_tensor("embed_scr", [TOK, C], F32, kind="Internal").ap()
    wf_scr = nc.dram_tensor("wf_scr", [P, 2 * KC * HID], F16, kind="Internal").ap()
    wp_scr = nc.dram_tensor("wp_scr", [P, 2 * KH * C], F16, kind="Internal").ap()
    wo_scr = nc.dram_tensor("wo_scr", [P, 2 * KH * C], F16, kind="Internal").ap()
    y_scr = nc.dram_tensor("y_scr", [B, 2, P, NP, 2 * BANK], F16, kind="Internal").ap()

    def batch_and_pair(pr):
        if isinstance(pr, int):
            return pr // NP, pr % NP
        return (pr >> 3).with_bounds(min_val=0, max_val=B - 1), (pr & 7).with_bounds(min_val=0, max_val=NP - 1)

    with ExitStack() as whole:
        def sb(ctx, name, shape, dt):
            return ctx.enter_context(nc.sbuf_tensor(name, shape, dt))

        def sem(name):
            return whole.enter_context(nc.semaphore(name))

        ps = whole.enter_context(nc.psum_tensor("ps", [P, 8, BANK], F32))
        ident = sb(whole, "ident", [P, P], F32)
        ident_big = sb(whole, "ident_big", [P, P], F16)
        causal = sb(whole, "causal", [P, P], F16)
        coef = sb(whole, "coef", [P, 4], F32)

        att = whole.enter_context(ExitStack())
        xT = sb(att, "xT", [P, 2, KC, TOK], F16)
        latT = sb(att, "latT", [P, 2, TOK], F16)
        wq = sb(att, "wq", [P, 2, KC, NH * HD], F16)
        wkvu = sb(att, "wkvu", [P, 2, 2 * NH * HD], F16)

        with ExitStack() as pre:
            emb = sb(pre, "emb", [P, NT, C], F32)

            def row(n):
                return emb[0:B, 4 * n:4 * (n + 1), :].rearrange("b i c -> b (i c)")

            tok_i = row(0).bitcast(I32)
            tok_f, col, keep, valid, sep_at, last_sep, pos = (row(n) for n in range(1, 8))
            pos_idx = sb(pre, "pos_idx", [P, TT, B], U32)
            stats = sb(pre, "stats", [P, NT, 6], F32)
            mv = sb(pre, "mv", [P, NT, 2], F32)
            var = sb(pre, "var", [P, NT], F32)
            std = sb(pre, "std", [P, NT], F32)
            rstd = sb(pre, "rstd", [P, NT], F32)
            tmp = sb(pre, "tmp", [P, NT], F32)
            xn = sb(pre, "xn", [P, 2, 4, C], F32)
            wq_f = sb(pre, "wq_f", [P, KC, NH * HD], F32)
            wkvd_f = sb(pre, "wkvd_f", [P, KC, R], F32)
            wkvu_f = sb(pre, "wkvu_f", [P, 2 * NH * HD], F32)
            wo_f = sb(pre, "wo_f", [P, KH, C], F32)
            wfc_f = sb(pre, "wfc_f", [P, KH, C], F32)
            wpr_f = sb(pre, "wpr_f", [P, KC, HID], F32)
            tern = sb(pre, "tern", [P, 2 * KH * C], F32)
            half_scale = sb(pre, "half_scale", [P, 2, KH], F32)
            row_scale = sb(pre, "row_scale", [P, KH + KC], F32)
            wkvd = sb(pre, "wkvd", [P, 2, KC, R], F16)
            wo16 = sb(pre, "wo16", [P, 2, KH, C], F16)
            wf16 = sb(pre, "wf16", [P, 2, KC, HID], F16)
            wp16 = sb(pre, "wp16", [P, 2, KH, C], F16)
            u_f = sb(pre, "u_f", [P, KH, RANK], F32)
            uT = sb(pre, "uT", [RANK, HID], F32)
            v_f = sb(pre, "v_f", [RANK, C], F32)
            fbT = sb(pre, "fbT", [RANK, RANK], F32)
            fbv = sb(pre, "fbv", [RANK, C], F32)
            gate_b = sb(pre, "gate_b", [P, 1], F32)
            top = sb(pre, "top", [P, 6], F32)
            top_all = sb(pre, "top_all", [P, 6], F32)
            pow2 = sb(pre, "pow2", [P, 6], F32)
            winv = sb(pre, "winv", [P, 6], F32)
            KVD, KVU, WQ, WO, WF, WP = range(6)

            tokens_in = sem("tokens_in")
            proj_w_in = sem("proj_w_in")
            ffn_w_in = sem("ffn_w_in")
            small_in = sem("small_in")
            consts_set = sem("consts_set")
            dve_step = sem("dve_step")
            pos_ready = sem("pos_ready")
            posT_ready = sem("posT_ready")
            idx_ready = sem("idx_ready")
            rows_in = sem("rows_in")
            top_ready = sem("top_ready")
            top_shared = sem("top_shared")
            winv_ready = sem("winv_ready")
            w_hi = sem("w_hi")
            w_lo = sem("w_lo")
            uT_ready = sem("uT_ready")
            uT_copied = sem("uT_copied")
            fbv_ready = sem("fbv_ready")
            fbv_copied = sem("fbv_copied")
            low_rank = sem("low_rank")
            fc_full = sem("fc_full")
            fcT_ready = sem("fcT_ready")
            proj_full = sem("proj_full")
            projT_ready = sem("projT_ready")
            var_ready = sem("var_ready")
            std_ready = sem("std_ready")
            xn_ready = sem("xn_ready")
            xT_ps = sem("xT_ps")
            xT_hi = sem("xT_hi")
            xT_lo = sem("xT_lo")
            lat_ps = sem("lat_ps")
            lat_hi = sem("lat_hi")
            lat_lo = sem("lat_lo")
            scratch_out = sem("scratch_out")

            with nc.Block() as block:
                @block.sync
                def _(sp):
                    sp.dma_start(tok_i[:, :], tokens).then_inc(tokens_in, 16)
                    sp.dma_start(wkvd_f[:, :, :], w_kvd.rearrange("(k p) n -> p k n", p=P)).then_inc(proj_w_in, 16)
                    sp.dma_start(wkvu_f[:, :], w_kvu).then_inc(proj_w_in, 16)
                    sp.dma_start(wq_f[:, :, :], w_q.rearrange("(k p) n -> p k n", p=P)).then_inc(proj_w_in, 16)
                    sp.dma_start(wo_f[:, :, :], w_out.rearrange("(k p) n -> p k n", p=P)).then_inc(proj_w_in, 16)
                    sp.dma_start(wfc_f[:, :, :], w_fc.rearrange("(k p) n -> p k n", p=P)).then_inc(ffn_w_in, 16)
                    sp.dma_start(wpr_f[:, :, :], w_proj.rearrange("(k p) n -> p k n", p=P)).then_inc(ffn_w_in, 16)
                    sp.dma_start(u_f[:, :, :], u.rearrange("(k p) r -> p k r", p=P)).then_inc(small_in, 16)
                    sp.dma_start(v_f[:, :], v).then_inc(small_in, 16)
                    sp.dma_start(fbT[:, :], fast_b.rearrange("s r -> r s"),
                                 allow_slow_non_contiguous=True).then_inc(small_in, 16)
                    sp.dma_start(gate_b[:, :], gate.rearrange("(a b) -> a b", b=1).broadcast_to([P, 1])).then_inc(small_in, 16)
                    sp.wait_ge(w_hi, 4)
                    sp.wait_ge(w_lo, 4)
                    sp.dma_start(wo_scr, wo16[:, :, :, :].rearrange("p l k n -> p (l k n)")).then_inc(scratch_out, 16)
                    sp.wait_ge(w_hi, 5)
                    sp.wait_ge(w_lo, 5)
                    sp.dma_start(wf_scr, wf16[:, :, :, :].rearrange("p l k n -> p (l k n)")).then_inc(scratch_out, 16)
                    sp.wait_ge(w_hi, 6)
                    sp.wait_ge(w_lo, 6)
                    sp.dma_start(wp_scr, wp16[:, :, :, :].rearrange("p l k n -> p (l k n)")).then_inc(scratch_out, 16)
                    sp.wait_ge(rows_in, 16 * NT)
                    sp.dma_start(embed_scr.rearrange("(i p) c -> p i c", p=P), emb[:, :, :]).then_inc(scratch_out, 16)
                    sp.wait_ge(scratch_out, 64)

                @block.gpsimd
                def _(pool):
                    pool.iota(col[:, :], [[1, T]], base=0, channel_multiplier=0,
                              allow_small_or_imprecise_dtypes=True).then_inc(consts_set, 1)
                    pool.memset(ident[:, :], 0.0).then_inc(consts_set, 1)
                    pool.memset(ident_big[:, :], 0.0).then_inc(consts_set, 1)
                    pool.memset(causal[:, :], 0.0).then_inc(consts_set, 1)
                    pool.memset(coef[:, 3:4], P_BIAS).then_inc(consts_set, 1)
                    pool.wait_ge(consts_set, 5)
                    pool.affine_select(out=ident[:, :], in_=ident[:, :], compare_op=ALU.not_equal, fill=1.0,
                                       base=0, pattern=[[-1, P]], channel_multiplier=1).then_inc(consts_set, 1)
                    pool.affine_select(out=ident_big[:, :], in_=ident_big[:, :], compare_op=ALU.not_equal,
                                       fill=ONE_ROW, base=0, pattern=[[-1, P]],
                                       channel_multiplier=1).then_inc(consts_set, 1)
                    pool.affine_select(out=causal[:, :], in_=causal[:, :], compare_op=ALU.is_ge, fill=-60000.0,
                                       base=0, pattern=[[-1, P]], channel_multiplier=1).then_inc(consts_set, 1)
                    pool.wait_ge(top_ready, 1)
                    pool.partition_all_reduce(top_all[:, 0:4], top[:, 0:4], P,
                                              bass.bass_isa.ReduceOp.max).then_inc(top_shared, 1)
                    pool.wait_ge(idx_ready, 1)
                    for i in range(NT):
                        b, t = i // TT, i % TT
                        pool.indirect_dma_start(
                            emb[:, i, :], None, table,
                            bass.IndirectOffsetOnAxis(ap=pos_idx[:, t, b:b + 1], axis=0)).then_inc(rows_in, 16)
                    pool.wait_ge(top_ready, 2)
                    pool.partition_all_reduce(top_all[:, 4:6], top[:, 4:6], P,
                                              bass.bass_isa.ReduceOp.max).then_inc(top_shared, 1)

                @block.vector
                def _(dve):
                    steps = [0]

                    def then(ins):
                        steps[0] += 1
                        ins.then_inc(dve_step, 1)
                        dve.wait_ge(dve_step, steps[0])

                    dve.wait_ge(tokens_in, 16)
                    dve.wait_ge(consts_set, 8)
                    then(dve.tensor_copy(tok_f[:, :], tok_i[:, :]))
                    dve.tensor_scalar(keep[:, :], tok_f[:, :], float(PAD_TOKEN), None, ALU.not_equal)
                    then(dve.scalar_tensor_tensor(sep_at[:, :], tok_f[:, :], float(SEP_TOKEN), col[:, :],
                                                  ALU.is_equal, ALU.mult))
                    dve.tensor_tensor_scan(valid[:, :], keep[:, :], keep[:, :], 1.0, ALU.mult, ALU.mult)
                    then(dve.tensor_tensor_scan(last_sep[:, :], sep_at[:, :], sep_at[:, :], 0.0, ALU.max, ALU.max))
                    then(dve.scalar_tensor_tensor(pos[:, :], col[:, :], 1.0, last_sep[:, :], ALU.add, ALU.subtract))
                    then(dve.tensor_tensor(pos[:, :], pos[:, :], valid[:, :], ALU.mult))
                    dve.tensor_scalar(pos[:, :], pos[:, :], 1.0, None, ALU.add).then_inc(pos_ready, 1)
                    dve.wait_ge(posT_ready, 1)
                    dve.tensor_copy(pos_idx[:, :, :], ps[:, 0, 0:NT].rearrange("p (t b) -> p t b", b=B)) \
                        .then_inc(idx_ready, 1)

                    def scales(a, b):
                        then(dve.tensor_single_scalar(pow2[:, a:b].bitcast(I32), top_all[:, a:b].bitcast(I32),
                                                      EXP_BITS, ALU.bitwise_and))
                        then(dve.tensor_scalar(pow2[:, a:b], pow2[:, a:b], 2.0 ** -30, None, ALU.max))
                        then(dve.reciprocal(winv[:, a:b], pow2[:, a:b]))
                        steps[0] += 1
                        dve.tensor_scalar(winv[:, a:b], winv[:, a:b], W_TOP, None, ALU.mult).then_inc(dve_step, 1)
                        dve.wait_ge(dve_step, steps[0])

                    dve.wait_ge(proj_w_in, 64)
                    flat = [(KVD, wkvd_f[:, :, :]), (KVU, wkvu_f[:, :]), (WQ, wq_f[:, :, :]), (WO, wo_f[:, :, :])]
                    for m, w in flat:
                        ins = dve.tensor_reduce(top[:, m:m + 1], w, AX_X if m == KVU else mybir.AxisListType.XY, ALU.max,
                                                apply_absolute_value=True)
                    ins.then_inc(top_ready, 1)
                    dve.wait_ge(top_shared, 1)
                    scales(0, 4)
                    dve.sem_inc(winv_ready, 1)
                    for m, w, hl in ((KVD, wkvd_f[:, :, :], wkvd), (KVU, wkvu_f[:, :], wkvu),
                                     (WQ, wq_f[:, :, :], wq), (WO, wo_f[:, :, :], wo16)):
                        dve.wait_ge(w_hi, m + 1)
                        dve.scalar_tensor_tensor(hl[:, 1], w, winv[:, m:m + 1], hl[:, 0],
                                                 ALU.mult, ALU.subtract).then_inc(w_lo, 1)

                    def ternary(w, n):
                        row = w.shape[2]
                        s = row_scale[:, 0:KH] if n == KH else row_scale[:, KH:KH + KC]
                        then(dve.tensor_reduce(s, w, AX_X, ALU.add, apply_absolute_value=True))
                        then(dve.tensor_scalar(s, s, 1.0 / row, EPS, ALU.mult, ALU.max))
                        hs = half_scale[:, 0, 0:n]
                        minus_hs = half_scale[:, 1, 0:n]
                        then(dve.tensor_scalar(hs, s, 0.5, None, ALU.mult))
                        then(dve.tensor_scalar(minus_hs, s, -0.5, None, ALU.mult))
                        above = tern[:, 0:n * row].rearrange("p (n r) -> p n r", n=n)
                        tw = tern[:, n * row:2 * n * row].rearrange("p (n r) -> p n r", n=n)

                        def by_row(x):
                            return x.unsqueeze(2).broadcast_to([P, n, row])

                        then(dve.tensor_tensor(above, w, by_row(hs), ALU.is_gt))
                        then(dve.tensor_tensor(tw, w, by_row(minus_hs), ALU.is_lt))
                        then(dve.tensor_tensor(tw, tw, above, ALU.subtract))
                        then(dve.tensor_tensor(tw, w, tw, ALU.add))
                        then(dve.tensor_tensor(tw, w, tw, ALU.subtract))
                        ins = dve.tensor_tensor(w, tw, by_row(s), ALU.mult)
                        return ins

                    dve.wait_ge(ffn_w_in, 32)
                    ternary(wpr_f[:, :, :], KC).then_inc(proj_full, 1)
                    then(ternary(wfc_f[:, :, :], KH))
                    dve.wait_ge(low_rank, 1)
                    dve.wait_ge(small_in, 64)
                    dve.scalar_tensor_tensor(wfc_f[:, :, :],
                                             ps[:, 4:8, :].rearrange("p b (k c) -> p (b k) c", c=C),
                                             gate_b[:, 0:1], wfc_f[:, :, :], ALU.mult, ALU.add).then_inc(fc_full, 1)
                    dve.wait_ge(fc_full, 1)
                    dve.wait_ge(proj_full, 1)
                    dve.tensor_reduce(top[:, WF:WF + 1], wfc_f[:, :, :], mybir.AxisListType.XY, ALU.max,
                                      apply_absolute_value=True)
                    dve.tensor_reduce(top[:, WP:WP + 1], wpr_f[:, :, :], mybir.AxisListType.XY, ALU.max,
                                      apply_absolute_value=True).then_inc(top_ready, 1)
                    dve.wait_ge(top_shared, 2)
                    scales(4, 6)
                    dve.sem_inc(winv_ready, 1)
                    dve.wait_ge(w_hi, 5)
                    dve.scalar_tensor_tensor(wf16[:, 1].rearrange("p k (b n) -> p (k b) n", b=2), ps[:, 0:4, :],
                                             winv[:, WF:WF + 1], wf16[:, 0].rearrange("p k (b n) -> p (k b) n", b=2),
                                             ALU.mult, ALU.subtract).then_inc(w_lo, 1)
                    dve.wait_ge(w_hi, 6)
                    dve.scalar_tensor_tensor(wp16[:, 1].rearrange("p (b k) n -> p b (k n)", b=4), ps[:, 4:8, :],
                                             winv[:, WP:WP + 1], wp16[:, 0].rearrange("p (b k) n -> p b (k n)", b=4),
                                             ALU.mult, ALU.subtract).then_inc(w_lo, 1)
                    then(dve.tensor_tensor(coef[:, 1:2], pow2[:, KVD:KVD + 1], pow2[:, KVU:KVU + 1], ALU.mult))
                    then(dve.scalar_tensor_tensor(coef[:, 0:1], pow2[:, WQ:WQ + 1], 0.5, coef[:, 1:2],
                                                  ALU.mult, ALU.mult))
                    then(dve.scalar_tensor_tensor(coef[:, 1:2], pow2[:, WO:WO + 1], 0.5, coef[:, 1:2],
                                                  ALU.mult, ALU.mult))
                    then(dve.tensor_tensor(coef[:, 2:3], pow2[:, WF:WF + 1], pow2[:, WF:WF + 1], ALU.mult))
                    then(dve.scalar_tensor_tensor(coef[:, 2:3], pow2[:, WP:WP + 1], 0.25, coef[:, 2:3],
                                                  ALU.mult, ALU.mult))

                    dve.wait_ge(rows_in, 16 * NT)
                    for i in range(NT):
                        ins = dve.bn_stats(stats[:, i, :], emb[:, i, :])
                    then(ins)
                    for i in range(NT):
                        ins = dve.bn_aggr(mv[:, i, :], stats[:, i, :])
                    then(ins)
                    dve.tensor_scalar(var[:, :], mv[:, :, 1], EPS, None, ALU.add).then_inc(var_ready, 1)
                    dve.wait_ge(std_ready, 1)
                    then(dve.reciprocal(rstd[:, :], std[:, :]))
                    then(dve.tensor_tensor(tmp[:, :], rstd[:, :], rstd[:, :], ALU.mult))
                    then(dve.tensor_tensor(tmp[:, :], tmp[:, :], var[:, :], ALU.mult))
                    then(dve.tensor_scalar(tmp[:, :], tmp[:, :], -0.5 * X_SCALE, 1.5 * X_SCALE, ALU.mult, ALU.add))
                    then(dve.tensor_tensor(rstd[:, :], rstd[:, :], tmp[:, :], ALU.mult))

                    def normalise(g):
                        if g >= 2:
                            dve.wait_ge(xT_ps, KC * (g - 1))
                        for j in range(4):
                            i = 4 * g + j
                            ins = dve.tensor_scalar(xn[:, g % 2, j, :], emb[:, i, :], mv[:, i, 0:1], rstd[:, i:i + 1],
                                                    ALU.subtract, ALU.mult)
                        ins.then_inc(xn_ready, 1)

                    def lat_low(g):
                        dve.wait_ge(lat_hi, g + 1)
                        dve.scalar_tensor_tensor(latT[:, 1, BANK * g:BANK * (g + 1)], ps[:, 4 + g % 2, :], LAT_SHIFT,
                                                 latT[:, 0, BANK * g:BANK * (g + 1)],
                                                 ALU.mult, ALU.subtract).then_inc(lat_lo, 1)

                    normalise(0)
                    for g in range(GROUPS):
                        if g + 1 < GROUPS:
                            normalise(g + 1)
                        for k in range(KC):
                            n = KC * g + k
                            dve.wait_ge(xT_hi, n + 1)
                            dve.tensor_tensor(xT[:, 1, k, BANK * g:BANK * (g + 1)], ps[:, n % 4, :],
                                              xT[:, 0, k, BANK * g:BANK * (g + 1)], ALU.subtract).then_inc(xT_lo, 1)
                        if g >= 1:
                            lat_low(g - 1)
                    lat_low(GROUPS - 1)

                @block.scalar
                def _(act):
                    act.wait_ge(uT_ready, 1)
                    act.activation(uT[:, :], ps[0:RANK, 2:4, :].rearrange("r b n -> r (b n)"),
                                   ACT.Copy).then_inc(uT_copied, 1)
                    act.wait_ge(fbv_ready, 1)
                    act.activation(fbv[:, :], ps[0:RANK, 1, 0:C], ACT.Copy).then_inc(fbv_copied, 1)
                    act.wait_ge(winv_ready, 1)
                    for m, w, hl in ((KVD, wkvd_f[:, :, :], wkvd), (KVU, wkvu_f[:, :], wkvu),
                                     (WQ, wq_f[:, :, :], wq), (WO, wo_f[:, :, :], wo16)):
                        act.activation(hl[:, 0], w, ACT.Copy, scale=winv[:, m:m + 1]).then_inc(w_hi, 1)
                    act.wait_ge(winv_ready, 2)
                    act.wait_ge(fcT_ready, 1)
                    act.activation(wf16[:, 0].rearrange("p k (b n) -> p (k b) n", b=2), ps[:, 0:4, :], ACT.Copy,
                                   scale=winv[:, WF:WF + 1]).then_inc(w_hi, 1)
                    act.wait_ge(projT_ready, 1)
                    act.activation(wp16[:, 0].rearrange("p (b k) n -> p b (k n)", b=4), ps[:, 4:8, :], ACT.Copy,
                                   scale=winv[:, WP:WP + 1]).then_inc(w_hi, 1)
                    act.wait_ge(var_ready, 1)
                    act.activation(std[:, :], var[:, :], ACT.Sqrt).then_inc(std_ready, 1)

                    def lat_high(g):
                        act.wait_ge(lat_ps, g + 1)
                        act.activation(latT[:, 0, BANK * g:BANK * (g + 1)], ps[:, 4 + g % 2, :], ACT.Copy,
                                       scale=LAT_SHIFT).then_inc(lat_hi, 1)

                    for g in range(GROUPS):
                        for k in range(KC):
                            n = KC * g + k
                            act.wait_ge(xT_ps, n + 1)
                            act.activation(xT[:, 0, k, BANK * g:BANK * (g + 1)], ps[:, n % 4, :],
                                           ACT.Copy).then_inc(xT_hi, 1)
                        if g >= 1:
                            lat_high(g - 1)
                    lat_high(GROUPS - 1)

                @block.tensor
                def _(pe):
                    pe.wait_ge(consts_set, 8)
                    pe.wait_ge(pos_ready, 1)
                    for t in range(TT):
                        ins = pe.transpose(ps[:, 0, B * t:B * (t + 1)], pos[:, P * t:P * (t + 1)], ident[0:B, 0:B])
                    ins.then_inc(posT_ready, 1)
                    pe.wait_ge(small_in, 64)
                    for k in range(KH):
                        ins = pe.transpose(ps[0:RANK, 2 + k // 4, P * (k % 4):P * (k % 4 + 1)], u_f[:, k, :],
                                           ident[:, :])
                    ins.then_inc(uT_ready, 1)
                    pe.matmul(ps[0:RANK, 1, 0:C], fbT[:, :], v_f[:, :], start=True, stop=True).then_inc(fbv_ready, 1)
                    pe.wait_ge(uT_copied, 1)
                    pe.wait_ge(fbv_copied, 1)
                    for k in range(KH):
                        ins = pe.matmul(ps[:, 4 + k // 2, C * (k % 2):C * (k % 2 + 1)], uT[:, P * k:P * (k + 1)],
                                        fbv[:, :], start=True, stop=True)
                    ins.then_inc(low_rank, 1)
                    pe.wait_ge(idx_ready, 1)
                    pe.wait_ge(fc_full, 1)
                    for k in range(KC):
                        for h in range(KH):
                            ins = pe.transpose(ps[:, 2 * k + h // 4, P * (h % 4):P * (h % 4 + 1)],
                                               wfc_f[:, h, P * k:P * (k + 1)], ident[:, :])
                    ins.then_inc(fcT_ready, 1)
                    for h in range(KH):
                        for k in range(KC):
                            ins = pe.transpose(ps[:, 4 + h // 2, C * (h % 2) + P * k:C * (h % 2) + P * (k + 1)],
                                               wpr_f[:, k, P * h:P * (h + 1)], ident[:, :])
                    ins.then_inc(projT_ready, 1)
                    pe.wait_ge(w_hi, 6)
                    pe.wait_ge(w_lo, 6)

                    def latent(g):
                        pe.wait_ge(xT_hi, KC * (g + 1))
                        pe.wait_ge(xT_lo, KC * (g + 1))
                        if g >= 2:
                            pe.wait_ge(lat_lo, g - 1)
                        n = 0
                        for k in range(KC):
                            for wl, xl in ((0, 0), (0, 1), (1, 0)):
                                ins = pe.matmul(ps[:, 4 + g % 2, :], wkvd[:, wl, k, :],
                                                xT[:, xl, k, BANK * g:BANK * (g + 1)],
                                                start=(n == 0), stop=(n == 3 * KC - 1))
                                n += 1
                        ins.then_inc(lat_ps, 1)

                    for g in range(GROUPS):
                        pe.wait_ge(xn_ready, g + 1)
                        for k in range(KC):
                            n = KC * g + k
                            if n >= 4:
                                pe.wait_ge(xT_lo, n - 3)
                            for j in range(4):
                                ins = pe.transpose(ps[:, n % 4, P * j:P * (j + 1)],
                                                   xn[:, g % 2, j, P * k:P * (k + 1)], ident[:, :])
                            ins.then_inc(xT_ps, 1)
                        if g >= 1:
                            latent(g - 1)
                    latent(GROUPS - 1)

        NHEADS = B * NH
        with ExitStack() as main:
            q1 = sb(main, "q1", [P, 4, T], F16)
            q2 = sb(main, "q2", [P, 4, T], F16)
            k1 = sb(main, "k1", [P, 4, T], F16)
            k2 = sb(main, "k2", [P, 4, T], F16)
            q_pair = sb(main, "q_pair", [P, 2, 2, T], F16)
            k_pair = sb(main, "k_pair", [P, 2, 2, T], F16)
            v_hi = sb(main, "v_hi", [P, 2, TT, 2, HD + 1], F16)
            v_lo = sb(main, "v_lo", [P, 2, TT, 2, HD], F16)
            STEPS = [(c, kt) for c in range(2) for kt in range(4 * (c + 1))]
            q_from = [max(BANK * c, P * kt) for c, kt in STEPS]
            width = [BANK * (c + 1) - f for (c, kt), f in zip(STEPS, q_from)]
            at = [sum(width[:s]) for s in range(len(STEPS))]
            NS = len(STEPS)
            AREA = sum(width)
            DIAG = [s for s, (c, kt) in enumerate(STEPS) if kt >= 4 * c]
            FULL = [s for s, (c, kt) in enumerate(STEPS) if kt < 4 * c]
            prob = sb(main, "prob", [P, 2, AREA], F32)
            prob_lo = sb(main, "prob_lo", [P, 2, AREA], F16)
            row_max = sb(main, "row_max", [P, 2, NS], F32)
            row_max_all = sb(main, "row_max_all", [P, 2, TT], F32)
            max_row8 = sb(main, "max_row8", [TT, 2, P], F16)
            rsum = sb(main, "rsum", [P, 2, 4], F32)
            y_st = sb(main, "y_st", [P, 2, TT, P], F32)
            y_sp = sb(main, "y_sp", [P, 2, 2, 2, BANK], F16)
            MSTEPS = [(t, h) for t in range(TT) for h in range(t // 4 + 1)]
            assert len(MSTEPS) == NS
            ND, NF = len(DIAG), len(FULL)

            S_BANK, M_BANK, O_BANK, J_BANK = 0, 2, 4, 6

            ones_set = sem("ones_set")
            qk_ps = sem("qk_ps")
            qk_hi = sem("qk_hi")
            qk_lo = sem("qk_lo")
            laid = [sem("laid_even"), sem("laid_odd")]
            v_ps = sem("v_ps")
            v_hi_done = sem("v_hi_done")
            v_lo_done = sem("v_lo_done")
            mx_ps = sem("mx_ps")
            mx_red = sem("mx_red")
            mx_comb = sem("mx_comb")
            mx_pair = sem("mx_pair")
            mxT_ps = sem("mxT_ps")
            mxT_out = sem("mxT_out")
            mx_row = sem("mx_row")
            sc_ps = sem("sc_ps")
            sc_exp = sem("sc_exp")
            exp_seen = sem("exp_seen")
            masked = sem("masked")
            lo_diag = sem("lo_diag")
            lo_full = sem("lo_full")
            pv_ps = sem("pv_ps")
            recip = sem("recip")
            y_norm = sem("y_norm")
            yT_ps = sem("yT_ps")
            yT_hi = sem("yT_hi")
            yT_lo = sem("yT_lo")
            y_out = [sem("y_out_even"), sem("y_out_odd")]

            JOB = (1, 2, 4, 7, 10)
            LO_STEP = (6, 7, 9, 10)

            class Slot:
                def __init__(self, it, k, first=False, zero=False, last=False, tail=False):
                    self.it, self.k = it, k
                    self.first, self.zero, self.last, self.tail = first, zero, last, tail
                    g = 4 * it + k
                    self.g = g
                    known = first or zero or last or tail
                    self.score = not first and not tail
                    self.pv = (not known) or (zero and k >= 1) or last or (tail and k == 0)
                    self.maxima = (not known) or (first and k >= 2) or zero or (last and k < 2)
                    self.row = (not known) or (first and k == 3) or zero or (last and k < 3)
                    self.qk = k % 2 == 0 and (not known or first or zero)
                    self.v = k % 2 == 1 and (not known or (first and k == 3) or zero or (last and k == 1))
                    self.y = k % 2 == 1 and (not known or (zero and k == 3) or last or (tail and k == 1))
                    self.lay = (not known) or (first and k >= 1) or zero or (last and k < 1)
                    self.even = k % 2 == 0

            def slots(eng, run):
                for k in range(4):
                    run(Slot(-1, k, first=True))
                for k in range(4):
                    run(Slot(0, k, zero=True))
                with eng.Fori(1, NHEADS // 4 - 1) as it:
                    for k in range(4):
                        run(Slot(it, k))
                for k in range(4):
                    run(Slot(NHEADS // 4 - 1, k, last=True))
                for k in range(2):
                    run(Slot(NHEADS // 4, k, tail=True))

            with nc.Block() as block:
                @block.sync
                def _(sp):
                    def slot(s):
                        if s.lay:
                            h = s.g + 3
                            r, a = (s.k + 3) % 4, (s.k + 3) % 2
                            pr = 2 * s.it + (s.k + 3) // 2
                            src = ((s.k + 3) // 2) % 2
                            split, used = 4 * pr + 4, NS * (h - 3)
                            if not isinstance(h, int):
                                split, used = sp.snap(split), sp.snap(used)
                            if not s.first and not (s.zero and s.k == 0):
                                sp.wait_ge(sc_ps, used)
                            elif h >= 2:
                                sp.wait_ge(mx_ps, NS * (h - 1))
                            sp.wait_ge(qk_hi, split)
                            sp.wait_ge(qk_lo, split)
                            rows = slice(HD * a, HD * (a + 1))
                            for dst, half, pair_, l in ((q1, 0, q_pair, 0), (q1, 1, q_pair, 1), (q2, 0, q_pair, 0),
                                                        (k1, 0, k_pair, 0), (k1, 1, k_pair, 0), (k2, 0, k_pair, 1)):
                                sp.dma_start(dst[HD * half:HD * (half + 1), r, :],
                                             pair_[rows, src, l, :]).then_inc(laid[a], 16)
                        if s.row:
                            h = s.g + 1
                            sp.wait_ge(mxT_out, h + 1)
                            sp.dma_start(q2[HD:HD + 1, (s.k + 1) % 4, :].rearrange("o (t n) -> o t n", t=TT),
                                         max_row8[:, (s.k + 1) % 2, :]).then_inc(mx_row, 16)
                        if s.y:
                            pr = 2 * s.it + s.k // 2 - 1
                            par = (s.k // 2 - 1) % 2
                            sp.wait_ge(yT_hi, 2 * pr + 2)
                            sp.wait_ge(yT_lo, 2 * pr + 2)
                            b_, hp = batch_and_pair(pr)
                            for half in range(2):
                                dst = y_scr[bass.ds(b_, 1), half, :, bass.ds(hp, 1), :].rearrange("a p b n -> p (a b n)")
                                sp.dma_start(dst, y_sp[:, par, half, :, :].rearrange("p l n -> p (l n)")) \
                                    .then_inc(y_out[par], 16)

                    slots(sp, slot)
                    sp.wait_ge(y_out[0], 32 * (NHEADS // 4))
                    sp.wait_ge(y_out[1], 32 * (NHEADS // 4))

                @block.gpsimd
                def _(pool):
                    pool.memset(k2[HD:HD + 1, :, :], ONE_ROW).then_inc(ones_set, 1)
                    pool.wait_ge(ones_set, 1)
                    pool.memset(v_hi[:, :, :, :, HD:HD + 1], 1.0).then_inc(ones_set, 1)

                    def slot(s):
                        if not s.score:
                            return
                        e = s.k % 2
                        for n, st in enumerate(DIAG):
                            c, kt = STEPS[st]
                            block_ = prob[:, e, at[st]:at[st] + P]
                            span = slice(at[st], at[st] + width[st])
                            pool.wait_ge(sc_exp, NS * s.g + st + 1)
                            pool.sem_inc(exp_seen, 1)
                            pool.affine_select(out=block_, in_=block_, compare_op=ALU.is_ge, fill=0.0, base=0,
                                               pattern=[[1, P]], channel_multiplier=-1).then_inc(masked, 1)
                            pool.wait_ge(masked, ND * s.g + n + 1)
                            if n == 0 and not (s.zero and s.k < 2):
                                pool.wait_ge(pv_ps, TT * (s.g - 1))
                            pool.tensor_tensor(prob_lo[:, e, span], prob[:, e, span],
                                               prob[:, e, :].bitcast(BF16)[:, 2 * at[st] + 1:2 * (at[st] + width[st]):2],
                                               ALU.subtract).then_inc(lo_diag, 1)

                    slots(pool, slot)

                @block.scalar
                def _(act):
                    def slot(s):
                        e = s.k % 2
                        for st in range(NS):
                            if s.score:
                                act.wait_ge(sc_ps, NS * s.g + st + 1)
                                if st == 0 and not (s.zero and s.k < 2):
                                    act.wait_ge(pv_ps, TT * (s.g - 1))
                                    act.wait_ge(lo_full, NF * (s.g - 1))
                                act.activation(prob[:, e, at[st]:at[st] + width[st]],
                                               ps[:, S_BANK + st % 2, 0:width[st]], ACT.Exp,
                                               bias=coef[:, 3:4], scale=coef[:, 0:1]).then_inc(sc_exp, 1)
                            if st == JOB[1] and s.row:
                                h = s.g + 1
                                act.wait_ge(mxT_ps, h + 1)
                                if not (s.first or (s.zero and s.k == 0)):
                                    act.wait_ge(mx_row, 16 * (h - 1))
                                act.activation(max_row8[:, (s.k + 1) % 2, :],
                                               ps[0:TT, J_BANK + (1 if s.even else 0), 0:P], ACT.Copy,
                                               scale=-1.0 / ONE_ROW).then_inc(mxT_out, 1)
                            elif st in JOB and st != JOB[1]:
                                j = (0, None, 1, 2, 3)[JOB.index(st)]
                                if s.even and s.qk:
                                    pr, par = 2 * s.it + s.k // 2 + 2, (s.k // 2) % 2
                                    bank = J_BANK + (0, 0, 1, 0)[j]
                                    act.wait_ge(qk_ps, 4 * pr + j + 1)
                                    if j == 0 and not s.first:
                                        act.wait_ge(laid[0], 96 * (pr - 1))
                                        act.wait_ge(laid[1], 96 * (pr - 1))
                                    dst = (q_pair if j < 2 else k_pair)[:, par, 0, BANK * (j % 2):BANK * (j % 2 + 1)]
                                    act.activation(dst, ps[:, bank, :], ACT.Copy,
                                                   scale=Q_SHIFT if j < 2 else KV_SHIFT).then_inc(qk_hi, 1)
                                if not s.even and j < 2 and s.v:
                                    pr, par = 2 * s.it + s.k // 2 + 1, (s.k // 2 + 1) % 2
                                    act.wait_ge(v_ps, 2 * pr + j + 1)
                                    if st == JOB[0] and not (s.first or (s.zero and s.k == 1)):
                                        act.wait_ge(pv_ps, TT * (s.g - 1))
                                    if st == JOB[0] and s.first:
                                        act.wait_ge(ones_set, 2)
                                    act.activation(v_hi[:, par, 4 * j:4 * j + 4, :, 0:HD],
                                                   ps[:, J_BANK + 1, :].rearrange("p (t a d) -> p t a d", t=4, a=2),
                                                   ACT.Copy, scale=KV_SHIFT).then_inc(v_hi_done, 1)
                                if not s.even and j >= 2 and s.y:
                                    pr, par = 2 * s.it + s.k // 2 - 1, (s.k // 2 - 1) % 2
                                    half = j - 2
                                    act.wait_ge(yT_ps, 2 * pr + half + 1)
                                    if not (s.zero and s.k == 3):
                                        act.wait_ge(y_out[1 - par], 32 * s.it)
                                    act.activation(y_sp[:, par, half, 0, :], ps[:, J_BANK + half, :],
                                                   ACT.Copy).then_inc(yT_hi, 1)

                    slots(act, slot)

                @block.vector
                def _(dve):
                    def normalise(s_it, k, chunk):
                        h = 4 * s_it + k
                        par, a = (k // 2) % 2, k % 2
                        o = ps[:, O_BANK + chunk, 0:4 * (HD + 1)].rearrange("p (t d) -> p t d", t=4)
                        dve.wait_ge(pv_ps, TT * h + 4 * (chunk + 1))
                        dve.reciprocal(rsum[:, chunk, :], o[:, :, HD]).then_inc(recip, 1)
                        dve.wait_ge(recip, 2 * h + chunk + 1)
                        dve.tensor_tensor(y_st[:, par, 4 * chunk:4 * chunk + 4, HD * a:HD * (a + 1)], o[:, :, 0:HD],
                                          rsum[:, chunk, :].unsqueeze(2).broadcast_to([P, 4, HD]),
                                          ALU.mult).then_inc(y_norm, 1)

                    def slot(s):
                        e = s.k % 2
                        for st in range(NS):
                            if s.maxima:
                                h, me = s.g + 2, s.k % 2
                                t, half = MSTEPS[st]
                                w = min(BANK, P * (t + 1) - BANK * half)
                                dve.wait_ge(mx_ps, NS * h + st + 1)
                                if st == 0 and not s.first:
                                    dve.wait_ge(mx_comb, h - 1)
                                c_ = t if half == 0 else TT + t - 4
                                dve.tensor_reduce(row_max[:, me, c_:c_ + 1], ps[:, M_BANK + st % 2, 0:w], AX_X,
                                                  ALU.max).then_inc(mx_red, 1)
                            if s.score and st in LO_STEP:
                                f = FULL[LO_STEP.index(st)]
                                span = slice(at[f], at[f] + width[f])
                                dve.wait_ge(sc_exp, NS * s.g + f + 1)
                                if f == FULL[0] and not (s.zero and s.k < 2):
                                    dve.wait_ge(pv_ps, TT * (s.g - 1))
                                dve.tensor_tensor(prob_lo[:, e, span], prob[:, e, span],
                                                  prob[:, e, :].bitcast(BF16)[:, 2 * at[f] + 1:2 * (at[f] + width[f]):2],
                                                  ALU.subtract).then_inc(lo_full, 1)
                            if st == 0 and ((not s.first and not s.zero and not s.tail) or (s.zero and s.k >= 2)
                                            or (s.tail and s.k < 2)):
                                kk = s.k - 2
                                normalise(s.it + (kk // 4), kk % 4, 1)
                            if st == 4 and s.pv:
                                kk = s.k - 1
                                normalise(s.it + (kk // 4), kk % 4, 0)
                            if st - 1 in JOB and st - 1 != JOB[1]:
                                j = (0, None, 1, 2, 3)[JOB.index(st - 1)]
                                if s.even and s.qk:
                                    pr, par = 2 * s.it + s.k // 2 + 2, (s.k // 2) % 2
                                    bank = J_BANK + (0, 0, 1, 0)[j]
                                    cols = slice(BANK * (j % 2), BANK * (j % 2 + 1))
                                    hl = q_pair if j < 2 else k_pair
                                    dve.wait_ge(qk_hi, 4 * pr + j + 1)
                                    dve.scalar_tensor_tensor(hl[:, par, 1, cols], ps[:, bank, :],
                                                             Q_SHIFT if j < 2 else KV_SHIFT, hl[:, par, 0, cols],
                                                             ALU.mult, ALU.subtract).then_inc(qk_lo, 1)
                                if not s.even and j < 2 and s.v:
                                    pr, par = 2 * s.it + s.k // 2 + 1, (s.k // 2 + 1) % 2
                                    dve.wait_ge(v_hi_done, 2 * pr + j + 1)
                                    for a in range(2):
                                        ins = dve.scalar_tensor_tensor(
                                            v_lo[:, par, 4 * j:4 * j + 4, a, :],
                                            ps[:, J_BANK + 1, :].rearrange("p (t a d) -> p t a d", t=4, a=2)[:, :, a, :],
                                            KV_SHIFT, v_hi[:, par, 4 * j:4 * j + 4, a, 0:HD], ALU.mult, ALU.subtract)
                                    ins.then_inc(v_lo_done, 1)
                                if not s.even and j >= 2 and s.y:
                                    pr, par = 2 * s.it + s.k // 2 - 1, (s.k // 2 - 1) % 2
                                    half = j - 2
                                    dve.wait_ge(yT_hi, 2 * pr + half + 1)
                                    dve.tensor_tensor(y_sp[:, par, half, 1, :], ps[:, J_BANK + half, :],
                                                      y_sp[:, par, half, 0, :], ALU.subtract).then_inc(yT_lo, 1)
                        if s.maxima:
                            h, me = s.g + 2, s.k % 2
                            dve.wait_ge(mx_red, NS * (h + 1))
                            if not s.first:
                                dve.wait_ge(mxT_ps, h - 1)
                            dve.tensor_copy(row_max_all[:, me, 0:4], row_max[:, me, 0:4]).then_inc(mx_pair, 1)
                            dve.tensor_tensor(row_max_all[:, me, 4:TT], row_max[:, me, 4:TT], row_max[:, me, TT:NS],
                                              ALU.max).then_inc(mx_comb, 1)

                    slots(dve, slot)

                @block.tensor
                def _(pe):
                    passes = ((0, 0), (1, 0), (0, 1))

                    def score_step(s, st):
                        c, kt = STEPS[st]
                        r = s.k % 4
                        keys = slice(P * kt, P * (kt + 1))
                        qs = slice(q_from[st], q_from[st] + width[st])
                        dst = ps[:, S_BANK + st % 2, 0:width[st]]
                        if st == 0:
                            pe.wait_ge(mx_row, 16 * (s.g + 1))
                        if not (s.zero and s.k == 0 and st < 2):
                            pe.wait_ge(sc_exp, NS * s.g + st - 1)
                        pe.matmul(dst, k1[:, r, keys], q1[:, r, qs], start=True, stop=False)
                        pe.matmul(dst, k2[0:HD + 1, r, keys], q2[0:HD + 1, r, qs], start=False,
                                  stop=True).then_inc(sc_ps, 1)

                    def max_step(s, st):
                        h, r = s.g + 2, (s.k + 2) % 4
                        t, half = MSTEPS[st]
                        w = min(BANK, P * (t + 1) - BANK * half)
                        dst = ps[:, M_BANK + st % 2, 0:w]
                        diag = half == t // 4
                        if st == 0:
                            pe.wait_ge(laid[s.k % 2], 96 * (2 * s.it + (s.k + 2) // 2 + 1))
                        if not (s.first and s.k == 2 and st < 2):
                            pe.wait_ge(mx_red, NS * h + st - 1)
                        ins = pe.matmul(dst, q1[:, r, P * t:P * (t + 1)], k1[:, r, BANK * half:BANK * half + w],
                                        start=True, stop=not diag)
                        if diag:
                            ins = pe.matmul(dst[:, w - P:w], ident_big[:, :], causal[:, :], start=False, stop=True)
                        ins.then_inc(mx_ps, 1)

                    def pv_blocks(s, st):
                        kk = (s.k - 1) % 4
                        it = s.it + (s.k - 1) // 4
                        h = 4 * it + kk
                        e, par, a = kk % 2, (kk // 2) % 2, kk % 2
                        tri = [(t, kt) for t in range(TT) for kt in range(t + 1)]
                        for t, kt in tri[3 * st:3 * st + 3]:
                            if t == 0:
                                pe.wait_ge(v_hi_done, 2 * (2 * it + kk // 2) + 2)
                                pe.wait_ge(v_lo_done, 2 * (2 * it + kk // 2) + 2)
                            if kt == 0:
                                pe.wait_ge(lo_diag, ND * h + t + 1)
                                if t == 4:
                                    pe.wait_ge(lo_full, NF * (h + 1))
                                if t % 4 == 0 and not (s.zero and s.k == 1):
                                    pe.wait_ge(y_norm, 2 * (h - 1) + t // 4 + 1)
                            b = STEPS.index((t // 4, kt))
                            o = at[b] + P * t - q_from[b]
                            dst = ps[:, O_BANK + t // 4, (HD + 1) * (t % 4):(HD + 1) * (t % 4 + 1)]
                            p_hi = prob[:, e, :].bitcast(BF16)[:, 2 * o + 1:2 * (o + P):2]
                            pe.matmul(dst, p_hi, v_hi[:, par, kt, a, :], start=(kt == 0), stop=False)
                            pe.matmul(dst[:, 0:HD], p_hi, v_lo[:, par, kt, a, :], start=False, stop=False)
                            ins = pe.matmul(dst, prob_lo[:, e, o:o + P], v_hi[:, par, kt, a, :], start=False,
                                            stop=(kt == t))
                            if kt == t:
                                ins.then_inc(pv_ps, 1)

                    def job(s, j):
                        if j == 1:
                            if s.row:
                                h = s.g + 1
                                bank = J_BANK + (1 if s.even else 0)
                                pe.wait_ge(mx_comb, h + 1)
                                pe.wait_ge(mx_pair, h + 1)
                                if s.even and (not s.first) and not (s.zero and s.k <= 2):
                                    pe.wait_ge(yT_lo, 2 * (2 * s.it + s.k // 2 - 2) + 2)
                                if not s.even:
                                    if s.qk_before:
                                        pe.wait_ge(qk_lo, 4 * (2 * s.it + s.k // 2 + 2) + 4)
                                pe.transpose(ps[0:TT, bank, 0:P], row_max_all[:, (s.k + 1) % 2, :],
                                             ident[:, :]).then_inc(mxT_ps, 1)
                            return
                        j = (0, None, 1, 2, 3)[j]
                        if s.even and s.qk:
                            pr = 2 * s.it + s.k // 2 + 2
                            bank = J_BANK + (0, 0, 1, 0)[j]
                            b_, hp = batch_and_pair(pr)
                            tok = b_ * T + BANK * (j % 2)
                            if j == 0 and (not s.first) and not (s.zero and s.k <= 2):
                                pe.wait_ge(yT_lo, 2 * (2 * s.it + s.k // 2 - 2) + 1)
                            if j == 0 and s.first and s.k == 2:
                                pe.wait_ge(qk_lo, 4)
                            if j == 0 and s.zero:
                                pe.wait_ge(mxT_out, s.g + 0) if s.k == 0 else pe.wait_ge(mxT_out, s.g)
                            if j == 1 or j == 3:
                                pe.wait_ge(qk_lo, 4 * pr + (1 if j == 1 else 2))
                            if j == 2 and s.row:
                                pe.wait_ge(mxT_out, s.g + 2)
                            n = 0
                            if j < 2:
                                for k in range(KC):
                                    for wl, xl in passes:
                                        ins = pe.matmul(ps[:, bank, :], wq[:, wl, k, bass.ds(hp * P, P)],
                                                        xT[:, xl, k, bass.ds(tok, BANK)], start=(n == 0),
                                                        stop=(n == 3 * KC - 1))
                                        n += 1
                            else:
                                for wl, xl in passes:
                                    ins = pe.matmul(ps[:, bank, :], wkvu[:, wl, bass.ds(hp * P, P)],
                                                    latT[:, xl, bass.ds(tok, BANK)], start=(n == 0), stop=(n == 2))
                                    n += 1
                            ins.then_inc(qk_ps, 1)
                        if not s.even and j < 2 and s.v:
                            pr = 2 * s.it + s.k // 2 + 1
                            b_, hp = batch_and_pair(pr)
                            if j == 0 and s.qk_before:
                                pe.wait_ge(qk_lo, 4 * (2 * s.it + s.k // 2 + 2) + 3)
                            if j == 0 and s.last:
                                pe.wait_ge(mxT_out, s.g + 1)
                            if j == 1:
                                pe.wait_ge(v_lo_done, 2 * pr + 1)
                            for t in range(4):
                                n = 0
                                for vl, ll in passes:
                                    ins = pe.matmul(ps[:, J_BANK + 1, P * t:P * (t + 1)],
                                                    latT[:, ll, bass.ds(b_ * T + BANK * j + P * t, P)],
                                                    wkvu[:, vl, bass.ds(hp * P + NH * HD, P)],
                                                    start=(n == 0), stop=(n == 2))
                                    n += 1
                            ins.then_inc(v_ps, 1)
                        if not s.even and j >= 2 and s.y:
                            pr, par = 2 * s.it + s.k // 2 - 1, (s.k // 2 - 1) % 2
                            half = j - 2
                            pe.wait_ge(y_norm, 4 * pr + 4)
                            if half == 0:
                                if s.row:
                                    pe.wait_ge(mxT_out, s.g + 2)
                                elif s.last or s.tail:
                                    pe.wait_ge(yT_lo, 2 * pr - 1)
                            if half == 1:
                                if s.v:
                                    pe.wait_ge(v_lo_done, 2 * (2 * s.it + s.k // 2 + 1) + 2)
                                elif s.last or s.tail:
                                    pe.wait_ge(yT_lo, 2 * pr)
                            for t in range(4):
                                ins = pe.transpose(ps[:, J_BANK + half, P * t:P * (t + 1)],
                                                   y_st[:, par, 4 * half + t, :], ident[:, :])
                            ins.then_inc(yT_ps, 1)

                    def slot(s):
                        s.qk_before = not s.even and not s.last and not s.tail
                        for st in range(NS):
                            if s.score:
                                score_step(s, st)
                            if s.maxima:
                                max_step(s, st)
                            if s.pv:
                                pv_blocks(s, st)
                            if st in JOB:
                                job(s, JOB.index(st))

                    slots(pe, slot)

        att.close()

        with ExitStack() as fin:
            wo = sb(fin, "wo", [P, 2, KH, C], F16)
            wf = sb(fin, "wf", [P, 2, KC, HID], F16)
            wp = sb(fin, "wp", [P, 2, KH, C], F16)
            yT = sb(fin, "yT", [P, 2, KH, 2, BANK], F16)
            resid = sb(fin, "resid", [P, 2, 4, C], F32)
            h2 = sb(fin, "h2", [P, 2, 4, C], F32)
            st2 = sb(fin, "st2", [P, 2, 4, 6], F32)
            mv2 = sb(fin, "mv2", [P, 2, 4, 2], F32)
            var2 = sb(fin, "var2", [P, 2, 4], F32)
            std2 = sb(fin, "std2", [P, 2, 4], F32)
            rstd2 = sb(fin, "rstd2", [P, 2, 4], F32)
            tmp2 = sb(fin, "tmp2", [P, 2, 4], F32)
            xn2 = sb(fin, "xn2", [P, 2, 4, C], F32)
            x2T = sb(fin, "x2T", [P, 2, 2, KC, BANK], F16)
            relu = sb(fin, "relu", [P, 2, BANK], F32)
            r_sq = sb(fin, "r_sq", [P, 2, BANK], F32)
            rT = sb(fin, "rT", [P, 2, 2, KH, BANK], F16)
            res = sb(fin, "res", [P, 2, 4, C], F32)

            ffn_w = sem("ffn_w")
            yT_in = [sem("yT_in_even"), sem("yT_in_odd")]
            resid_in = [sem("resid_in_even"), sem("resid_in_odd")]
            att_ps = sem("att_ps")
            h2_done = sem("h2_done")
            ln_step = sem("ln_step")
            stats_seen = sem("stats_seen")
            var2_ready = sem("var2_ready")
            std2_ready = sem("std2_ready")
            xn2_ready = sem("xn2_ready")
            ln_last = sem("ln_last")
            x2T_ps = sem("x2T_ps")
            x2T_hi = sem("x2T_hi")
            x2T_lo = sem("x2T_lo")
            fc_ps = sem("fc_ps")
            relu_done = sem("relu_done")
            sq_done = sem("sq_done")
            r_hi = sem("r_hi")
            r_lo = sem("r_lo")
            out_ps = sem("out_ps")
            res_done = sem("res_done")
            out_sent = [sem("out_sent_even"), sem("out_sent_odd")]
            FC_BANK, AT_BANK, PR_BANK, XT_BANK = 0, 2, 4, 6

            def half_of(i):
                return i // 2 if isinstance(i, int) else i >> 1

            def groups(eng, start, run):
                start()
                for par in range(2):
                    run(par, par, par == 0, False)
                with eng.Fori(1, GROUPS // 2 - 1) as it:
                    for par in range(2):
                        run(2 * it + par, par, False, False)
                for par in range(2):
                    run(GROUPS - 2 + par, par, False, par == 1)

            with nc.Block() as block:
                @block.sync
                def _(sp):
                    sp.dma_start(wo[:, :, :, :].rearrange("p l k n -> p (l k n)"), wo_scr).then_inc(ffn_w, 16)

                    def load(i, par, wait):
                        if wait:
                            sp.wait_ge(att_ps, 4 * (i - 1))
                            sp.wait_ge(h2_done, 4 * (i - 1))
                        b_, half = (i // 2, i % 2)
                        src = y_scr[b_, half, :, :, :] if isinstance(i, int) else \
                            y_scr.rearrange("b h p k n -> (b h) p k n")[bass.ds(i, 1)] \
                            .rearrange("a p k n -> p (a k) n")
                        sp.dma_start(yT[:, par].rearrange("p k l n -> p k (l n)"), src).then_inc(yT_in[par], 16)
                        e_src = embed_scr.rearrange("(g j p) c -> g p j c", j=4, p=P)
                        e_src = e_src[i] if isinstance(i, int) else \
                            e_src[bass.ds(i, 1)].rearrange("a p j c -> p (a j) c")
                        sp.dma_start(resid[:, par, :, :], e_src).then_inc(resid_in[par], 16)

                    def start():
                        load(0, 0, False)
                        sp.dma_start(wf[:, :, :, :].rearrange("p l k n -> p (l k n)"), wf_scr).then_inc(ffn_w, 16)
                        sp.dma_start(wp[:, :, :, :].rearrange("p l k n -> p (l k n)"), wp_scr).then_inc(ffn_w, 16)
                        load(1, 1, False)

                    def run(i, par, first, last):
                        if not isinstance(i, int) or i + 2 < GROUPS:
                            load(i + 2, par, True)
                        sp.wait_ge(res_done, 4 * (i + 1))
                        o_dst = out.rearrange("b (h j p) c -> (b h) p j c", j=4, p=P)
                        o_dst = o_dst[i] if isinstance(i, int) else \
                            o_dst[bass.ds(i, 1)].rearrange("a p j c -> p (a j) c")
                        sp.dma_start(o_dst, res[:, par, :, :]).then_inc(out_sent[par], 16)

                    groups(sp, start, run)
                    sp.wait_ge(out_sent[0], 16 * (GROUPS // 2))
                    sp.wait_ge(out_sent[1], 16 * (GROUPS // 2))

                @block.gpsimd
                def _(pool):
                    def run(i, par, first, last):
                        for jt in range(KH):
                            pool.wait_ge(relu_done, KH * i + jt + 1)
                            if not (first and jt < 2):
                                pool.wait_ge(r_hi, KH * i + jt - 1)
                                pool.wait_ge(r_lo, KH * i + jt - 1)
                            pool.tensor_tensor(r_sq[:, jt % 2, :], relu[:, jt % 2, :], relu[:, jt % 2, :],
                                               ALU.mult).then_inc(sq_done, 1)

                    groups(pool, lambda: None, run)

                @block.scalar
                def _(act):
                    def high(i, par, first):
                        for k in range(KC):
                            act.wait_ge(x2T_ps, KC * i + k + 1)
                            if k == 0 and not first:
                                act.wait_ge(fc_ps, KH * (i - 1))
                            act.activation(x2T[:, par, 0, k, :], ps[:, XT_BANK + k, :], ACT.Copy).then_inc(x2T_hi, 1)

                    def root(i, par):
                        act.wait_ge(var2_ready, i + 1)
                        act.activation(std2[:, par, :], var2[:, par, :], ACT.Sqrt).then_inc(std2_ready, 1)

                    def start():
                        root(0, 0)
                        high(0, 0, True)

                    def run(i, par, first, last):
                        def r_high(jt):
                            act.wait_ge(sq_done, KH * i + jt + 1)
                            if jt == 0 and not (isinstance(i, int) and i < 2):
                                act.wait_ge(out_ps, 4 * (i - 1))
                            act.activation(rT[:, par, 0, jt, :], r_sq[:, jt % 2, :], ACT.Copy).then_inc(r_hi, 1)

                        for jt in range(KH):
                            act.wait_ge(fc_ps, KH * i + jt + 1)
                            if not (first and jt < 2):
                                act.wait_ge(sq_done, KH * i + jt - 1)
                            act.activation(relu[:, jt % 2, :], ps[:, FC_BANK + jt % 2, :], ACT.Relu,
                                           scale=H_SHIFT).then_inc(relu_done, 1)
                            if jt:
                                r_high(jt - 1)
                        r_high(KH - 1)
                        if not last:
                            root(i + 1, 1 - par)
                            high(i + 1, 1 - par, first)

                    groups(act, start, run)

                @block.vector
                def _(dve):
                    LN = 6

                    def norm2(i, par, first):
                        for j in range(4):
                            dve.wait_ge(att_ps, 4 * i + j + 1)
                            if j == 0:
                                dve.wait_ge(resid_in[par], 16 * (half_of(i) + 1))
                                if not first:
                                    dve.wait_ge(res_done, 4 * (i - 1))
                            dve.scalar_tensor_tensor(h2[:, par, j, :], ps[:, AT_BANK + j % 2, 0:C], coef[:, 1:2],
                                                     resid[:, par, j, :], ALU.mult, ALU.add).then_inc(h2_done, 1)
                        dve.wait_ge(h2_done, 4 * i + 4)
                        for j in range(4):
                            ins = dve.bn_stats(st2[:, par, j, :], h2[:, par, j, :])
                        ins.then_inc(ln_step, 1)
                        dve.wait_ge(ln_step, LN * i + 1)
                        dve.sem_inc(stats_seen, 1)
                        for j in range(4):
                            ins = dve.bn_aggr(mv2[:, par, j, :], st2[:, par, j, :])
                        ins.then_inc(ln_step, 1)
                        dve.wait_ge(ln_step, LN * i + 2)
                        dve.tensor_scalar(var2[:, par, :], mv2[:, par, :, 1], EPS, None, ALU.add).then_inc(var2_ready, 1)
                        dve.wait_ge(std2_ready, i + 1)
                        dve.reciprocal(rstd2[:, par, :], std2[:, par, :]).then_inc(ln_step, 1)
                        dve.wait_ge(ln_step, LN * i + 3)
                        dve.tensor_tensor(tmp2[:, par, :], rstd2[:, par, :], rstd2[:, par, :], ALU.mult) \
                            .then_inc(ln_step, 1)
                        dve.wait_ge(ln_step, LN * i + 4)
                        dve.tensor_tensor(tmp2[:, par, :], tmp2[:, par, :], var2[:, par, :], ALU.mult) \
                            .then_inc(ln_step, 1)
                        dve.wait_ge(ln_step, LN * i + 5)
                        dve.tensor_scalar(tmp2[:, par, :], tmp2[:, par, :], -0.5 * X_SCALE, 1.5 * X_SCALE, ALU.mult,
                                          ALU.add).then_inc(ln_step, 1)
                        dve.wait_ge(ln_step, LN * i + 6)
                        dve.tensor_tensor(rstd2[:, par, :], rstd2[:, par, :], tmp2[:, par, :], ALU.mult) \
                            .then_inc(ln_last, 1)
                        dve.wait_ge(ln_last, i + 1)
                        for j in range(4):
                            if j == 0 and not first:
                                dve.wait_ge(x2T_ps, KC * (i - 1))
                            ins = dve.tensor_scalar(xn2[:, par, j, :], h2[:, par, j, :], mv2[:, par, j, 0:1],
                                                    rstd2[:, par, j:j + 1], ALU.subtract, ALU.mult)
                        ins.then_inc(xn2_ready, 1)

                    def low(i, par):
                        for k in range(KC):
                            dve.wait_ge(x2T_hi, KC * i + k + 1)
                            dve.tensor_tensor(x2T[:, par, 1, k, :], ps[:, XT_BANK + k, :], x2T[:, par, 0, k, :],
                                              ALU.subtract).then_inc(x2T_lo, 1)

                    def start():
                        norm2(0, 0, True)
                        low(0, 0)

                    def run(i, par, first, last):
                        for jt in range(KH):
                            dve.wait_ge(r_hi, KH * i + jt + 1)
                            dve.tensor_tensor(rT[:, par, 1, jt, :], r_sq[:, jt % 2, :], rT[:, par, 0, jt, :],
                                              ALU.subtract).then_inc(r_lo, 1)
                        if not last:
                            norm2(i + 1, 1 - par, first)
                        for j in range(4):
                            dve.wait_ge(out_ps, 4 * i + j + 1)
                            if j == 0 and not (isinstance(i, int) and i < 2):
                                dve.wait_ge(out_sent[par], 16 * half_of(i))
                            dve.scalar_tensor_tensor(res[:, par, j, :], ps[:, PR_BANK + j % 2, 0:C], coef[:, 2:3],
                                                     h2[:, par, j, :], ALU.mult, ALU.add).then_inc(res_done, 1)
                        if not last:
                            low(i + 1, 1 - par)

                    groups(dve, start, run)

                @block.tensor
                def _(pe):
                    def attention_out(i, par, first):
                        pe.wait_ge(yT_in[par], 16 * (half_of(i) + 1))
                        for j in range(4):
                            if not (first and j < 2):
                                pe.wait_ge(h2_done, 4 * i + j - 1)
                            n = 0
                            for k in range(KH):
                                for yl, wl in ((0, 0), (0, 1), (1, 0)):
                                    ins = pe.matmul(ps[:, AT_BANK + j % 2, 0:C], yT[:, par, k, yl, P * j:P * (j + 1)],
                                                    wo[:, wl, k, :], start=(n == 0), stop=(n == 3 * KH - 1))
                                    n += 1
                            ins.then_inc(att_ps, 1)

                    def turn(i, par, first):
                        pe.wait_ge(xn2_ready, i + 1)
                        for k in range(KC):
                            if not first:
                                pe.wait_ge(x2T_lo, KC * (i - 1) + k + 1)
                            for j in range(4):
                                ins = pe.transpose(ps[:, XT_BANK + k, P * j:P * (j + 1)],
                                                   xn2[:, par, j, P * k:P * (k + 1)], ident[:, :])
                            ins.then_inc(x2T_ps, 1)

                    def start():
                        pe.wait_ge(ffn_w, 48)
                        attention_out(0, 0, True)
                        turn(0, 0, True)

                    def run(i, par, first, last):
                        pe.wait_ge(x2T_hi, KC * (i + 1))
                        pe.wait_ge(x2T_lo, KC * (i + 1))
                        for jt in range(KH):
                            if not (first and jt < 2):
                                pe.wait_ge(relu_done, KH * i + jt - 1)
                            n = 0
                            for k in range(KC):
                                for wl, xl in ((0, 0), (0, 1), (1, 0)):
                                    ins = pe.matmul(ps[:, FC_BANK + jt % 2, :], wf[:, wl, k, P * jt:P * (jt + 1)],
                                                    x2T[:, par, xl, k, :], start=(n == 0), stop=(n == 3 * KC - 1))
                                    n += 1
                            ins.then_inc(fc_ps, 1)
                        if not last:
                            attention_out(i + 1, 1 - par, False)
                        pe.wait_ge(r_hi, KH * (i + 1))
                        pe.wait_ge(r_lo, KH * (i + 1))
                        for j in range(4):
                            if not (first and j < 2):
                                pe.wait_ge(res_done, 4 * i + j - 1)
                            n = 0
                            for jt in range(KH):
                                for rl, wl in ((0, 0), (0, 1), (1, 0)):
                                    ins = pe.matmul(ps[:, PR_BANK + j % 2, 0:C], rT[:, par, rl, jt, P * j:P * (j + 1)],
                                                    wp[:, wl, jt, :], start=(n == 0), stop=(n == 3 * KH - 1))
                                    n += 1
                            ins.then_inc(out_ps, 1)
                        if not last:
                            turn(i + 1, 1 - par, False)

                    groups(pe, start, run)


_INS = ['x', 'L0_tok_weights', 'L0_attn_w_kv_down', 'L0_attn_w_kv_up', 'L0_attn_w_q', 'L0_attn_w_out',
        'L0_ffn_fast_b', 'L0_ffn_w_fc', 'L0_ffn_w_proj', 'L0_ffn_u', 'L0_ffn_v', 'L0_ffn_gate']


def kernel(**inputs):
    import numpy as _np
    import concourse.bacc as _bacc
    from concourse import mybir as _mybir
    from concourse.bass_utils import run_bass_kernel_spmd as _run

    nc = _bacc.Bacc("TRN2", target_bir_lowering=False, num_devices=1)
    arrays, args = {}, []
    for name in _INS:
        a = _np.ascontiguousarray(inputs[name])
        if a.ndim == 0:
            a = a.reshape(1)
        arrays[f"in_{name}_dram"] = a
        args.append(nc.dram_tensor(f"in_{name}_dram", a.shape, _mybir.dt.from_np(a.dtype), kind="ExternalInput").ap())
    shape = tuple(inputs['x'].shape) + (inputs['L0_tok_weights'].shape[1],)
    args.append(nc.dram_tensor("out_0_dram", shape, F32, kind="ExternalOutput").ap())
    layer_kernel(nc, *args)
    r = _run(nc, [arrays], core_ids=[0])
    return r.results[0]["out_0_dram"]
```

```python
from contextlib import ExitStack

import concourse.bass as bass
from concourse import mybir

F32 = mybir.dt.float32
F16 = mybir.dt.float16
BF16 = mybir.dt.bfloat16
I32 = mybir.dt.int32
U32 = mybir.dt.uint32
ALU = mybir.AluOpType
ACT = mybir.ActivationFunctionType
AX_X = mybir.AxisListType.X

P = 128
BANK = 512
PAD_TOKEN, SEP_TOKEN = 1, 4
EPS = 1e-5
X_SCALE = 64.0
W_TOP = 64.0
LAT_SHIFT = 2.0 ** -6
Q_SHIFT = 2.0 ** -9
KV_SHIFT = 2.0 ** -17
ONE_ROW = 2.0 ** 15
P_BIAS = 6.931471805599453
H_SHIFT = 2.0 ** -14
EXP_BITS = 0x7F800000


def layer_kernel(nc, tokens, table, w_kvd, w_kvu, w_q, w_out, fast_b, w_fc, w_proj, u, v, gate, out):
    B, T = tokens.shape
    C = table.shape[1]
    R = w_kvd.shape[1]
    HID = w_fc.shape[0]
    RANK = fast_b.shape[0]
    HD = 64
    NH = w_q.shape[1] // HD
    KC = C // P
    TT = T // P
    NT = B * TT
    KH = HID // P
    NP = NH // 2
    TOK = B * T
    GROUPS = TOK // BANK
    assert R == P and T == 2 * BANK and C == 256 and NH * HD == HID

    embed_scr = nc.dram_tensor("embed_scr", [TOK, C], F32, kind="Internal").ap()
    wo_scr = nc.dram_tensor("wo_scr", [P, 2 * KH * C], F16, kind="Internal").ap()
    y_scr = nc.dram_tensor("y_scr", [B, 2, P, NP, 2 * BANK], F16, kind="Internal").ap()

    def batch_and_pair(pr):
        if isinstance(pr, int):
            return pr // NP, pr % NP
        return (pr >> 3).with_bounds(min_val=0, max_val=B - 1), (pr & 7).with_bounds(min_val=0, max_val=NP - 1)

    with ExitStack() as whole:
        def sb(ctx, name, shape, dt):
            return ctx.enter_context(nc.sbuf_tensor(name, shape, dt))

        def sem(name):
            return whole.enter_context(nc.semaphore(name))

        ps = whole.enter_context(nc.psum_tensor("ps", [P, 8, BANK], F32))
        ident = sb(whole, "ident", [P, P], F32)
        ident_big = sb(whole, "ident_big", [P, P], F16)
        causal = sb(whole, "causal", [P, P], F16)
        coef = sb(whole, "coef", [P, 4], F32)

        att = whole.enter_context(ExitStack())
        x_area = sb(att, "x_area", [P, 2 * KC * TOK], F16)
        lat_area = sb(att, "lat_area", [P, 2 * TOK], F16)
        qk_area = sb(att, "qk_area", [P, 8 * T], F16)
        xT = x_area[:, :].rearrange("p (l k n) -> p l k n", l=2, k=KC)
        latT = lat_area[:, :].rearrange("p (l n) -> p l n", l=2)
        q_pair = qk_area[:, 0:4 * T].rearrange("p (r l n) -> p r l n", r=2, l=2)
        k_pair = qk_area[:, 4 * T:8 * T].rearrange("p (r l n) -> p r l n", r=2, l=2)
        YG = KH * 2 * BANK
        yT = [qk_area[:, 0:YG].rearrange("p (k l n) -> p k l n", k=KH, l=2),
              x_area[:, 0:YG].rearrange("p (k l n) -> p k l n", k=KH, l=2)]
        wo = x_area[:, YG:YG + 2 * KH * C]
        wfc_f = x_area[:, YG + 2 * KH * C:].bitcast(F32).rearrange("p (k c) -> p k c", k=KH)
        wpr_f = lat_area[:, 0:2 * KH * C].bitcast(F32).rearrange("p (k n) -> p k n", k=KC)
        assert YG == 8 * T and YG + 4 * KH * C == 2 * KC * TOK
        wq = sb(att, "wq", [P, 2, KC, NH * HD], F16)
        wkvu = sb(att, "wkvu", [P, 2, 2 * NH * HD], F16)
        pow2 = sb(whole, "pow2", [P, 6], F32)
        winv = sb(whole, "winv", [P, 6], F32)
        KVD, KVU, WQ, WO, WF, WP = range(6)
        uT = sb(whole, "uT", [RANK, HID], F32)
        fbv = sb(whole, "fbv", [RANK, C], F32)

        with ExitStack() as pre:
            emb = sb(pre, "emb", [P, NT, C], F32)

            def row(n):
                return emb[0:B, 4 * n:4 * (n + 1), :].rearrange("b i c -> b (i c)")

            tok_i = row(0).bitcast(I32)
            col, keep, valid, sep_at, last_sep, pos = (row(n) for n in range(1, 7))
            pos_idx = sb(pre, "pos_idx", [P, TT, B], U32)
            stats = sb(pre, "stats", [P, NT, 6], F32)
            mv = sb(pre, "mv", [P, NT, 2], F32)
            var = sb(pre, "var", [P, NT], F32)
            std = sb(pre, "std", [P, NT], F32)
            rstd = sb(pre, "rstd", [P, NT], F32)
            tmp = sb(pre, "tmp", [P, NT], F32)
            minus_mean = sb(pre, "minus_mean", [P, NT], F32)
            xn = sb(pre, "xn", [P, 2, 4, C], F32)
            wq_f = sb(pre, "wq_f", [P, KC, NH * HD], F32)
            wkvd_f = sb(pre, "wkvd_f", [P, KC, R], F32)
            wkvu_f = sb(pre, "wkvu_f", [P, 2 * NH * HD], F32)
            wo_f = sb(pre, "wo_f", [P, KH, C], F32)
            wkvd = sb(pre, "wkvd", [P, 2, KC, R], F16)
            wo16 = sb(pre, "wo16", [P, 2, KH, C], F16)
            u_f = sb(pre, "u_f", [P, KH, RANK], F32)
            v_f = sb(pre, "v_f", [RANK, C], F32)
            fbT = sb(pre, "fbT", [RANK, RANK], F32)
            gate_b = sb(pre, "gate_b", [P, 1], F32)
            top = sb(pre, "top", [P, 4], F32)
            top_all = sb(pre, "top_all", [P, 4], F32)

            tokens_in = sem("tokens_in")
            proj_w_in = sem("proj_w_in")
            small_in = sem("small_in")
            consts_set = sem("consts_set")
            dve_step = sem("dve_step")
            pos_ready = sem("pos_ready")
            posT_ready = sem("posT_ready")
            idx_ready = sem("idx_ready")
            rows_in = [sem(f"rows_in_{b}") for b in range(B)]
            top_ready = sem("top_ready")
            top_shared = sem("top_shared")
            winv_ready = sem("winv_ready")
            w_hi = sem("w_hi")
            w_lo = sem("w_lo")
            uT_ready = sem("uT_ready")
            uT_copied = sem("uT_copied")
            fbv_ready = sem("fbv_ready")
            fbv_copied = sem("fbv_copied")
            var_ready = sem("var_ready")
            std_ready = sem("std_ready")
            rstd_ready = sem("rstd_ready")
            xn_ready = sem("xn_ready")
            xT_ps = sem("xT_ps")
            xT_hi = sem("xT_hi")
            xT_lo = sem("xT_lo")
            lat_ps = sem("lat_ps")
            lat_hi = sem("lat_hi")
            lat_lo = sem("lat_lo")
            scratch_out = sem("scratch_out")
            MATRICES = ((KVD, wkvd_f[:, :, :], wkvd), (KVU, wkvu_f[:, :], wkvu),
                        (WQ, wq_f[:, :, :], wq), (WO, wo_f[:, :, :], wo16))

            with nc.Block() as block:
                @block.sync
                def _(sp):
                    sp.dma_start(tok_i[:, :], tokens).then_inc(tokens_in, 16)
                    sp.dma_start(wkvd_f[:, :, :], w_kvd.rearrange("(k p) n -> p k n", p=P)).then_inc(proj_w_in, 16)
                    sp.dma_start(wkvu_f[:, :], w_kvu).then_inc(proj_w_in, 16)
                    sp.dma_start(wq_f[:, :, :], w_q.rearrange("(k p) n -> p k n", p=P)).then_inc(proj_w_in, 16)
                    sp.dma_start(wo_f[:, :, :], w_out.rearrange("(k p) n -> p k n", p=P)).then_inc(proj_w_in, 16)
                    sp.dma_start(u_f[:, :, :], u.rearrange("(k p) r -> p k r", p=P)).then_inc(small_in, 16)
                    sp.dma_start(v_f[:, :], v).then_inc(small_in, 16)
                    sp.dma_start(fbT[:, :], fast_b.rearrange("s r -> r s"),
                                 allow_slow_non_contiguous=True).then_inc(small_in, 16)
                    sp.dma_start(gate_b[:, :], gate.rearrange("(a b) -> a b", b=1).broadcast_to([P, 1])).then_inc(small_in, 16)
                    for b in range(B):
                        sp.wait_ge(rows_in[b], 16 * TT)
                        sp.dma_start(embed_scr[T * b:T * (b + 1)].rearrange("(i p) c -> p i c", p=P),
                                     emb[:, TT * b:TT * (b + 1), :]).then_inc(scratch_out, 16)
                    sp.wait_ge(w_hi, 4)
                    sp.wait_ge(w_lo, 4)
                    sp.dma_start(wo_scr, wo16[:, :, :, :].rearrange("p l k n -> p (l k n)")).then_inc(scratch_out, 16)
                    sp.wait_ge(scratch_out, 16 * (B + 1))

                @block.gpsimd
                def _(pool):
                    pool.iota(col[:, :], [[1, T]], base=0, channel_multiplier=0,
                              allow_small_or_imprecise_dtypes=True).then_inc(consts_set, 1)
                    pool.memset(ident[:, :], 0.0).then_inc(consts_set, 1)
                    pool.memset(ident_big[:, :], 0.0).then_inc(consts_set, 1)
                    pool.memset(causal[:, :], 0.0).then_inc(consts_set, 1)
                    pool.memset(coef[:, 3:4], P_BIAS).then_inc(consts_set, 1)
                    pool.wait_ge(consts_set, 5)
                    pool.affine_select(out=ident[:, :], in_=ident[:, :], compare_op=ALU.not_equal, fill=1.0,
                                       base=0, pattern=[[-1, P]], channel_multiplier=1).then_inc(consts_set, 1)
                    pool.affine_select(out=ident_big[:, :], in_=ident_big[:, :], compare_op=ALU.not_equal,
                                       fill=ONE_ROW, base=0, pattern=[[-1, P]],
                                       channel_multiplier=1).then_inc(consts_set, 1)
                    pool.affine_select(out=causal[:, :], in_=causal[:, :], compare_op=ALU.is_ge, fill=-60000.0,
                                       base=0, pattern=[[-1, P]], channel_multiplier=1).then_inc(consts_set, 1)
                    pool.wait_ge(idx_ready, 1)
                    for i in range(NT):
                        b, t = i // TT, i % TT
                        if i == TT + 2:
                            pool.wait_ge(top_ready, 1)
                            pool.partition_all_reduce(top_all[:, :], top[:, :], P,
                                                      bass.bass_isa.ReduceOp.max).then_inc(top_shared, 1)
                        pool.indirect_dma_start(
                            emb[:, i, :], None, table,
                            bass.IndirectOffsetOnAxis(ap=pos_idx[:, t, b:b + 1], axis=0)).then_inc(rows_in[b], 16)

                @block.vector
                def _(dve):
                    steps = [0]

                    def then(ins):
                        steps[0] += 1
                        ins.then_inc(dve_step, 1)
                        dve.wait_ge(dve_step, steps[0])

                    dve.wait_ge(tokens_in, 16)
                    dve.wait_ge(consts_set, 8)
                    dve.tensor_scalar(keep[:, :], tok_i[:, :], float(PAD_TOKEN), None, ALU.not_equal)
                    then(dve.scalar_tensor_tensor(sep_at[:, :], tok_i[:, :], float(SEP_TOKEN), col[:, :],
                                                  ALU.is_equal, ALU.mult))
                    then(dve.tensor_tensor_scan(last_sep[:, :], sep_at[:, :], sep_at[:, :], 0.0, ALU.max, ALU.max))
                    dve.tensor_tensor_scan(valid[:, :], keep[:, :], keep[:, :], 1.0, ALU.mult, ALU.mult)
                    then(dve.scalar_tensor_tensor(pos[:, :], col[:, :], 1.0, last_sep[:, :], ALU.add, ALU.subtract))
                    dve.tensor_tensor(pos[:, :], pos[:, :], valid[:, :], ALU.mult).then_inc(pos_ready, 1)
                    dve.wait_ge(posT_ready, 1)
                    dve.tensor_scalar(pos_idx[:, :, :], ps[:, 0, 0:NT].rearrange("p (t b) -> p t b", b=B), 1.0, None,
                                      ALU.add).then_inc(idx_ready, 1)

                    dve.wait_ge(proj_w_in, 64)
                    for m, w, _hl in MATRICES:
                        ins = dve.tensor_reduce(top[:, m:m + 1], w, AX_X if m == KVU else mybir.AxisListType.XY, ALU.max,
                                                apply_absolute_value=True)
                    ins.then_inc(top_ready, 1)
                    dve.wait_ge(top_shared, 1)
                    then(dve.tensor_single_scalar(pow2[:, 0:4].bitcast(I32), top_all[:, :].bitcast(I32),
                                                  EXP_BITS, ALU.bitwise_and))
                    then(dve.tensor_scalar(pow2[:, 0:4], pow2[:, 0:4], 2.0 ** -30, None, ALU.max))
                    then(dve.reciprocal(winv[:, 0:4], pow2[:, 0:4]))
                    dve.tensor_scalar(winv[:, 0:4], winv[:, 0:4], W_TOP, None, ALU.mult).then_inc(winv_ready, 1)
                    dve.wait_ge(winv_ready, 1)

                    def weight_low(n):
                        m, w, hl = MATRICES[n]
                        dve.wait_ge(w_hi, n + 1)
                        dve.scalar_tensor_tensor(hl[:, 1], w, winv[:, m:m + 1], hl[:, 0],
                                                 ALU.mult, ALU.subtract).then_inc(w_lo, 1)

                    def norm_scales(b):
                        tiles = slice(TT * b, TT * (b + 1))
                        dve.wait_ge(rows_in[b], 16 * TT)
                        for i in range(TT * b, TT * (b + 1)):
                            ins = dve.bn_stats(stats[:, i, :], emb[:, i, :])
                        then(ins)
                        for i in range(TT * b, TT * (b + 1)):
                            ins = dve.bn_aggr(mv[:, i, :], stats[:, i, :])
                        then(ins)
                        dve.tensor_scalar(var[:, tiles], mv[:, tiles, 1], EPS, None, ALU.add).then_inc(var_ready, 1)
                        dve.wait_ge(std_ready, b + 1)
                        then(dve.reciprocal(rstd[:, tiles], std[:, tiles]))
                        then(dve.tensor_tensor(tmp[:, tiles], rstd[:, tiles], rstd[:, tiles], ALU.mult))
                        then(dve.tensor_tensor(tmp[:, tiles], tmp[:, tiles], var[:, tiles], ALU.mult))
                        then(dve.tensor_scalar(tmp[:, tiles], tmp[:, tiles], -0.5 * X_SCALE, 1.5 * X_SCALE,
                                               ALU.mult, ALU.add))
                        then(dve.tensor_tensor(rstd[:, tiles], rstd[:, tiles], tmp[:, tiles], ALU.mult))
                        dve.scalar_tensor_tensor(minus_mean[:, tiles], mv[:, tiles, 0], -1.0, rstd[:, tiles],
                                                 ALU.mult, ALU.mult).then_inc(rstd_ready, 1)

                    def x_low(g):
                        for k in range(KC):
                            n = KC * g + k
                            dve.wait_ge(xT_hi, n + 1)
                            dve.tensor_tensor(xT[:, 1, k, BANK * g:BANK * (g + 1)], ps[:, n % 4, :],
                                              xT[:, 0, k, BANK * g:BANK * (g + 1)], ALU.subtract).then_inc(xT_lo, 1)

                    def lat_low(g):
                        dve.wait_ge(lat_hi, g + 1)
                        dve.scalar_tensor_tensor(latT[:, 1, BANK * g:BANK * (g + 1)], ps[:, 4 + g % 2, :], LAT_SHIFT,
                                                 latT[:, 0, BANK * g:BANK * (g + 1)],
                                                 ALU.mult, ALU.subtract).then_inc(lat_lo, 1)

                    weight_low(0)
                    for b in range(B):
                        norm_scales(b)
                        if b < 3:
                            weight_low(b + 1)
                        else:
                            then(dve.tensor_tensor(coef[:, 1:2], pow2[:, KVD:KVD + 1], pow2[:, KVU:KVU + 1], ALU.mult))
                            dve.scalar_tensor_tensor(coef[:, 0:1], pow2[:, WQ:WQ + 1], 0.5, coef[:, 1:2],
                                                     ALU.mult, ALU.mult)
                            dve.scalar_tensor_tensor(coef[:, 1:2], pow2[:, WO:WO + 1], 0.5, coef[:, 1:2],
                                                     ALU.mult, ALU.mult)
                        x_low(2 * b)
                        if b:
                            lat_low(2 * b - 1)
                        x_low(2 * b + 1)
                        lat_low(2 * b)
                    lat_low(GROUPS - 1)

                @block.scalar
                def _(act):
                    act.wait_ge(uT_ready, 1)
                    act.activation(uT[:, :], ps[0:RANK, 2:4, :].rearrange("r b n -> r (b n)"),
                                   ACT.Copy).then_inc(uT_copied, 1)
                    act.wait_ge(fbv_ready, 1)
                    act.activation(fbv[:, :], ps[0:RANK, 1, 0:C], ACT.Copy,
                                   scale=gate_b[0:RANK, 0:1]).then_inc(fbv_copied, 1)
                    act.wait_ge(winv_ready, 1)
                    for m, w, hl in MATRICES:
                        act.activation(hl[:, 0], w, ACT.Copy, scale=winv[:, m:m + 1]).then_inc(w_hi, 1)

                    def normalise(g):
                        if g >= 2:
                            act.wait_ge(xT_ps, KC * (g - 1))
                        for j in range(4):
                            i = 4 * g + j
                            ins = act.activation(xn[:, g % 2, j, :], emb[:, i, :], ACT.Identity,
                                                 bias=minus_mean[:, i:i + 1], scale=rstd[:, i:i + 1])
                        ins.then_inc(xn_ready, 1)

                    def x_high(g):
                        for k in range(KC):
                            n = KC * g + k
                            act.wait_ge(xT_ps, n + 1)
                            act.activation(xT[:, 0, k, BANK * g:BANK * (g + 1)], ps[:, n % 4, :],
                                           ACT.Copy).then_inc(xT_hi, 1)

                    def lat_high(g):
                        act.wait_ge(lat_ps, g + 1)
                        act.activation(latT[:, 0, BANK * g:BANK * (g + 1)], ps[:, 4 + g % 2, :], ACT.Copy,
                                       scale=LAT_SHIFT).then_inc(lat_hi, 1)

                    for b in range(B):
                        act.wait_ge(var_ready, b + 1)
                        act.activation(std[:, TT * b:TT * (b + 1)], var[:, TT * b:TT * (b + 1)],
                                       ACT.Sqrt).then_inc(std_ready, 1)
                        act.wait_ge(rstd_ready, b + 1)
                        normalise(2 * b)
                        normalise(2 * b + 1)
                        x_high(2 * b)
                        if b:
                            lat_high(2 * b - 1)
                        x_high(2 * b + 1)
                        lat_high(2 * b)
                    lat_high(GROUPS - 1)

                @block.tensor
                def _(pe):
                    pe.wait_ge(consts_set, 8)
                    pe.wait_ge(pos_ready, 1)
                    for t in range(TT):
                        ins = pe.transpose(ps[:, 0, B * t:B * (t + 1)], pos[:, P * t:P * (t + 1)], ident[0:B, 0:B])
                    ins.then_inc(posT_ready, 1)
                    pe.wait_ge(small_in, 64)
                    for k in range(KH):
                        ins = pe.transpose(ps[0:RANK, 2 + k // 4, P * (k % 4):P * (k % 4 + 1)], u_f[:, k, :],
                                           ident[:, :])
                    ins.then_inc(uT_ready, 1)
                    pe.matmul(ps[0:RANK, 1, 0:C], fbT[:, :], v_f[:, :], start=True, stop=True).then_inc(fbv_ready, 1)
                    pe.wait_ge(idx_ready, 1)
                    pe.wait_ge(uT_copied, 1)
                    pe.wait_ge(fbv_copied, 1)
                    pe.wait_ge(w_lo, 1)

                    def latent(g):
                        pe.wait_ge(xT_hi, KC * (g + 1))
                        pe.wait_ge(xT_lo, KC * (g + 1))
                        if g >= 2:
                            pe.wait_ge(lat_lo, g - 1)
                        n = 0
                        for k in range(KC):
                            for wl, xl in ((0, 0), (0, 1), (1, 0)):
                                ins = pe.matmul(ps[:, 4 + g % 2, :], wkvd[:, wl, k, :],
                                                xT[:, xl, k, BANK * g:BANK * (g + 1)],
                                                start=(n == 0), stop=(n == 3 * KC - 1))
                                n += 1
                        ins.then_inc(lat_ps, 1)

                    for g in range(GROUPS):
                        pe.wait_ge(xn_ready, g + 1)
                        for k in range(KC):
                            n = KC * g + k
                            if n >= 4:
                                pe.wait_ge(xT_lo, n - 3)
                            for j in range(4):
                                ins = pe.transpose(ps[:, n % 4, P * j:P * (j + 1)],
                                                   xn[:, g % 2, j, P * k:P * (k + 1)], ident[:, :])
                            ins.then_inc(xT_ps, 1)
                        if g >= 1:
                            latent(g - 1)
                    latent(GROUPS - 1)

        NHEADS = B * NH
        with ExitStack() as main:
            q1 = sb(main, "q1", [P, 4, T], F16)
            q2 = sb(main, "q2", [P, 4, T], F16)
            k1 = sb(main, "k1", [P, 4, T], F16)
            k2 = sb(main, "k2", [P, 4, T], F16)
            v_hi = sb(main, "v_hi", [P, 2, TT, 2, HD + 1], F16)
            v_lo = sb(main, "v_lo", [P, 2, TT, 2, HD], F16)
            STEPS = [(c, kt) for c in range(2) for kt in range(4 * (c + 1))]
            q_from = [max(BANK * c, P * kt) for c, kt in STEPS]
            width = [BANK * (c + 1) - f for (c, kt), f in zip(STEPS, q_from)]
            at = [sum(width[:s]) for s in range(len(STEPS))]
            NS = len(STEPS)
            AREA = sum(width)
            DIAG = [s for s, (c, kt) in enumerate(STEPS) if kt >= 4 * c]
            FULL = [s for s, (c, kt) in enumerate(STEPS) if kt < 4 * c]
            prob = sb(main, "prob", [P, 2, AREA], F32)
            prob_lo = sb(main, "prob_lo", [P, 2, AREA], F16)
            row_max = sb(main, "row_max", [P, 2, NS], F32)
            row_max_all = sb(main, "row_max_all", [P, 2, TT], F32)
            max_row8 = sb(main, "max_row8", [TT, 2, P], F16)
            rsum = sb(main, "rsum", [P, 2, 4], F32)
            y_st = sb(main, "y_st", [P, 2, TT, P], F32)
            y_sp = sb(main, "y_sp", [P, 2, 2, 2, BANK], F16)
            MSTEPS = [(t, h) for t in range(TT) for h in range(t // 4 + 1)]
            assert len(MSTEPS) == NS
            POOL_LO = [st for st in range(NS) if st in DIAG or st == FULL[0]]
            DVE_LO = FULL[1:]
            ND, NPL, NVL = len(DIAG), len(POOL_LO), len(DVE_LO)

            S_BANK, M_BANK, O_BANK, J_BANK = 0, 2, 4, 6

            ones_set = sem("ones_set")
            qk_ps = sem("qk_ps")
            qk_hi = sem("qk_hi")
            qk_lo = sem("qk_lo")
            laid = [sem("laid_even"), sem("laid_odd")]
            v_ps = sem("v_ps")
            v_hi_done = sem("v_hi_done")
            v_lo_done = sem("v_lo_done")
            mx_ps = sem("mx_ps")
            mx_red = sem("mx_red")
            mx_comb = sem("mx_comb")
            mx_pair = sem("mx_pair")
            mxT_ps = sem("mxT_ps")
            mxT_out = sem("mxT_out")
            mx_row = sem("mx_row")
            sc_ps = sem("sc_ps")
            sc_exp = sem("sc_exp")
            exp_seen = sem("exp_seen")
            masked = sem("masked")
            lo_pool = sem("lo_pool")
            lo_dve = sem("lo_dve")
            pv_ps = sem("pv_ps")
            recip = sem("recip")
            y_norm = sem("y_norm")
            yT_ps = sem("yT_ps")
            yT_hi = sem("yT_hi")
            yT_lo = sem("yT_lo")
            ffn_w = sem("ffn_w")
            yT_in = [sem("yT_in_even"), sem("yT_in_odd")]
            y_out = [sem("y_out_even"), sem("y_out_odd")]

            JOB = (1, 2, 4, 7, 10)
            LO_STEP = (7, 9, 10)

            class Slot:
                def __init__(self, it, k, first=False, zero=False, last=False, tail=False):
                    self.it, self.k = it, k
                    self.first, self.zero, self.last, self.tail = first, zero, last, tail
                    g = 4 * it + k
                    self.g = g
                    known = first or zero or last or tail
                    self.score = not first and not tail
                    self.pv = (not known) or (zero and k >= 1) or last or (tail and k == 0)
                    self.maxima = (not known) or (first and k >= 2) or zero or (last and k < 2)
                    self.row = (not known) or (first and k == 3) or zero or (last and k < 3)
                    self.qk = k % 2 == 0 and (not known or first or zero)
                    self.v = k % 2 == 1 and (not known or (first and k == 3) or zero or (last and k == 1))
                    self.y = k % 2 == 1 and (not known or (zero and k == 3) or last or (tail and k == 1))
                    self.lay = (not known) or (first and k >= 1) or zero or (last and k < 1)
                    self.even = k % 2 == 0

            def slots(eng, run):
                for k in range(4):
                    run(Slot(-1, k, first=True))
                for k in range(4):
                    run(Slot(0, k, zero=True))
                with eng.Fori(1, NHEADS // 4 - 1) as it:
                    for k in range(4):
                        run(Slot(it, k))
                for k in range(4):
                    run(Slot(NHEADS // 4 - 1, k, last=True))
                for k in range(2):
                    run(Slot(NHEADS // 4, k, tail=True))

            with nc.Block() as block:
                @block.sync
                def _(sp):
                    def ffn_operands():
                        sp.wait_ge(qk_ps, 4 * (NHEADS // 2))
                        sp.dma_start(wo, wo_scr).then_inc(ffn_w, 16)
                        sp.dma_start(wfc_f, w_fc.rearrange("(k p) n -> p k n", p=P)).then_inc(ffn_w, 16)
                        sp.wait_ge(v_ps, 2 * (NHEADS // 2))
                        sp.dma_start(wpr_f, w_proj.rearrange("(k p) n -> p k n", p=P)).then_inc(ffn_w, 16)
                        for par in range(2):
                            sp.wait_ge(laid[par], 96 * (NHEADS // 2))
                        for i in range(2):
                            sp.dma_start(yT[i].rearrange("p k l n -> p k (l n)"), y_scr[0, i, :, :, :]).then_inc(yT_in[i], 16)

                    def slot(s):
                        if s.lay:
                            h = s.g + 3
                            r, a = (s.k + 3) % 4, (s.k + 3) % 2
                            pr = 2 * s.it + (s.k + 3) // 2
                            src = ((s.k + 3) // 2) % 2
                            split, used = 4 * pr + 4, NS * (h - 3)
                            if not isinstance(h, int):
                                split, used = sp.snap(split), sp.snap(used)
                            if not s.first and not (s.zero and s.k == 0):
                                sp.wait_ge(sc_ps, used)
                            elif h >= 2:
                                sp.wait_ge(mx_ps, NS * (h - 1))
                            sp.wait_ge(qk_hi, split)
                            sp.wait_ge(qk_lo, split)
                            rows = slice(HD * a, HD * (a + 1))
                            for dst, half, pair_, l in ((q1, 0, q_pair, 0), (q1, 1, q_pair, 1), (q2, 0, q_pair, 0),
                                                        (k1, 0, k_pair, 0), (k1, 1, k_pair, 0), (k2, 0, k_pair, 1)):
                                sp.dma_start(dst[HD * half:HD * (half + 1), r, :],
                                             pair_[rows, src, l, :]).then_inc(laid[a], 16)
                        if s.row:
                            h = s.g + 1
                            sp.wait_ge(mxT_out, h + 1)
                            sp.dma_start(q2[HD:HD + 1, (s.k + 1) % 4, :].rearrange("o (t n) -> o t n", t=TT),
                                         max_row8[:, (s.k + 1) % 2, :]).then_inc(mx_row, 16)
                        if s.last and s.k == 2:
                            ffn_operands()
                        if s.y:
                            pr = 2 * s.it + s.k // 2 - 1
                            par = (s.k // 2 - 1) % 2
                            sp.wait_ge(yT_hi, 2 * pr + 2)
                            sp.wait_ge(yT_lo, 2 * pr + 2)
                            b_, hp = batch_and_pair(pr)
                            for half in range(2):
                                dst = y_scr[bass.ds(b_, 1), half, :, bass.ds(hp, 1), :].rearrange("a p b n -> p (a b n)")
                                sp.dma_start(dst, y_sp[:, par, half, :, :].rearrange("p l n -> p (l n)")) \
                                    .then_inc(y_out[par], 16)

                    slots(sp, slot)

                @block.gpsimd
                def _(pool):
                    pool.memset(k2[HD:HD + 1, :, :], ONE_ROW).then_inc(ones_set, 1)
                    pool.wait_ge(ones_set, 1)
                    pool.memset(v_hi[:, :, :, :, HD:HD + 1], 1.0).then_inc(ones_set, 1)

                    def slot(s):
                        if not s.score:
                            return
                        e = s.k % 2
                        for n, st in enumerate(POOL_LO):
                            block_ = prob[:, e, at[st]:at[st] + P]
                            span = slice(at[st], at[st] + width[st])
                            pool.wait_ge(sc_exp, NS * s.g + st + 1)
                            if st in DIAG:
                                pool.sem_inc(exp_seen, 1)
                                pool.affine_select(out=block_, in_=block_, compare_op=ALU.is_ge, fill=0.0, base=0,
                                                   pattern=[[1, P]], channel_multiplier=-1).then_inc(masked, 1)
                                pool.wait_ge(masked, ND * s.g + DIAG.index(st) + 1)
                            if n == 0 and not (s.zero and s.k < 2):
                                pool.wait_ge(pv_ps, TT * (s.g - 1))
                            pool.tensor_tensor(prob_lo[:, e, span], prob[:, e, span],
                                               prob[:, e, :].bitcast(BF16)[:, 2 * at[st] + 1:2 * (at[st] + width[st]):2],
                                               ALU.subtract).then_inc(lo_pool, 1)

                    slots(pool, slot)

                @block.scalar
                def _(act):
                    def slot(s):
                        e = s.k % 2
                        for st in range(NS):
                            if s.score:
                                act.wait_ge(sc_ps, NS * s.g + st + 1)
                                if st == 0 and not (s.zero and s.k < 2):
                                    act.wait_ge(pv_ps, TT * (s.g - 1))
                                    act.wait_ge(lo_dve, NVL * (s.g - 1))
                                act.activation(prob[:, e, at[st]:at[st] + width[st]],
                                               ps[:, S_BANK + st % 2, 0:width[st]], ACT.Exp,
                                               bias=coef[:, 3:4], scale=coef[:, 0:1]).then_inc(sc_exp, 1)
                            if st == JOB[1] and s.row:
                                h = s.g + 1
                                act.wait_ge(mxT_ps, h + 1)
                                if not (s.first or (s.zero and s.k == 0)):
                                    act.wait_ge(mx_row, 16 * (h - 1))
                                act.activation(max_row8[:, (s.k + 1) % 2, :],
                                               ps[0:TT, J_BANK + (1 if s.even else 0), 0:P], ACT.Copy,
                                               scale=-1.0 / ONE_ROW).then_inc(mxT_out, 1)
                            elif st in JOB and st != JOB[1]:
                                j = (0, None, 1, 2, 3)[JOB.index(st)]
                                if s.even and s.qk:
                                    pr, par = 2 * s.it + s.k // 2 + 2, (s.k // 2) % 2
                                    bank = J_BANK + (0, 0, 1, 0)[j]
                                    act.wait_ge(qk_ps, 4 * pr + j + 1)
                                    if j == 0 and not s.first:
                                        act.wait_ge(laid[0], 96 * (pr - 1))
                                        act.wait_ge(laid[1], 96 * (pr - 1))
                                    dst = (q_pair if j < 2 else k_pair)[:, par, 0, BANK * (j % 2):BANK * (j % 2 + 1)]
                                    act.activation(dst, ps[:, bank, :], ACT.Copy,
                                                   scale=Q_SHIFT if j < 2 else KV_SHIFT).then_inc(qk_hi, 1)
                                if not s.even and j < 2 and s.v:
                                    pr, par = 2 * s.it + s.k // 2 + 1, (s.k // 2 + 1) % 2
                                    act.wait_ge(v_ps, 2 * pr + j + 1)
                                    if st == JOB[0] and not (s.first or (s.zero and s.k == 1)):
                                        act.wait_ge(pv_ps, TT * (s.g - 1))
                                    if st == JOB[0] and s.first:
                                        act.wait_ge(ones_set, 2)
                                    act.activation(v_hi[:, par, 4 * j:4 * j + 4, :, 0:HD],
                                                   ps[:, J_BANK + 1, :].rearrange("p (t a d) -> p t a d", t=4, a=2),
                                                   ACT.Copy, scale=KV_SHIFT).then_inc(v_hi_done, 1)
                                if not s.even and j >= 2 and s.y:
                                    pr, par = 2 * s.it + s.k // 2 - 1, (s.k // 2 - 1) % 2
                                    half = j - 2
                                    act.wait_ge(yT_ps, 2 * pr + half + 1)
                                    if not (s.zero and s.k == 3):
                                        act.wait_ge(y_out[1 - par], 32 * s.it)
                                    act.activation(y_sp[:, par, half, 0, :], ps[:, J_BANK + half, :],
                                                   ACT.Copy).then_inc(yT_hi, 1)

                    slots(act, slot)

                @block.vector
                def _(dve):
                    def normalise(s_it, k, chunk):
                        h = 4 * s_it + k
                        par, a = (k // 2) % 2, k % 2
                        o = ps[:, O_BANK + chunk, 0:4 * (HD + 1)].rearrange("p (t d) -> p t d", t=4)
                        dve.wait_ge(pv_ps, TT * h + 4 * (chunk + 1))
                        dve.reciprocal(rsum[:, chunk, :], o[:, :, HD]).then_inc(recip, 1)
                        dve.wait_ge(recip, 2 * h + chunk + 1)
                        dve.tensor_tensor(y_st[:, par, 4 * chunk:4 * chunk + 4, HD * a:HD * (a + 1)], o[:, :, 0:HD],
                                          rsum[:, chunk, :].unsqueeze(2).broadcast_to([P, 4, HD]),
                                          ALU.mult).then_inc(y_norm, 1)

                    def slot(s):
                        e = s.k % 2
                        for st in range(NS):
                            if s.maxima:
                                h, me = s.g + 2, s.k % 2
                                t, half = MSTEPS[st]
                                w = min(BANK, P * (t + 1) - BANK * half)
                                dve.wait_ge(mx_ps, NS * h + st + 1)
                                if st == 0 and not s.first:
                                    dve.wait_ge(mx_comb, h - 1)
                                c_ = t if half == 0 else TT + t - 4
                                dve.tensor_reduce(row_max[:, me, c_:c_ + 1], ps[:, M_BANK + st % 2, 0:w], AX_X,
                                                  ALU.max).then_inc(mx_red, 1)
                            if s.score and st in LO_STEP:
                                f = DVE_LO[LO_STEP.index(st)]
                                span = slice(at[f], at[f] + width[f])
                                dve.wait_ge(sc_exp, NS * s.g + f + 1)
                                if f == DVE_LO[0] and not (s.zero and s.k < 2):
                                    dve.wait_ge(pv_ps, TT * (s.g - 1))
                                dve.tensor_tensor(prob_lo[:, e, span], prob[:, e, span],
                                                  prob[:, e, :].bitcast(BF16)[:, 2 * at[f] + 1:2 * (at[f] + width[f]):2],
                                                  ALU.subtract).then_inc(lo_dve, 1)
                            if st == 0 and ((not s.first and not s.zero and not s.tail) or (s.zero and s.k >= 2)
                                            or (s.tail and s.k < 2)):
                                kk = s.k - 2
                                normalise(s.it + (kk // 4), kk % 4, 1)
                            if st == 4 and s.pv:
                                kk = s.k - 1
                                normalise(s.it + (kk // 4), kk % 4, 0)
                            if st - 1 in JOB and st - 1 != JOB[1]:
                                j = (0, None, 1, 2, 3)[JOB.index(st - 1)]
                                if s.even and s.qk:
                                    pr, par = 2 * s.it + s.k // 2 + 2, (s.k // 2) % 2
                                    bank = J_BANK + (0, 0, 1, 0)[j]
                                    cols = slice(BANK * (j % 2), BANK * (j % 2 + 1))
                                    hl = q_pair if j < 2 else k_pair
                                    dve.wait_ge(qk_hi, 4 * pr + j + 1)
                                    dve.scalar_tensor_tensor(hl[:, par, 1, cols], ps[:, bank, :],
                                                             Q_SHIFT if j < 2 else KV_SHIFT, hl[:, par, 0, cols],
                                                             ALU.mult, ALU.subtract).then_inc(qk_lo, 1)
                                if not s.even and j < 2 and s.v:
                                    pr, par = 2 * s.it + s.k // 2 + 1, (s.k // 2 + 1) % 2
                                    dve.wait_ge(v_hi_done, 2 * pr + j + 1)
                                    for a in range(2):
                                        ins = dve.scalar_tensor_tensor(
                                            v_lo[:, par, 4 * j:4 * j + 4, a, :],
                                            ps[:, J_BANK + 1, :].rearrange("p (t a d) -> p t a d", t=4, a=2)[:, :, a, :],
                                            KV_SHIFT, v_hi[:, par, 4 * j:4 * j + 4, a, 0:HD], ALU.mult, ALU.subtract)
                                    ins.then_inc(v_lo_done, 1)
                                if not s.even and j >= 2 and s.y:
                                    pr, par = 2 * s.it + s.k // 2 - 1, (s.k // 2 - 1) % 2
                                    half = j - 2
                                    dve.wait_ge(yT_hi, 2 * pr + half + 1)
                                    dve.tensor_tensor(y_sp[:, par, half, 1, :], ps[:, J_BANK + half, :],
                                                      y_sp[:, par, half, 0, :], ALU.subtract).then_inc(yT_lo, 1)
                        if s.maxima:
                            h, me = s.g + 2, s.k % 2
                            dve.wait_ge(mx_red, NS * (h + 1))
                            if not s.first:
                                dve.wait_ge(mxT_ps, h - 1)
                            dve.tensor_copy(row_max_all[:, me, 0:4], row_max[:, me, 0:4]).then_inc(mx_pair, 1)
                            dve.tensor_tensor(row_max_all[:, me, 4:TT], row_max[:, me, 4:TT], row_max[:, me, TT:NS],
                                              ALU.max).then_inc(mx_comb, 1)

                    slots(dve, slot)

                @block.tensor
                def _(pe):
                    passes = ((0, 0), (1, 0), (0, 1))

                    def score_step(s, st):
                        c, kt = STEPS[st]
                        r = s.k % 4
                        keys = slice(P * kt, P * (kt + 1))
                        qs = slice(q_from[st], q_from[st] + width[st])
                        dst = ps[:, S_BANK + st % 2, 0:width[st]]
                        if st == 0:
                            pe.wait_ge(mx_row, 16 * (s.g + 1))
                        if not (s.zero and s.k == 0 and st < 2):
                            pe.wait_ge(sc_exp, NS * s.g + st - 1)
                        pe.matmul(dst, k1[:, r, keys], q1[:, r, qs], start=True, stop=False)
                        pe.matmul(dst, k2[0:HD + 1, r, keys], q2[0:HD + 1, r, qs], start=False,
                                  stop=True).then_inc(sc_ps, 1)

                    def max_step(s, st):
                        h, r = s.g + 2, (s.k + 2) % 4
                        t, half = MSTEPS[st]
                        w = min(BANK, P * (t + 1) - BANK * half)
                        dst = ps[:, M_BANK + st % 2, 0:w]
                        diag = half == t // 4
                        if st == 0:
                            pe.wait_ge(laid[s.k % 2], 96 * (2 * s.it + (s.k + 2) // 2 + 1))
                        if not (s.first and s.k == 2 and st < 2):
                            pe.wait_ge(mx_red, NS * h + st - 1)
                        ins = pe.matmul(dst, q1[:, r, P * t:P * (t + 1)], k1[:, r, BANK * half:BANK * half + w],
                                        start=True, stop=not diag)
                        if diag:
                            ins = pe.matmul(dst[:, w - P:w], ident_big[:, :], causal[:, :], start=False, stop=True)
                        ins.then_inc(mx_ps, 1)

                    def pv_blocks(s, st):
                        kk = (s.k - 1) % 4
                        it = s.it + (s.k - 1) // 4
                        h = 4 * it + kk
                        e, par, a = kk % 2, (kk // 2) % 2, kk % 2
                        tri = [(t, kt) for t in range(TT) for kt in range(t + 1)]
                        for t, kt in tri[3 * st:3 * st + 3]:
                            if t == 0:
                                pe.wait_ge(v_hi_done, 2 * (2 * it + kk // 2) + 2)
                                pe.wait_ge(v_lo_done, 2 * (2 * it + kk // 2) + 2)
                            if kt == 0:
                                pe.wait_ge(lo_pool, NPL * h + POOL_LO.index(DIAG[t]) + 1)
                                if t == 4:
                                    pe.wait_ge(lo_dve, NVL * (h + 1))
                                if t % 4 == 0 and not (s.zero and s.k == 1):
                                    pe.wait_ge(y_norm, 2 * (h - 1) + t // 4 + 1)
                            b = STEPS.index((t // 4, kt))
                            o = at[b] + P * t - q_from[b]
                            dst = ps[:, O_BANK + t // 4, (HD + 1) * (t % 4):(HD + 1) * (t % 4 + 1)]
                            p_hi = prob[:, e, :].bitcast(BF16)[:, 2 * o + 1:2 * (o + P):2]
                            pe.matmul(dst, p_hi, v_hi[:, par, kt, a, :], start=(kt == 0), stop=False)
                            pe.matmul(dst[:, 0:HD], p_hi, v_lo[:, par, kt, a, :], start=False, stop=False)
                            ins = pe.matmul(dst, prob_lo[:, e, o:o + P], v_hi[:, par, kt, a, :], start=False,
                                            stop=(kt == t))
                            if kt == t:
                                ins.then_inc(pv_ps, 1)

                    def job(s, j):
                        if j == 1:
                            if s.row:
                                h = s.g + 1
                                bank = J_BANK + (1 if s.even else 0)
                                pe.wait_ge(mx_comb, h + 1)
                                pe.wait_ge(mx_pair, h + 1)
                                if s.even and (not s.first) and not (s.zero and s.k <= 2):
                                    pe.wait_ge(yT_lo, 2 * (2 * s.it + s.k // 2 - 2) + 2)
                                if not s.even:
                                    if s.qk_before:
                                        pe.wait_ge(qk_lo, 4 * (2 * s.it + s.k // 2 + 2) + 4)
                                pe.transpose(ps[0:TT, bank, 0:P], row_max_all[:, (s.k + 1) % 2, :],
                                             ident[:, :]).then_inc(mxT_ps, 1)
                            return
                        j = (0, None, 1, 2, 3)[j]
                        if s.even and s.qk:
                            pr = 2 * s.it + s.k // 2 + 2
                            bank = J_BANK + (0, 0, 1, 0)[j]
                            b_, hp = batch_and_pair(pr)
                            tok = b_ * T + BANK * (j % 2)
                            if j == 0 and (not s.first) and not (s.zero and s.k <= 2):
                                pe.wait_ge(yT_lo, 2 * (2 * s.it + s.k // 2 - 2) + 1)
                            if j == 0 and s.first and s.k == 2:
                                pe.wait_ge(qk_lo, 4)
                            if j == 0 and s.zero:
                                pe.wait_ge(mxT_out, s.g + 0) if s.k == 0 else pe.wait_ge(mxT_out, s.g)
                            if j == 1 or j == 3:
                                pe.wait_ge(qk_lo, 4 * pr + (1 if j == 1 else 2))
                            if j == 2 and s.row:
                                pe.wait_ge(mxT_out, s.g + 2)
                            n = 0
                            if j < 2:
                                for k in range(KC):
                                    for wl, xl in passes:
                                        ins = pe.matmul(ps[:, bank, :], wq[:, wl, k, bass.ds(hp * P, P)],
                                                        xT[:, xl, k, bass.ds(tok, BANK)], start=(n == 0),
                                                        stop=(n == 3 * KC - 1))
                                        n += 1
                            else:
                                for wl, xl in passes:
                                    ins = pe.matmul(ps[:, bank, :], wkvu[:, wl, bass.ds(hp * P, P)],
                                                    latT[:, xl, bass.ds(tok, BANK)], start=(n == 0), stop=(n == 2))
                                    n += 1
                            ins.then_inc(qk_ps, 1)
                        if not s.even and j < 2 and s.v:
                            pr = 2 * s.it + s.k // 2 + 1
                            b_, hp = batch_and_pair(pr)
                            if j == 0 and s.qk_before:
                                pe.wait_ge(qk_lo, 4 * (2 * s.it + s.k // 2 + 2) + 3)
                            if j == 0 and s.last:
                                pe.wait_ge(mxT_out, s.g + 1)
                            if j == 1:
                                pe.wait_ge(v_lo_done, 2 * pr + 1)
                            for t in range(4):
                                n = 0
                                for vl, ll in passes:
                                    ins = pe.matmul(ps[:, J_BANK + 1, P * t:P * (t + 1)],
                                                    latT[:, ll, bass.ds(b_ * T + BANK * j + P * t, P)],
                                                    wkvu[:, vl, bass.ds(hp * P + NH * HD, P)],
                                                    start=(n == 0), stop=(n == 2))
                                    n += 1
                            ins.then_inc(v_ps, 1)
                        if not s.even and j >= 2 and s.y:
                            pr, par = 2 * s.it + s.k // 2 - 1, (s.k // 2 - 1) % 2
                            half = j - 2
                            pe.wait_ge(y_norm, 4 * pr + 4)
                            if half == 0:
                                if s.row:
                                    pe.wait_ge(mxT_out, s.g + 2)
                                elif s.last or s.tail:
                                    pe.wait_ge(yT_lo, 2 * pr - 1)
                            if half == 1:
                                if s.v:
                                    pe.wait_ge(v_lo_done, 2 * (2 * s.it + s.k // 2 + 1) + 2)
                                elif s.last or s.tail:
                                    pe.wait_ge(yT_lo, 2 * pr)
                            for t in range(4):
                                ins = pe.transpose(ps[:, J_BANK + half, P * t:P * (t + 1)],
                                                   y_st[:, par, 4 * half + t, :], ident[:, :])
                            ins.then_inc(yT_ps, 1)

                    def slot(s):
                        s.qk_before = not s.even and not s.last and not s.tail
                        for st in range(NS):
                            if s.score:
                                score_step(s, st)
                            if s.maxima:
                                max_step(s, st)
                            if s.pv:
                                pv_blocks(s, st)
                            if st in JOB:
                                job(s, JOB.index(st))

                    slots(pe, slot)

        with ExitStack() as fin:
            wo_s = wo.rearrange("p (l k n) -> p l k n", l=2, k=KH)
            wf_s = wq[:, :, :, :]
            wp_s = wkvu[:, :, :].rearrange("p l (k n) -> p l k n", k=KH)
            resid = sb(fin, "resid", [P, 2, 4, C], F32)
            h2 = sb(fin, "h2", [P, 2, 4, C], F32)
            st2 = sb(fin, "st2", [P, 2, 4, 6], F32)
            mv2 = sb(fin, "mv2", [P, 2, 4, 2], F32)
            var2 = sb(fin, "var2", [P, 2, 4], F32)
            std2 = sb(fin, "std2", [P, 2, 4], F32)
            rstd2 = sb(fin, "rstd2", [P, 2, 4], F32)
            tmp2 = sb(fin, "tmp2", [P, 2, 4], F32)
            xn2 = sb(fin, "xn2", [P, 2, 4, C], F32)
            x2T = sb(fin, "x2T", [P, 2, 2, KC, BANK], F16)
            relu = sb(fin, "relu", [P, 2, BANK], F32)
            r_sq = sb(fin, "r_sq", [P, 2, BANK], F32)
            rT = sb(fin, "rT", [P, 2, 2, KH, BANK], F16)
            res = sb(fin, "res", [P, 2, 4, C], F32)
            row_scale = sb(fin, "row_scale", [P, KH + KC], F32)
            half_scale = sb(fin, "half_scale", [P, KH + KC], F32)
            minus_half = sb(fin, "minus_half", [P, KH + KC], F32)
            top2 = sb(fin, "top2", [P, 2], F32)
            top2_all = sb(fin, "top2_all", [P, 2], F32)
            spare = rT[:, :, :, :, :].rearrange("p a l k n -> p (a l k n)").bitcast(F32)
            fc_above, fc_t, pr_above, pr_t = (spare[:, n * KH * C:(n + 1) * KH * C] for n in range(4))
            FC_ROWS, PR_ROWS = slice(0, KH), slice(KH, KH + KC)

            resid_in = [sem("resid_in_even"), sem("resid_in_odd")]
            w_step = sem("w_step")
            pr_tern = sem("pr_tern")
            pr_step = sem("pr_step")
            pr_whole = sem("pr_whole")
            pr_scaled = sem("pr_scaled")
            prT_ps = sem("prT_ps")
            prT_hi = sem("prT_hi")
            prT_lo = sem("prT_lo")
            pr_top = sem("pr_top")
            fc_top = sem("fc_top")
            top2_shared = sem("top2_shared")
            low_rank = sem("low_rank")
            fc_full = sem("fc_full")
            pr_winv = sem("pr_winv")
            fc_winv = sem("fc_winv")
            fcT_ps = sem("fcT_ps")
            fcT_hi = sem("fcT_hi")
            fcT_lo = sem("fcT_lo")
            att_ps = sem("att_ps")
            h2_done = sem("h2_done")
            ln_step = sem("ln_step")
            stats_seen = sem("stats_seen")
            var2_ready = sem("var2_ready")
            std2_ready = sem("std2_ready")
            xn2_ready = sem("xn2_ready")
            ln_last = sem("ln_last")
            x2T_ps = sem("x2T_ps")
            x2T_hi = sem("x2T_hi")
            x2T_lo = sem("x2T_lo")
            fc_ps = sem("fc_ps")
            relu_done = sem("relu_done")
            sq_done = sem("sq_done")
            r_hi = sem("r_hi")
            r_lo = sem("r_lo")
            out_ps = sem("out_ps")
            res_done = sem("res_done")
            out_sent = [sem("out_sent_even"), sem("out_sent_odd")]
            FC_BANK, AT_BANK, PR_BANK, XT_BANK = 0, 2, 4, 6

            def half_of(i):
                return i // 2 if isinstance(i, int) else i >> 1

            def groups(eng, start, run):
                start()
                for par in range(2):
                    run(par, 0, par, par == 0, False)
                with eng.Fori(1, GROUPS // 2 - 1) as it:
                    for par in range(2):
                        run(2 * it + par, it, par, False, False)
                for par in range(2):
                    run(GROUPS - 2 + par, GROUPS // 2 - 1, par, False, par == 1)

            with nc.Block() as block:
                @block.sync
                def _(sp):
                    def load_resid(i, par):
                        e_src = embed_scr.rearrange("(g j p) c -> g p j c", j=4, p=P)
                        e_src = e_src[i] if isinstance(i, int) else \
                            e_src[bass.ds(i, 1)].rearrange("a p j c -> p (a j) c")
                        sp.dma_start(resid[:, par, :, :], e_src).then_inc(resid_in[par], 16)

                    def load(i, par):
                        sp.wait_ge(att_ps, 4 * (i - 1))
                        sp.wait_ge(h2_done, 4 * (i - 1))
                        src = y_scr.rearrange("b h p k n -> (b h) p k n")[bass.ds(i, 1)] \
                            .rearrange("a p k n -> p (a k) n")
                        sp.dma_start(yT[par].rearrange("p k l n -> p k (l n)"), src).then_inc(yT_in[par], 16)
                        load_resid(i, par)

                    def start():
                        load_resid(0, 0)
                        load_resid(1, 1)
                        sp.wait_ge(y_out[0], 32 * (NHEADS // 4))
                        sp.wait_ge(y_out[1], 32 * (NHEADS // 4))

                    def run(i, half, par, first, last):
                        if not isinstance(i, int) or i + 2 < GROUPS:
                            load(i + 2, par)
                        sp.wait_ge(res_done, 4 * (i + 1))
                        o_dst = out.rearrange("b (h j p) c -> (b h) p j c", j=4, p=P)
                        o_dst = o_dst[i] if isinstance(i, int) else \
                            o_dst[bass.ds(i, 1)].rearrange("a p j c -> p (a j) c")
                        sp.dma_start(o_dst, res[:, par, :, :]).then_inc(out_sent[par], 16)

                    groups(sp, start, run)
                    sp.wait_ge(out_sent[0], 16 * (GROUPS // 2))
                    sp.wait_ge(out_sent[1], 16 * (GROUPS // 2))

                @block.gpsimd
                def _(pool):
                    def start():
                        pool.wait_ge(pr_top, 1)
                        pool.partition_all_reduce(top2_all[:, 1:2], top2[:, 1:2], P,
                                                  bass.bass_isa.ReduceOp.max).then_inc(top2_shared, 1)
                        w = wpr_f.rearrange("p k n -> p (k n)")
                        pool.wait_ge(pr_tern, 1)
                        pool.tensor_tensor(pr_t, w, pr_t, ALU.add).then_inc(pr_step, 1)
                        pool.wait_ge(pr_step, 1)
                        pool.tensor_tensor(pr_t, w, pr_t, ALU.subtract).then_inc(pr_whole, 1)
                        pool.wait_ge(fc_top, 1)
                        pool.partition_all_reduce(top2_all[:, 0:1], top2[:, 0:1], P,
                                                  bass.bass_isa.ReduceOp.max).then_inc(top2_shared, 1)

                    def run(i, half, par, first, last):
                        for jt in range(KH):
                            pool.wait_ge(relu_done, KH * i + jt + 1)
                            if not (first and jt < 2):
                                pool.wait_ge(r_hi, KH * i + jt - 1)
                                pool.wait_ge(r_lo, KH * i + jt - 1)
                            pool.tensor_tensor(r_sq[:, jt % 2, :], relu[:, jt % 2, :], relu[:, jt % 2, :],
                                               ALU.mult).then_inc(sq_done, 1)

                    groups(pool, start, run)

                @block.scalar
                def _(act):
                    def high(i, par, first):
                        for k in range(KC):
                            act.wait_ge(x2T_ps, KC * i + k + 1)
                            if k == 0 and not first:
                                act.wait_ge(fc_ps, KH * (i - 1))
                            act.activation(x2T[:, par, 0, k, :], ps[:, XT_BANK + k, :], ACT.Copy).then_inc(x2T_hi, 1)

                    def root(i, par):
                        act.wait_ge(var2_ready, i + 1)
                        act.activation(std2[:, par, :], var2[:, par, :], ACT.Sqrt).then_inc(std2_ready, 1)

                    def start():
                        act.wait_ge(pr_whole, 1)
                        for k in range(KC):
                            act.activation(wpr_f[:, k, :], pr_t[:, HID * k:HID * (k + 1)], ACT.Copy,
                                           scale=row_scale[:, KH + k:KH + k + 1]).then_inc(pr_scaled, 1)
                        act.wait_ge(pr_winv, 1)
                        for n in range(2):
                            act.wait_ge(prT_ps, n + 1)
                            act.activation(wp_s[:, 0, 4 * n:4 * n + 4, :].rearrange("p (b h) n -> p b (h n)", b=2),
                                           ps[:, XT_BANK:XT_BANK + 2, :], ACT.Copy,
                                           scale=winv[:, WP:WP + 1]).then_inc(prT_hi, 1)
                        root(0, 0)
                        act.wait_ge(fc_winv, 1)
                        for k, bank in enumerate((FC_BANK, PR_BANK)):
                            act.wait_ge(fcT_ps, k + 1)
                            act.activation(wf_s[:, 0, k, :].rearrange("p (b n) -> p b n", b=2), ps[:, bank:bank + 2, :],
                                           ACT.Copy, scale=winv[:, WF:WF + 1]).then_inc(fcT_hi, 1)
                        high(0, 0, True)

                    def run(i, half, par, first, last):
                        def r_high(jt):
                            act.wait_ge(sq_done, KH * i + jt + 1)
                            if jt == 0 and not (isinstance(i, int) and i < 2):
                                act.wait_ge(out_ps, 4 * (i - 1))
                            act.activation(rT[:, par, 0, jt, :], r_sq[:, jt % 2, :], ACT.Copy).then_inc(r_hi, 1)

                        for jt in range(KH):
                            act.wait_ge(fc_ps, KH * i + jt + 1)
                            if not (first and jt < 2):
                                act.wait_ge(sq_done, KH * i + jt - 1)
                            act.activation(relu[:, jt % 2, :], ps[:, FC_BANK + jt % 2, :], ACT.Relu,
                                           scale=H_SHIFT).then_inc(relu_done, 1)
                            if jt:
                                r_high(jt - 1)
                        r_high(KH - 1)
                        if not last:
                            root(i + 1, 1 - par)
                            high(i + 1, 1 - par, first)

                    groups(act, start, run)

                @block.vector
                def _(dve):
                    LN = 6
                    w_steps = [0]

                    def then(ins):
                        w_steps[0] += 1
                        ins.then_inc(w_step, 1)
                        dve.wait_ge(w_step, w_steps[0])

                    def residual(i, j, par, first):
                        dve.wait_ge(att_ps, 4 * i + j + 1)
                        if j == 0:
                            dve.wait_ge(resid_in[par], 16 * (half_of(i) + 1))
                            if not first:
                                dve.wait_ge(res_done, 4 * (i - 1))
                        dve.scalar_tensor_tensor(h2[:, par, j, :], ps[:, AT_BANK + j % 2, 0:C], coef[:, 1:2],
                                                 resid[:, par, j, :], ALU.mult, ALU.add).then_inc(h2_done, 1)

                    def norm2(i, par):
                        dve.wait_ge(h2_done, 4 * i + 4)
                        for j in range(4):
                            ins = dve.bn_stats(st2[:, par, j, :], h2[:, par, j, :])
                        ins.then_inc(ln_step, 1)
                        dve.wait_ge(ln_step, LN * i + 1)
                        dve.sem_inc(stats_seen, 1)
                        for j in range(4):
                            ins = dve.bn_aggr(mv2[:, par, j, :], st2[:, par, j, :])
                        ins.then_inc(ln_step, 1)
                        dve.wait_ge(ln_step, LN * i + 2)
                        dve.tensor_scalar(var2[:, par, :], mv2[:, par, :, 1], EPS, None, ALU.add).then_inc(var2_ready, 1)
                        dve.wait_ge(std2_ready, i + 1)
                        dve.reciprocal(rstd2[:, par, :], std2[:, par, :]).then_inc(ln_step, 1)
                        dve.wait_ge(ln_step, LN * i + 3)
                        dve.tensor_tensor(tmp2[:, par, :], rstd2[:, par, :], rstd2[:, par, :], ALU.mult) \
                            .then_inc(ln_step, 1)
                        dve.wait_ge(ln_step, LN * i + 4)
                        dve.tensor_tensor(tmp2[:, par, :], tmp2[:, par, :], var2[:, par, :], ALU.mult) \
                            .then_inc(ln_step, 1)
                        dve.wait_ge(ln_step, LN * i + 5)
                        dve.tensor_scalar(tmp2[:, par, :], tmp2[:, par, :], -0.5 * X_SCALE, 1.5 * X_SCALE, ALU.mult,
                                          ALU.add).then_inc(ln_step, 1)
                        dve.wait_ge(ln_step, LN * i + 6)
                        dve.tensor_tensor(rstd2[:, par, :], rstd2[:, par, :], tmp2[:, par, :], ALU.mult) \
                            .then_inc(ln_last, 1)
                        dve.wait_ge(ln_last, i + 1)
                        for j in range(4):
                            if j == 0 and not (isinstance(i, int) and i < 2):
                                dve.wait_ge(x2T_ps, KC * (i - 1))
                            ins = dve.tensor_scalar(xn2[:, par, j, :], h2[:, par, j, :], mv2[:, par, j, 0:1],
                                                    rstd2[:, par, j:j + 1], ALU.subtract, ALU.mult)
                        ins.then_inc(xn2_ready, 1)

                    def low(i, par):
                        for k in range(KC):
                            dve.wait_ge(x2T_hi, KC * i + k + 1)
                            dve.tensor_tensor(x2T[:, par, 1, k, :], ps[:, XT_BANK + k, :], x2T[:, par, 0, k, :],
                                              ALU.subtract).then_inc(x2T_lo, 1)

                    def row_scales(w, rows):
                        s = row_scale[:, rows]
                        then(dve.tensor_reduce(s, w, AX_X, ALU.add, apply_absolute_value=True))
                        then(dve.tensor_scalar(s, s, 1.0 / w.shape[2], EPS, ALU.mult, ALU.max))
                        dve.tensor_scalar(half_scale[:, rows], s, 0.5, None, ALU.mult)
                        then(dve.tensor_scalar(minus_half[:, rows], s, -0.5, None, ALU.mult))

                    def is_above(w, rows, above):
                        n, row = w.shape[1], w.shape[2]
                        then(dve.tensor_tensor(above.rearrange("p (n r) -> p n r", n=n), w,
                                               half_scale[:, rows].unsqueeze(2).broadcast_to([P, n, row]), ALU.is_gt))

                    def minus_ternary(w, rows, above, t):
                        n, row = w.shape[1], w.shape[2]
                        for k in range(n):
                            r = rows.start + k
                            ins = dve.scalar_tensor_tensor(t[:, row * k:row * (k + 1)], w[:, k, :], minus_half[:, r:r + 1],
                                                           above[:, row * k:row * (k + 1)], ALU.is_lt, ALU.subtract)
                        return ins

                    def exponent(m, col):
                        c, m_ = slice(m, m + 1), slice(col, col + 1)
                        then(dve.tensor_single_scalar(pow2[:, c].bitcast(I32), top2_all[:, m_].bitcast(I32),
                                                      EXP_BITS, ALU.bitwise_and))
                        then(dve.tensor_scalar(pow2[:, c], pow2[:, c], 2.0 ** -30, None, ALU.max))
                        then(dve.reciprocal(winv[:, c], pow2[:, c]))
                        return dve.tensor_scalar(winv[:, c], winv[:, c], W_TOP, None, ALU.mult)

                    def proj_low(n):
                        dve.wait_ge(prT_hi, n + 1)
                        dve.scalar_tensor_tensor(wp_s[:, 1, 4 * n:4 * n + 4, :].rearrange("p (b h) n -> p b (h n)", b=2),
                                                 ps[:, XT_BANK:XT_BANK + 2, :], winv[:, WP:WP + 1],
                                                 wp_s[:, 0, 4 * n:4 * n + 4, :].rearrange("p (b h) n -> p b (h n)", b=2),
                                                 ALU.mult, ALU.subtract).then_inc(prT_lo, 1)

                    def fc_low(k):
                        bank = (FC_BANK, PR_BANK)[k]
                        dve.wait_ge(fcT_hi, k + 1)
                        dve.scalar_tensor_tensor(wf_s[:, 1, k, :].rearrange("p (b n) -> p b n", b=2),
                                                 ps[:, bank:bank + 2, :], winv[:, WF:WF + 1],
                                                 wf_s[:, 0, k, :].rearrange("p (b n) -> p b n", b=2),
                                                 ALU.mult, ALU.subtract).then_inc(fcT_lo, 1)

                    def start():
                        dve.wait_ge(ffn_w, 48)
                        row_scales(wpr_f, PR_ROWS)
                        dve.tensor_reduce(top2[:, 1:2], row_scale[:, PR_ROWS], AX_X, ALU.max).then_inc(pr_top, 1)
                        is_above(wpr_f, PR_ROWS, pr_above)
                        minus_ternary(wpr_f, PR_ROWS, pr_above, pr_t).then_inc(pr_tern, 1)
                        dve.wait_ge(top2_shared, 1)
                        exponent(WP, 1).then_inc(pr_winv, 1)
                        row_scales(wfc_f, FC_ROWS)
                        residual(0, 0, 0, True)
                        is_above(wfc_f, FC_ROWS, fc_above)
                        residual(0, 1, 0, True)
                        then(minus_ternary(wfc_f, FC_ROWS, fc_above, fc_t))
                        residual(0, 2, 0, True)
                        w_all = wfc_f.rearrange("p k c -> p (k c)")
                        then(dve.tensor_tensor(fc_t, w_all, fc_t, ALU.add))
                        residual(0, 3, 0, True)
                        then(dve.tensor_tensor(fc_t, w_all, fc_t, ALU.subtract))
                        dve.wait_ge(low_rank, 1)
                        for k in range(KH):
                            bank = (FC_BANK, PR_BANK)[k // 4] + (k % 4) // 2
                            ins = dve.scalar_tensor_tensor(wfc_f[:, k, :], fc_t[:, C * k:C * (k + 1)],
                                                           row_scale[:, k:k + 1],
                                                           ps[:, bank, C * (k % 2):C * (k % 2 + 1)],
                                                           ALU.mult, ALU.add)
                        ins.then_inc(fc_full, 1)
                        dve.wait_ge(pr_winv, 1)
                        proj_low(0)
                        residual(1, 0, 1, True)
                        dve.wait_ge(fc_full, 1)
                        dve.tensor_reduce(top2[:, 0:1], wfc_f, mybir.AxisListType.XY, ALU.max,
                                          apply_absolute_value=True).then_inc(fc_top, 1)
                        residual(1, 1, 1, True)
                        proj_low(1)
                        dve.wait_ge(top2_shared, 2)
                        exponent(WF, 0).then_inc(fc_winv, 1)
                        dve.wait_ge(fc_winv, 1)
                        norm2(0, 0)
                        residual(1, 2, 1, True)
                        residual(1, 3, 1, True)
                        fc_low(0)
                        fc_low(1)
                        then(dve.tensor_tensor(coef[:, 2:3], pow2[:, WF:WF + 1], pow2[:, WF:WF + 1], ALU.mult))
                        then(dve.scalar_tensor_tensor(coef[:, 2:3], pow2[:, WP:WP + 1], 0.25, coef[:, 2:3],
                                                      ALU.mult, ALU.mult))
                        low(0, 0)

                    def run(i, half, par, first, last):
                        for jt in range(KH):
                            dve.wait_ge(r_hi, KH * i + jt + 1)
                            dve.tensor_tensor(rT[:, par, 1, jt, :], r_sq[:, jt % 2, :], rT[:, par, 0, jt, :],
                                              ALU.subtract).then_inc(r_lo, 1)
                        if not last:
                            if not first:
                                for j in range(4):
                                    residual(i + 1, j, 1 - par, False)
                            norm2(i + 1, 1 - par)
                        for j in range(4):
                            dve.wait_ge(out_ps, 4 * i + j + 1)
                            if j == 0 and not (isinstance(i, int) and i < 2):
                                dve.wait_ge(out_sent[par], 16 * half)
                            dve.scalar_tensor_tensor(res[:, par, j, :], ps[:, PR_BANK + j % 2, 0:C], coef[:, 2:3],
                                                     h2[:, par, j, :], ALU.mult, ALU.add).then_inc(res_done, 1)
                            if j == 1 and not last:
                                low(i + 1, 1 - par)

                    groups(dve, start, run)

                @block.tensor
                def _(pe):
                    def attention_out(i, par, j, first):
                        if j == 0:
                            pe.wait_ge(yT_in[par], 16 * (half_of(i) + 1))
                        if not (first and j < 2):
                            pe.wait_ge(h2_done, 4 * i + j - 1)
                        n = 0
                        for k in range(KH):
                            for yl, wl in ((0, 0), (0, 1), (1, 0)):
                                ins = pe.matmul(ps[:, AT_BANK + j % 2, 0:C], yT[par][:, k, yl, P * j:P * (j + 1)],
                                                wo_s[:, wl, k, :], start=(n == 0), stop=(n == 3 * KH - 1))
                                n += 1
                        ins.then_inc(att_ps, 1)

                    def turn(i, par, first):
                        pe.wait_ge(xn2_ready, i + 1)
                        for k in range(KC):
                            if not first:
                                pe.wait_ge(x2T_lo, KC * (i - 1) + k + 1)
                            for j in range(4):
                                ins = pe.transpose(ps[:, XT_BANK + k, P * j:P * (j + 1)],
                                                   xn2[:, par, j, P * k:P * (k + 1)], ident[:, :])
                            ins.then_inc(x2T_ps, 1)

                    def proj_turn(n):
                        pe.wait_ge(pr_scaled, KC)
                        if n:
                            pe.wait_ge(prT_lo, n)
                        for h in range(4 * n, 4 * n + 4):
                            for k in range(KC):
                                c = C * (h % 2) + P * k
                                ins = pe.transpose(ps[:, XT_BANK + (h % 4) // 2, c:c + P],
                                                   wpr_f[:, k, P * h:P * (h + 1)], ident[:, :])
                        ins.then_inc(prT_ps, 1)

                    def start():
                        for k in range(KH):
                            bank = (FC_BANK, PR_BANK)[k // 4] + (k % 4) // 2
                            ins = pe.matmul(ps[:, bank, C * (k % 2):C * (k % 2 + 1)], uT[:, P * k:P * (k + 1)],
                                            fbv[:, :], start=True, stop=True)
                        ins.then_inc(low_rank, 1)
                        pe.wait_ge(ffn_w, 48)
                        for j in range(4):
                            attention_out(0, 0, j, True)
                        proj_turn(0)
                        attention_out(1, 1, 0, False)
                        attention_out(1, 1, 1, False)
                        proj_turn(1)
                        attention_out(1, 1, 2, False)
                        attention_out(1, 1, 3, False)
                        pe.wait_ge(fc_full, 1)
                        for k, bank in enumerate((FC_BANK, PR_BANK)):
                            for h in range(KH):
                                ins = pe.transpose(ps[:, bank + h // 4, P * (h % 4):P * (h % 4 + 1)],
                                                   wfc_f[:, h, P * k:P * (k + 1)], ident[:, :])
                            ins.then_inc(fcT_ps, 1)
                        pe.wait_ge(prT_lo, 2)
                        turn(0, 0, True)
                        pe.wait_ge(fcT_hi, 2)
                        pe.wait_ge(fcT_lo, 2)

                    def run(i, half, par, first, last):
                        pe.wait_ge(x2T_hi, KC * (i + 1))
                        pe.wait_ge(x2T_lo, KC * (i + 1))
                        for jt in range(KH):
                            if not (first and jt < 2):
                                pe.wait_ge(relu_done, KH * i + jt - 1)
                            n = 0
                            for k in range(KC):
                                for wl, xl in ((0, 0), (0, 1), (1, 0)):
                                    ins = pe.matmul(ps[:, FC_BANK + jt % 2, :], wf_s[:, wl, k, P * jt:P * (jt + 1)],
                                                    x2T[:, par, xl, k, :], start=(n == 0), stop=(n == 3 * KC - 1))
                                    n += 1
                            ins.then_inc(fc_ps, 1)
                        if not last and not first:
                            for j in range(4):
                                attention_out(i + 1, 1 - par, j, False)
                        for j in range(4):
                            if not (first and j < 2):
                                pe.wait_ge(res_done, 4 * i + j - 1)
                            n = 0
                            for jt in range(KH):
                                if j == 0:
                                    pe.wait_ge(r_hi, KH * i + jt + 1)
                                    pe.wait_ge(r_lo, KH * i + jt + 1)
                                for rl, wl in ((0, 0), (0, 1), (1, 0)):
                                    ins = pe.matmul(ps[:, PR_BANK + j % 2, 0:C], rT[:, par, rl, jt, P * j:P * (j + 1)],
                                                    wp_s[:, wl, jt, :], start=(n == 0), stop=(n == 3 * KH - 1))
                                    n += 1
                            ins.then_inc(out_ps, 1)
                            if j == 1 and not last:
                                turn(i + 1, 1 - par, False)

                    groups(pe, start, run)


_INS = ['x', 'L0_tok_weights', 'L0_attn_w_kv_down', 'L0_attn_w_kv_up', 'L0_attn_w_q', 'L0_attn_w_out',
        'L0_ffn_fast_b', 'L0_ffn_w_fc', 'L0_ffn_w_proj', 'L0_ffn_u', 'L0_ffn_v', 'L0_ffn_gate']


def kernel(**inputs):
    import numpy as _np
    import concourse.bacc as _bacc
    from concourse import mybir as _mybir
    from concourse.bass_utils import run_bass_kernel_spmd as _run

    nc = _bacc.Bacc("TRN2", target_bir_lowering=False, num_devices=1)
    arrays, args = {}, []
    for name in _INS:
        a = _np.ascontiguousarray(inputs[name])
        if a.ndim == 0:
            a = a.reshape(1)
        arrays[f"in_{name}_dram"] = a
        args.append(nc.dram_tensor(f"in_{name}_dram", a.shape, _mybir.dt.from_np(a.dtype), kind="ExternalInput").ap())
    shape = tuple(inputs['x'].shape) + (inputs['L0_tok_weights'].shape[1],)
    args.append(nc.dram_tensor("out_0_dram", shape, F32, kind="ExternalOutput").ap())
    layer_kernel(nc, *args)
    r = _run(nc, [arrays], core_ids=[0])
    return r.results[0]["out_0_dram"]
```

```python
from contextlib import ExitStack

import concourse.bass as bass
from concourse import mybir

F32 = mybir.dt.float32
F16 = mybir.dt.float16
BF16 = mybir.dt.bfloat16
I32 = mybir.dt.int32
U32 = mybir.dt.uint32
ALU = mybir.AluOpType
ACT = mybir.ActivationFunctionType
AX_X = mybir.AxisListType.X

P = 128
BANK = 512
PAD_TOKEN, SEP_TOKEN = 1, 4
EPS = 1e-5
X_SCALE = 64.0
W_TOP = 64.0
LAT_SHIFT = 2.0 ** -6
Q_SHIFT = 2.0 ** -9
KV_SHIFT = 2.0 ** -17
MASKED = -2.0 ** 33
ONE_ROW = 2.0 ** 15
P_BIAS = 6.931471805599453
H_SHIFT = 2.0 ** -14
EXP_BITS = 0x7F800000


def layer_kernel(nc, tokens, table, w_kvd, w_kvu, w_q, w_out, fast_b, w_fc, w_proj, u, v, gate, out):
    B, T = tokens.shape
    C = table.shape[1]
    R = w_kvd.shape[1]
    HID = w_fc.shape[0]
    RANK = fast_b.shape[0]
    HD = 64
    NH = w_q.shape[1] // HD
    KC = C // P
    TT = T // P
    NT = B * TT
    KH = HID // P
    NP = NH // 2
    TOK = B * T
    GROUPS = TOK // BANK
    assert R == P and T == 2 * BANK and C == 256 and NH * HD == HID

    embed_scr = nc.dram_tensor("embed_scr", [TOK, C], F32, kind="Internal").ap()
    wo_scr = nc.dram_tensor("wo_scr", [P, 2 * KH * C], F16, kind="Internal").ap()
    y_scr = nc.dram_tensor("y_scr", [B, 2, P, NP, 2 * BANK], F16, kind="Internal").ap()

    def batch_and_pair(pr):
        if isinstance(pr, int):
            return pr // NP, pr % NP
        return (pr >> 3).with_bounds(min_val=0, max_val=B - 1), (pr & 7).with_bounds(min_val=0, max_val=NP - 1)

    with ExitStack() as whole:
        def sb(ctx, name, shape, dt):
            return ctx.enter_context(nc.sbuf_tensor(name, shape, dt))

        def sem(name):
            return whole.enter_context(nc.semaphore(name))

        ps = whole.enter_context(nc.psum_tensor("ps", [P, 8, BANK], F32))
        ident = sb(whole, "ident", [P, P], F32)
        causal = sb(whole, "causal", [P, BANK], F32)
        coef = sb(whole, "coef", [P, 4], F32)

        pow2 = sb(whole, "pow2", [P, 6], F32)
        winv = sb(whole, "winv", [P, 6], F32)
        KVD, KVU, WQ, WO, WF, WP = range(6)
        uT = sb(whole, "uT", [RANK, HID], F32)
        fbv = sb(whole, "fbv", [RANK, C], F32)

        att = whole.enter_context(ExitStack())
        x_area = sb(att, "x_area", [P, 2 * KC * TOK], F16)
        lat_area = sb(att, "lat_area", [P, 2 * TOK], F16)
        qk_area = sb(att, "qk_area", [P, 8 * T], F16)
        xT = x_area[:, :].rearrange("p (l k n) -> p l k n", l=2, k=KC)
        latT = lat_area[:, :].rearrange("p (l n) -> p l n", l=2)
        q_pair = qk_area[:, 0:4 * T].rearrange("p (r l n) -> p r l n", r=2, l=2)
        k_pair = qk_area[:, 4 * T:8 * T].rearrange("p (r l n) -> p r l n", r=2, l=2)
        YG = KH * 2 * BANK
        yT = [qk_area[:, 0:YG].rearrange("p (k l n) -> p k l n", k=KH, l=2),
              x_area[:, 0:YG].rearrange("p (k l n) -> p k l n", k=KH, l=2)]
        wo = x_area[:, YG:YG + 2 * KH * C]
        wfc_f = x_area[:, YG + 2 * KH * C:].bitcast(F32).rearrange("p (k c) -> p k c", k=KH)
        res = lat_area[:, 2 * KH * C:].bitcast(F32).rearrange("p (r j c) -> p r j c", r=2, j=4)
        wpr_f = lat_area[:, 0:2 * KH * C].bitcast(F32).rearrange("p (k n) -> p k n", k=KC)
        assert YG == 8 * T and YG + 4 * KH * C == 2 * KC * TOK
        wq = sb(att, "wq", [P, 2, KC, NH * HD], F16)
        wkvu = sb(att, "wkvu", [P, 2, 2 * NH * HD], F16)

        q1 = sb(att, "q1", [P, 4, T], F16)
        q2 = sb(att, "q2", [P, 4, T], F16)
        k1 = sb(att, "k1", [P, 4, T], F16)
        k2 = sb(att, "k2", [P, 4, T], F16)
        y_sp = sb(att, "y_sp", [P, 2, 2, 2, BANK], F16)
        S_BANK, M_BANK, O_BANK, J_BANK = 0, 2, 4, 6
        JOB_BANK = (J_BANK + 1, J_BANK, J_BANK + 1, J_BANK)
        PASSES = ((0, 0), (1, 0), (0, 1))
        qk_ps = sem("qk_ps")
        qk_hi = sem("qk_hi")
        qk_lo = sem("qk_lo")
        laid = [sem("laid_even"), sem("laid_odd")]

        def project(pe, pr, j, first=0, last=None):
            b_, hp = batch_and_pair(pr)
            tok = b_ * T + BANK * (j % 2)
            products = [(k, wl, xl) for k in range(KC if j < 2 else 1) for wl, xl in PASSES]
            for n in range(first, last or len(products)):
                k, wl, xl = products[n]
                if j < 2:
                    w, x = wq[:, wl, k, bass.ds(hp * P, P)], xT[:, xl, k, bass.ds(tok, BANK)]
                else:
                    w, x = wkvu[:, wl, bass.ds(hp * P, P)], latT[:, xl, bass.ds(tok, BANK)]
                ins = pe.matmul(ps[:, JOB_BANK[j], :], w, x, start=(n == 0), stop=(n == len(products) - 1))
            if n == len(products) - 1:
                ins.then_inc(qk_ps, 1)

        def qk_high(act, par, j):
            dst = (q_pair if j < 2 else k_pair)[:, par, 0, BANK * (j % 2):BANK * (j % 2 + 1)]
            act.activation(dst, ps[:, JOB_BANK[j], :], ACT.Copy, scale=Q_SHIFT if j < 2 else KV_SHIFT).then_inc(qk_hi, 1)

        def qk_low(dve, par, j):
            hl = q_pair if j < 2 else k_pair
            cols = slice(BANK * (j % 2), BANK * (j % 2 + 1))
            dve.scalar_tensor_tensor(hl[:, par, 1, cols], ps[:, JOB_BANK[j], :], Q_SHIFT if j < 2 else KV_SHIFT,
                                     hl[:, par, 0, cols], ALU.mult, ALU.subtract).then_inc(qk_lo, 1)

        def lay_out(sp, src, r, a):
            rows = slice(HD * a, HD * (a + 1))
            for dst, half, pair_, l in ((q1, 0, q_pair, 0), (q1, 1, q_pair, 1), (q2, 0, q_pair, 0),
                                        (k1, 0, k_pair, 0), (k1, 1, k_pair, 0), (k2, 0, k_pair, 1)):
                sp.dma_start(dst[HD * half:HD * (half + 1), r, :], pair_[rows, src, l, :]).then_inc(laid[a], 16)

        with ExitStack() as pre:
            emb = sb(pre, "emb", [P, NT, C], F32)

            def row(n):
                return emb[0:B, 4 * n:4 * (n + 1), :].rearrange("b i c -> b (i c)")

            tok_i = row(0).bitcast(I32)
            col, keep, valid, sep_at, last_sep, pos = (row(n) for n in range(1, 7))
            pos_idx = sb(pre, "pos_idx", [P, TT, B], U32)
            stats = sb(pre, "stats", [P, NT, 6], F32)
            mv = sb(pre, "mv", [P, NT, 2], F32)
            var = sb(pre, "var", [P, NT], F32)
            std = sb(pre, "std", [P, NT], F32)
            rstd = sb(pre, "rstd", [P, NT], F32)
            tmp = sb(pre, "tmp", [P, NT], F32)
            minus_mean = sb(pre, "minus_mean", [P, NT], F32)
            xn = sb(pre, "xn", [P, 2, 4, C], F32)
            wq_f = sb(pre, "wq_f", [P, KC, NH * HD], F32)
            wkvd_f = sb(pre, "wkvd_f", [P, KC, R], F32)
            wkvu_f = sb(pre, "wkvu_f", [P, 2 * NH * HD], F32)
            wo_f = sb(pre, "wo_f", [P, KH, C], F32)
            wkvd = sb(pre, "wkvd", [P, 2, KC, R], F16)
            wo16 = sb(pre, "wo16", [P, 2, KH, C], F16)
            u_f = sb(pre, "u_f", [P, KH, RANK], F32)
            v_f = sb(pre, "v_f", [RANK, C], F32)
            fbT = sb(pre, "fbT", [RANK, RANK], F32)
            gate_b = sb(pre, "gate_b", [P, 1], F32)
            top = sb(pre, "top", [P, 4], F32)
            top_all = sb(pre, "top_all", [P, 4], F32)

            tokens_in = sem("tokens_in")
            proj_w_in = sem("proj_w_in")
            small_in = sem("small_in")
            consts_set = sem("consts_set")
            dve_step = sem("dve_step")
            pos_ready = sem("pos_ready")
            posT_ready = sem("posT_ready")
            idx_ready = sem("idx_ready")
            rows_in = [sem(f"rows_in_{b}") for b in range(B)]
            top_ready = sem("top_ready")
            top_shared = sem("top_shared")
            winv_ready = sem("winv_ready")
            w_hi = sem("w_hi")
            w_lo = sem("w_lo")
            w_scaled = sem("w_scaled")
            w_lo_pool = sem("w_lo_pool")
            uT_ready = sem("uT_ready")
            uT_copied = sem("uT_copied")
            fbv_ready = sem("fbv_ready")
            fbv_copied = sem("fbv_copied")
            var_ready = sem("var_ready")
            std_ready = sem("std_ready")
            rstd_ready = sem("rstd_ready")
            xn_ready = sem("xn_ready")
            xT_ps = sem("xT_ps")
            xT_hi = sem("xT_hi")
            xT_lo = sem("xT_lo")
            lat_ps = sem("lat_ps")
            lat_hi = sem("lat_hi")
            lat_lo = sem("lat_lo")
            scratch_out = sem("scratch_out")
            FIRST_JOBS = (2, 3, 0, 1)
            FIRST_PAIR = {4: (0, 1), 5: (2,), 6: (3,)}
            MATRICES = ((KVD, wkvd_f[:, :, :], wkvd), (KVU, wkvu_f[:, :], wkvu),
                        (WQ, wq_f[:, :, :], wq), (WO, wo_f[:, :, :], wo16))

            with nc.Block() as block:
                @block.sync
                def _(sp):
                    sp.dma_start(tok_i[:, :], tokens).then_inc(tokens_in, 16)
                    sp.dma_start(wkvd_f[:, :, :], w_kvd.rearrange("(k p) n -> p k n", p=P)).then_inc(proj_w_in, 16)
                    sp.dma_start(wkvu_f[:, :], w_kvu).then_inc(proj_w_in, 16)
                    sp.dma_start(wq_f[:, :, :], w_q.rearrange("(k p) n -> p k n", p=P)).then_inc(proj_w_in, 16)
                    sp.dma_start(wo_f[:, :, :], w_out.rearrange("(k p) n -> p k n", p=P)).then_inc(proj_w_in, 16)
                    sp.dma_start(u_f[:, :, :], u.rearrange("(k p) r -> p k r", p=P)).then_inc(small_in, 16)
                    sp.dma_start(v_f[:, :], v).then_inc(small_in, 16)
                    sp.dma_start(fbT[:, :], fast_b.rearrange("s r -> r s"),
                                 allow_slow_non_contiguous=True).then_inc(small_in, 16)
                    sp.dma_start(gate_b[:, :], gate.rearrange("(a b) -> a b", b=1).broadcast_to([P, 1])).then_inc(small_in, 16)
                    for b in range(B):
                        sp.wait_ge(rows_in[b], 16 * TT)
                        sp.dma_start(embed_scr[T * b:T * (b + 1)].rearrange("(i p) c -> p i c", p=P),
                                     emb[:, TT * b:TT * (b + 1), :]).then_inc(scratch_out, 16)
                    sp.wait_ge(w_hi, 4)
                    sp.wait_ge(w_lo_pool, 2)
                    sp.dma_start(wo_scr, wo16[:, :, :, :].rearrange("p l k n -> p (l k n)")).then_inc(scratch_out, 16)
                    sp.wait_ge(qk_hi, 4)
                    sp.wait_ge(qk_lo, 4)
                    lay_out(sp, 0, 0, 0)
                    sp.wait_ge(scratch_out, 16 * (B + 1))

                @block.gpsimd
                def _(pool):
                    pool.iota(col[:, :], [[1, T]], base=0, channel_multiplier=0,
                              allow_small_or_imprecise_dtypes=True).then_inc(consts_set, 1)
                    pool.memset(ident[:, :], 0.0).then_inc(consts_set, 1)
                    pool.memset(causal[:, :], 0.0).then_inc(consts_set, 1)
                    pool.memset(coef[:, 3:4], P_BIAS).then_inc(consts_set, 1)
                    pool.wait_ge(consts_set, 4)
                    pool.affine_select(out=ident[:, :], in_=ident[:, :], compare_op=ALU.not_equal, fill=1.0,
                                       base=0, pattern=[[-1, P]], channel_multiplier=1).then_inc(consts_set, 1)
                    pool.affine_select(out=causal[:, BANK - P:BANK], in_=causal[:, BANK - P:BANK],
                                       compare_op=ALU.is_ge, fill=MASKED,
                                       base=0, pattern=[[-1, P]], channel_multiplier=1).then_inc(consts_set, 1)
                    pool.wait_ge(idx_ready, 1)
                    for i in range(NT):
                        b, t = i // TT, i % TT
                        if i == TT - 2:
                            pool.wait_ge(top_ready, 1)
                            pool.partition_all_reduce(top_all[:, :], top[:, :], P,
                                                      bass.bass_isa.ReduceOp.max).then_inc(top_shared, 1)
                        pool.indirect_dma_start(
                            emb[:, i, :], None, table,
                            bass.IndirectOffsetOnAxis(ap=pos_idx[:, t, b:b + 1], axis=0)).then_inc(rows_in[b], 16)
                    for n in (2, 3):
                        _m, w, hl = MATRICES[n]
                        pool.wait_ge(w_hi, n + 1)
                        pool.wait_ge(w_scaled, n - 1)
                        pool.tensor_tensor(hl[:, 1], w, hl[:, 0], ALU.subtract).then_inc(w_lo_pool, 1)

                @block.vector
                def _(dve):
                    steps = [0]

                    def then(ins):
                        steps[0] += 1
                        ins.then_inc(dve_step, 1)
                        dve.wait_ge(dve_step, steps[0])

                    dve.wait_ge(tokens_in, 16)
                    dve.wait_ge(consts_set, 6)
                    dve.tensor_scalar(keep[:, :], tok_i[:, :], float(PAD_TOKEN), None, ALU.not_equal)
                    then(dve.scalar_tensor_tensor(sep_at[:, :], tok_i[:, :], float(SEP_TOKEN), col[:, :],
                                                  ALU.is_equal, ALU.mult))
                    then(dve.tensor_tensor_scan(last_sep[:, :], sep_at[:, :], sep_at[:, :], 0.0, ALU.max, ALU.max))
                    dve.tensor_tensor_scan(valid[:, :], keep[:, :], keep[:, :], 1.0, ALU.mult, ALU.mult)
                    then(dve.scalar_tensor_tensor(pos[:, :], col[:, :], 1.0, last_sep[:, :], ALU.add, ALU.subtract))
                    dve.tensor_tensor(pos[:, :], pos[:, :], valid[:, :], ALU.mult).then_inc(pos_ready, 1)
                    dve.wait_ge(posT_ready, 1)
                    dve.tensor_scalar(pos_idx[:, :, :], ps[:, 0, 0:NT].rearrange("p (t b) -> p t b", b=B), 1.0, None,
                                      ALU.add).then_inc(idx_ready, 1)

                    dve.wait_ge(proj_w_in, 64)
                    for m, w, _hl in MATRICES:
                        ins = dve.tensor_reduce(top[:, m:m + 1], w, AX_X if m == KVU else mybir.AxisListType.XY, ALU.max,
                                                apply_absolute_value=True)
                    ins.then_inc(top_ready, 1)
                    dve.wait_ge(top_shared, 1)
                    then(dve.tensor_single_scalar(pow2[:, 0:4].bitcast(I32), top_all[:, :].bitcast(I32),
                                                  EXP_BITS, ALU.bitwise_and))
                    then(dve.tensor_scalar(pow2[:, 0:4], pow2[:, 0:4], 2.0 ** -30, None, ALU.max))
                    then(dve.reciprocal(winv[:, 0:4], pow2[:, 0:4]))
                    dve.tensor_scalar(winv[:, 0:4], winv[:, 0:4], W_TOP, None, ALU.mult).then_inc(winv_ready, 1)
                    dve.wait_ge(winv_ready, 1)

                    def weight_low(n):
                        m, w, hl = MATRICES[n]
                        dve.wait_ge(w_hi, n + 1)
                        dve.scalar_tensor_tensor(hl[:, 1], w, winv[:, m:m + 1], hl[:, 0],
                                                 ALU.mult, ALU.subtract).then_inc(w_lo, 1)

                    def statistics(b):
                        tiles = slice(TT * b, TT * (b + 1))
                        dve.wait_ge(rows_in[b], 16 * TT)
                        for i in range(TT * b, TT * (b + 1)):
                            ins = dve.bn_stats(stats[:, i, :], emb[:, i, :])
                        then(ins)
                        for i in range(TT * b, TT * (b + 1)):
                            ins = dve.bn_aggr(mv[:, i, :], stats[:, i, :])
                        then(ins)
                        dve.tensor_scalar(var[:, tiles], mv[:, tiles, 1], EPS, None, ALU.add).then_inc(var_ready, 1)

                    def norm_scales(b):
                        tiles = slice(TT * b, TT * (b + 1))
                        dve.wait_ge(std_ready, b + 1)
                        then(dve.reciprocal(rstd[:, tiles], std[:, tiles]))
                        then(dve.tensor_tensor(tmp[:, tiles], rstd[:, tiles], rstd[:, tiles], ALU.mult))
                        then(dve.tensor_tensor(tmp[:, tiles], tmp[:, tiles], var[:, tiles], ALU.mult))
                        then(dve.tensor_scalar(tmp[:, tiles], tmp[:, tiles], -0.5 * X_SCALE, 1.5 * X_SCALE,
                                               ALU.mult, ALU.add))
                        then(dve.tensor_tensor(rstd[:, tiles], rstd[:, tiles], tmp[:, tiles], ALU.mult))
                        dve.scalar_tensor_tensor(minus_mean[:, tiles], mv[:, tiles, 0], -1.0, rstd[:, tiles],
                                                 ALU.mult, ALU.mult).then_inc(rstd_ready, 1)

                    def x_low(g):
                        for k in range(KC):
                            n = KC * g + k
                            dve.wait_ge(xT_hi, n + 1)
                            dve.tensor_tensor(xT[:, 1, k, BANK * g:BANK * (g + 1)], ps[:, n % 4, :],
                                              xT[:, 0, k, BANK * g:BANK * (g + 1)], ALU.subtract).then_inc(xT_lo, 1)

                    def lat_low(g):
                        dve.wait_ge(lat_hi, g + 1)
                        dve.scalar_tensor_tensor(latT[:, 1, BANK * g:BANK * (g + 1)], ps[:, 4 + g % 2, :], LAT_SHIFT,
                                                 latT[:, 0, BANK * g:BANK * (g + 1)],
                                                 ALU.mult, ALU.subtract).then_inc(lat_lo, 1)

                    def coefficients():
                        then(dve.tensor_tensor(coef[:, 1:2], pow2[:, KVD:KVD + 1], pow2[:, KVU:KVU + 1], ALU.mult))
                        dve.scalar_tensor_tensor(coef[:, 0:1], pow2[:, WQ:WQ + 1], 0.5, coef[:, 1:2],
                                                 ALU.mult, ALU.mult)
                        dve.scalar_tensor_tensor(coef[:, 1:2], pow2[:, WO:WO + 1], 0.5, coef[:, 1:2],
                                                 ALU.mult, ALU.mult)

                    weight_low(0)
                    statistics(0)
                    weight_low(1)
                    norm_scales(0)
                    coefficients()
                    for g in range(GROUPS):
                        b = g // 2 + 1
                        if g % 2 == 0 and b < B:
                            statistics(b)
                        x_low(g)
                        if g % 2 == 0 and b < B:
                            norm_scales(b)
                        if g >= 2:
                            lat_low(g - 2)
                        for n in FIRST_PAIR.get(g, ()):
                            dve.wait_ge(qk_hi, n + 1)
                            qk_low(dve, 0, FIRST_JOBS[n])
                    lat_low(GROUPS - 2)
                    lat_low(GROUPS - 1)

                @block.scalar
                def _(act):
                    act.wait_ge(uT_ready, 1)
                    act.activation(uT[:, :], ps[0:RANK, 2:4, :].rearrange("r b n -> r (b n)"),
                                   ACT.Copy).then_inc(uT_copied, 1)
                    act.wait_ge(fbv_ready, 1)
                    act.activation(fbv[:, :], ps[0:RANK, 1, 0:C], ACT.Copy,
                                   scale=gate_b[0:RANK, 0:1]).then_inc(fbv_copied, 1)
                    act.wait_ge(winv_ready, 1)
                    for m, w, hl in MATRICES:
                        act.activation(hl[:, 0], w, ACT.Copy, scale=winv[:, m:m + 1]).then_inc(w_hi, 1)

                    def scale_for_pool(n):
                        m, w, _hl = MATRICES[n]
                        act.wait_ge(w_hi, n + 1)
                        act.activation(w, w, ACT.Copy, scale=winv[:, m:m + 1]).then_inc(w_scaled, 1)

                    def normalise(g):
                        if g >= 2:
                            act.wait_ge(xT_ps, KC * (g - 1))
                        for j in range(4):
                            i = 4 * g + j
                            ins = act.activation(xn[:, g % 2, j, :], emb[:, i, :], ACT.Identity,
                                                 bias=minus_mean[:, i:i + 1], scale=rstd[:, i:i + 1])
                        ins.then_inc(xn_ready, 1)

                    def x_high(g):
                        for k in range(KC):
                            n = KC * g + k
                            act.wait_ge(xT_ps, n + 1)
                            act.activation(xT[:, 0, k, BANK * g:BANK * (g + 1)], ps[:, n % 4, :],
                                           ACT.Copy).then_inc(xT_hi, 1)

                    def lat_high(g):
                        act.wait_ge(lat_ps, g + 1)
                        act.activation(latT[:, 0, BANK * g:BANK * (g + 1)], ps[:, 4 + g % 2, :], ACT.Copy,
                                       scale=LAT_SHIFT).then_inc(lat_hi, 1)

                    def root(b):
                        act.wait_ge(var_ready, b + 1)
                        act.activation(std[:, TT * b:TT * (b + 1)], var[:, TT * b:TT * (b + 1)],
                                       ACT.Sqrt).then_inc(std_ready, 1)

                    root(0)
                    act.wait_ge(rstd_ready, 1)
                    normalise(0)
                    normalise(1)
                    for g in range(GROUPS):
                        x_high(g)
                        if g % 2 == 0 and g // 2 + 1 < B:
                            root(g // 2 + 1)
                        if g < 2:
                            scale_for_pool(g + 2)
                        if g >= 2:
                            lat_high(g - 2)
                        for n in FIRST_PAIR.get(g, ()):
                            act.wait_ge(qk_ps, n + 1)
                            qk_high(act, 0, FIRST_JOBS[n])
                        if g + 2 < GROUPS:
                            act.wait_ge(rstd_ready, g // 2 + 2)
                            normalise(g + 2)
                    lat_high(GROUPS - 2)
                    lat_high(GROUPS - 1)

                @block.tensor
                def _(pe):
                    pe.wait_ge(consts_set, 6)
                    pe.wait_ge(pos_ready, 1)
                    for t in range(TT):
                        ins = pe.transpose(ps[:, 0, B * t:B * (t + 1)], pos[:, P * t:P * (t + 1)], ident[0:B, 0:B])
                    ins.then_inc(posT_ready, 1)
                    pe.wait_ge(small_in, 64)
                    for k in range(KH):
                        ins = pe.transpose(ps[0:RANK, 2 + k // 4, P * (k % 4):P * (k % 4 + 1)], u_f[:, k, :],
                                           ident[:, :])
                    ins.then_inc(uT_ready, 1)
                    pe.matmul(ps[0:RANK, 1, 0:C], fbT[:, :], v_f[:, :], start=True, stop=True).then_inc(fbv_ready, 1)
                    pe.wait_ge(idx_ready, 1)
                    pe.wait_ge(uT_copied, 1)
                    pe.wait_ge(fbv_copied, 1)
                    pe.wait_ge(w_lo, 1)

                    def latent(g):
                        pe.wait_ge(xT_hi, KC * (g + 1))
                        pe.wait_ge(xT_lo, KC * (g + 1))
                        if g >= 2:
                            pe.wait_ge(lat_lo, g - 1)
                        n = 0
                        for k in range(KC):
                            for wl, xl in ((0, 0), (0, 1), (1, 0)):
                                ins = pe.matmul(ps[:, 4 + g % 2, :], wkvd[:, wl, k, :],
                                                xT[:, xl, k, BANK * g:BANK * (g + 1)],
                                                start=(n == 0), stop=(n == 3 * KC - 1))
                                n += 1
                        ins.then_inc(lat_ps, 1)

                    for g in range(GROUPS):
                        pe.wait_ge(xn_ready, g + 1)
                        for k in range(KC):
                            n = KC * g + k
                            if n >= 4:
                                pe.wait_ge(xT_lo, n - 3)
                            for j in range(4):
                                ins = pe.transpose(ps[:, n % 4, P * j:P * (j + 1)],
                                                   xn[:, g % 2, j, P * k:P * (k + 1)], ident[:, :])
                            ins.then_inc(xT_ps, 1)
                        if g >= 1:
                            latent(g - 1)
                        for n in FIRST_PAIR.get(g, ()):
                            if n == 0:
                                pe.wait_ge(w_lo, 2)
                                pe.wait_ge(lat_lo, 2)
                            if n == 2:
                                pe.wait_ge(w_lo_pool, 1)
                            if n >= 2:
                                pe.wait_ge(qk_lo, n - 1)
                            project(pe, 0, FIRST_JOBS[n])
                    latent(GROUPS - 1)

        NHEADS = B * NH
        with ExitStack() as main:
            v_hi = sb(main, "v_hi", [P, 2, TT, 2, HD + 1], F16)
            v_lo = sb(main, "v_lo", [P, 2, TT, 2, HD], F16)
            STEPS = [(c, kt) for c in range(2) for kt in range(4 * (c + 1))]
            q_from = [max(BANK * c, P * kt) for c, kt in STEPS]
            width = [BANK * (c + 1) - f for (c, kt), f in zip(STEPS, q_from)]
            at = [sum(width[:s]) for s in range(len(STEPS))]
            NS = len(STEPS)
            AREA = sum(width)
            DIAG = [s for s, (c, kt) in enumerate(STEPS) if kt >= 4 * c]
            FULL = [s for s, (c, kt) in enumerate(STEPS) if kt < 4 * c]
            prob = sb(main, "prob", [P, 2, AREA], F32)
            prob_lo = sb(main, "prob_lo", [P, 2, AREA], F16)
            masked_scores = sb(main, "masked_scores", [P, 2, BANK], F32)
            row_max = sb(main, "row_max", [P, 2, 2, TT], F32)
            row_max_all = sb(main, "row_max_all", [P, 2, TT], F32)
            max_row8 = sb(main, "max_row8", [TT, 2, P], F16)
            rsum = sb(main, "rsum", [P, 2, 4], F32)
            y_st = sb(main, "y_st", [P, 2, TT, P], F32)
            MSTEPS = [(t, h) for t in range(TT) for h in range(t // 4 + 1)]
            assert len(MSTEPS) == NS
            POOL_LO = [st for st in range(NS) if st in DIAG or st == FULL[0]]
            DVE_LO = FULL[1:]
            ND, NPL, NVL = len(DIAG), len(POOL_LO), len(DVE_LO)

            ones_set = sem("ones_set")
            v_ps = sem("v_ps")
            v_hi_done = sem("v_hi_done")
            v_lo_done = sem("v_lo_done")
            mx_ps = sem("mx_ps")
            scores_seen = sem("scores_seen")
            mx_red = sem("mx_red")
            mx_comb = sem("mx_comb")
            mxT_ps = sem("mxT_ps")
            mxT_out = sem("mxT_out")
            mx_row = sem("mx_row")
            sc_ps = sem("sc_ps")
            sc_exp = sem("sc_exp")
            exp_seen = sem("exp_seen")
            masked = sem("masked")
            lo_pool = sem("lo_pool")
            lo_dve = sem("lo_dve")
            pv_ps = sem("pv_ps")
            recip = sem("recip")
            y_norm = sem("y_norm")
            yT_ps = sem("yT_ps")
            yT_hi = sem("yT_hi")
            yT_lo = sem("yT_lo")
            ffn_w = sem("ffn_w")
            yT_in = [sem("yT_in_even"), sem("yT_in_odd")]
            y_out = [sem("y_out_even"), sem("y_out_odd")]

            JOB = (1, 2, 5, 7, 10)
            LO_STEP = (7, 9, 10)

            class Slot:
                def __init__(self, it, k, first=False, zero=False, last=False, tail=False):
                    self.it, self.k = it, k
                    self.first, self.zero, self.last, self.tail = first, zero, last, tail
                    g = 4 * it + k
                    self.g = g
                    known = first or zero or last or tail
                    self.score = not first and not tail
                    self.pv = (not known) or (zero and k >= 1) or last or (tail and k == 0)
                    self.maxima = (not known) or (first and k >= 2) or zero or (last and k < 2)
                    self.row = (not known) or (first and k == 3) or zero or (last and k < 3)
                    self.qk = k % 2 == 0 and (not known or (first and k == 2) or zero)
                    self.v = k % 2 == 1 and (not known or (first and k == 3) or zero or (last and k == 1))
                    self.y = k % 2 == 1 and (not known or (zero and k == 3) or last or (tail and k == 1))
                    self.lay = (not known) or (first and k >= 2) or zero or (last and k < 1)
                    self.even = k % 2 == 0

            def slots(eng, run):
                for k in range(4):
                    run(Slot(-1, k, first=True))
                for k in range(4):
                    run(Slot(0, k, zero=True))
                with eng.Fori(1, NHEADS // 4 - 1) as it:
                    for k in range(4):
                        run(Slot(it, k))
                for k in range(4):
                    run(Slot(NHEADS // 4 - 1, k, last=True))
                for k in range(2):
                    run(Slot(NHEADS // 4, k, tail=True))

            with nc.Block() as block:
                @block.sync
                def _(sp):
                    def ffn_operands():
                        sp.wait_ge(qk_ps, 4 * (NHEADS // 2))
                        sp.dma_start(wo, wo_scr).then_inc(ffn_w, 16)
                        sp.dma_start(wfc_f, w_fc.rearrange("(k p) n -> p k n", p=P)).then_inc(ffn_w, 16)
                        sp.wait_ge(v_ps, 2 * (NHEADS // 2))
                        sp.dma_start(wpr_f, w_proj.rearrange("(k p) n -> p k n", p=P)).then_inc(ffn_w, 16)
                        for par in range(2):
                            sp.wait_ge(laid[par], 96 * (NHEADS // 2))
                        for i in range(2):
                            sp.dma_start(yT[i].rearrange("p k l n -> p k (l n)"), y_scr[0, i, :, :, :]).then_inc(yT_in[i], 16)

                    def slot(s):
                        if s.lay:
                            h = s.g + 3
                            r, a = (s.k + 3) % 4, (s.k + 3) % 2
                            pr = 2 * s.it + (s.k + 3) // 2
                            src = ((s.k + 3) // 2) % 2
                            split, used = 4 * pr + 4, NS * (h - 3)
                            if not isinstance(h, int):
                                split, used = sp.snap(split), sp.snap(used)
                            if not s.first and not (s.zero and s.k == 0):
                                sp.wait_ge(sc_ps, used)
                            elif h >= 2:
                                sp.wait_ge(mx_ps, NS * (h - 1))
                            sp.wait_ge(qk_hi, split)
                            sp.wait_ge(qk_lo, split)
                            lay_out(sp, src, r, a)
                        if s.row:
                            h = s.g + 1
                            sp.wait_ge(mxT_out, h + 1)
                            sp.dma_start(q2[HD:HD + 1, (s.k + 1) % 4, :].rearrange("o (t n) -> o t n", t=TT),
                                         max_row8[:, (s.k + 1) % 2, :]).then_inc(mx_row, 16)
                        if s.last and s.k == 2:
                            ffn_operands()
                        if s.y:
                            pr = 2 * s.it + s.k // 2 - 1
                            par = (s.k // 2 - 1) % 2
                            sp.wait_ge(yT_hi, 2 * pr + 2)
                            sp.wait_ge(yT_lo, 2 * pr + 2)
                            b_, hp = batch_and_pair(pr)
                            for half in range(2):
                                dst = y_scr[bass.ds(b_, 1), half, :, bass.ds(hp, 1), :].rearrange("a p b n -> p (a b n)")
                                sp.dma_start(dst, y_sp[:, par, half, :, :].rearrange("p l n -> p (l n)")) \
                                    .then_inc(y_out[par], 16)

                    slots(sp, slot)

                @block.gpsimd
                def _(pool):
                    pool.memset(k2[HD:HD + 1, :, :], ONE_ROW).then_inc(ones_set, 1)
                    pool.wait_ge(ones_set, 1)
                    pool.memset(v_hi[:, :, :, :, HD:HD + 1], 1.0).then_inc(ones_set, 1)
                    pool.memset(row_max[:, :, 1, 0:4], MASKED).then_inc(ones_set, 1)

                    def slot(s):
                        if not s.score:
                            return
                        e = s.k % 2
                        for n, st in enumerate(POOL_LO):
                            block_ = prob[:, e, at[st]:at[st] + P]
                            span = slice(at[st], at[st] + width[st])
                            pool.wait_ge(sc_exp, NS * s.g + st + 1)
                            if st in DIAG:
                                pool.sem_inc(exp_seen, 1)
                                pool.affine_select(out=block_, in_=block_, compare_op=ALU.is_ge, fill=0.0, base=0,
                                                   pattern=[[1, P]], channel_multiplier=-1).then_inc(masked, 1)
                                pool.wait_ge(masked, ND * s.g + DIAG.index(st) + 1)
                            if n == 0 and not (s.zero and s.k < 2):
                                pool.wait_ge(pv_ps, TT * (s.g - 1))
                            pool.tensor_tensor(prob_lo[:, e, span], prob[:, e, span],
                                               prob[:, e, :].bitcast(BF16)[:, 2 * at[st] + 1:2 * (at[st] + width[st]):2],
                                               ALU.subtract).then_inc(lo_pool, 1)

                    slots(pool, slot)

                @block.scalar
                def _(act):
                    def slot(s):
                        e = s.k % 2
                        for st in range(NS):
                            if s.score:
                                act.wait_ge(sc_ps, NS * s.g + st + 1)
                                if st == 0 and not (s.zero and s.k < 2):
                                    act.wait_ge(pv_ps, TT * (s.g - 1))
                                    act.wait_ge(lo_dve, NVL * (s.g - 1))
                                act.activation(prob[:, e, at[st]:at[st] + width[st]],
                                               ps[:, S_BANK + st % 2, 0:width[st]], ACT.Exp,
                                               bias=coef[:, 3:4], scale=coef[:, 0:1]).then_inc(sc_exp, 1)
                            if st == JOB[1] and s.row:
                                h = s.g + 1
                                act.wait_ge(mxT_ps, h + 1)
                                if not (s.first or (s.zero and s.k == 0)):
                                    act.wait_ge(mx_row, 16 * (h - 1))
                                act.activation(max_row8[:, (s.k + 1) % 2, :],
                                               ps[0:TT, J_BANK, 0:P], ACT.Copy,
                                               scale=-1.0 / ONE_ROW).then_inc(mxT_out, 1)
                            elif st in JOB and st != JOB[1]:
                                j = (0, None, 1, 2, 3)[JOB.index(st)]
                                if s.even and s.qk:
                                    pr, par = 2 * s.it + s.k // 2 + 2, (s.k // 2) % 2
                                    act.wait_ge(qk_ps, 4 * pr + j + 1)
                                    if j == 0 and not s.first:
                                        act.wait_ge(laid[0], 96 * (pr - 1))
                                        act.wait_ge(laid[1], 96 * (pr - 1))
                                    qk_high(act, par, j)
                                if not s.even and j < 2 and s.v:
                                    pr, par = 2 * s.it + s.k // 2 + 1, (s.k // 2 + 1) % 2
                                    act.wait_ge(v_ps, 2 * pr + j + 1)
                                    if st == JOB[0] and not (s.first or (s.zero and s.k == 1)):
                                        act.wait_ge(pv_ps, TT * (s.g - 1))
                                    if st == JOB[0] and s.first:
                                        act.wait_ge(ones_set, 2)
                                    act.activation(v_hi[:, par, 4 * j:4 * j + 4, :, 0:HD],
                                                   ps[:, JOB_BANK[j], :].rearrange("p (t a d) -> p t a d", t=4, a=2),
                                                   ACT.Copy, scale=KV_SHIFT).then_inc(v_hi_done, 1)
                                if not s.even and j >= 2 and s.y:
                                    pr, par = 2 * s.it + s.k // 2 - 1, (s.k // 2 - 1) % 2
                                    half = j - 2
                                    act.wait_ge(yT_ps, 2 * pr + half + 1)
                                    if not (s.zero and s.k == 3):
                                        act.wait_ge(y_out[1 - par], 32 * s.it)
                                    act.activation(y_sp[:, par, half, 0, :], ps[:, JOB_BANK[j], :],
                                                   ACT.Copy).then_inc(yT_hi, 1)

                    slots(act, slot)

                @block.vector
                def _(dve):
                    def normalise(s_it, k, chunk):
                        h = 4 * s_it + k
                        par, a = (k // 2) % 2, k % 2
                        o = ps[:, O_BANK + chunk, 0:4 * (HD + 1)].rearrange("p (t d) -> p t d", t=4)
                        dve.wait_ge(pv_ps, TT * h + 4 * (chunk + 1))
                        dve.reciprocal(rsum[:, chunk, :], o[:, :, HD]).then_inc(recip, 1)
                        dve.wait_ge(recip, 2 * h + chunk + 1)
                        dve.tensor_tensor(y_st[:, par, 4 * chunk:4 * chunk + 4, HD * a:HD * (a + 1)], o[:, :, 0:HD],
                                          rsum[:, chunk, :].unsqueeze(2).broadcast_to([P, 4, HD]),
                                          ALU.mult).then_inc(y_norm, 1)

                    def slot(s):
                        e = s.k % 2
                        for st in range(NS):
                            if s.maxima:
                                h, me = s.g + 2, s.k % 2
                                t, half = MSTEPS[st]
                                w = min(BANK, P * (t + 1) - BANK * half)
                                dve.wait_ge(mx_ps, NS * h + st + 1)
                                if st == 0 and not s.first:
                                    dve.wait_ge(mx_comb, h - 1)
                                if half == t // 4:
                                    dve.sem_inc(scores_seen, 1)
                                    dve.tensor_tensor_reduce(masked_scores[:, st % 2, 0:w], ps[:, M_BANK + st % 2, 0:w],
                                                             causal[:, BANK - w:BANK], 1.0, MASKED, ALU.add, ALU.max,
                                                             row_max[:, me, half, t:t + 1]).then_inc(mx_red, 1)
                                else:
                                    dve.tensor_reduce(row_max[:, me, half, t:t + 1], ps[:, M_BANK + st % 2, 0:w], AX_X,
                                                      ALU.max).then_inc(mx_red, 1)
                            if s.score and st in LO_STEP:
                                f = DVE_LO[LO_STEP.index(st)]
                                span = slice(at[f], at[f] + width[f])
                                dve.wait_ge(sc_exp, NS * s.g + f + 1)
                                if f == DVE_LO[0] and not (s.zero and s.k < 2):
                                    dve.wait_ge(pv_ps, TT * (s.g - 1))
                                dve.tensor_tensor(prob_lo[:, e, span], prob[:, e, span],
                                                  prob[:, e, :].bitcast(BF16)[:, 2 * at[f] + 1:2 * (at[f] + width[f]):2],
                                                  ALU.subtract).then_inc(lo_dve, 1)
                            if st == 1 and ((not s.first and not s.zero and not s.tail) or (s.zero and s.k >= 2)
                                            or (s.tail and s.k < 2)):
                                kk = s.k - 2
                                normalise(s.it + (kk // 4), kk % 4, 1)
                            if st == 4 and s.pv:
                                kk = s.k - 1
                                normalise(s.it + (kk // 4), kk % 4, 0)
                            if st - 1 in JOB and st - 1 != JOB[1]:
                                j = (0, None, 1, 2, 3)[JOB.index(st - 1)]
                                if s.even and s.qk:
                                    pr, par = 2 * s.it + s.k // 2 + 2, (s.k // 2) % 2
                                    dve.wait_ge(qk_hi, 4 * pr + j + 1)
                                    qk_low(dve, par, j)
                                if not s.even and j < 2 and s.v:
                                    pr, par = 2 * s.it + s.k // 2 + 1, (s.k // 2 + 1) % 2
                                    dve.wait_ge(v_hi_done, 2 * pr + j + 1)
                                    for a in range(2):
                                        ins = dve.scalar_tensor_tensor(
                                            v_lo[:, par, 4 * j:4 * j + 4, a, :],
                                            ps[:, JOB_BANK[j], :].rearrange("p (t a d) -> p t a d", t=4, a=2)[:, :, a, :],
                                            KV_SHIFT, v_hi[:, par, 4 * j:4 * j + 4, a, 0:HD], ALU.mult, ALU.subtract)
                                    ins.then_inc(v_lo_done, 1)
                                if not s.even and j >= 2 and s.y:
                                    pr, par = 2 * s.it + s.k // 2 - 1, (s.k // 2 - 1) % 2
                                    half = j - 2
                                    dve.wait_ge(yT_hi, 2 * pr + half + 1)
                                    dve.tensor_tensor(y_sp[:, par, half, 1, :], ps[:, JOB_BANK[j], :],
                                                      y_sp[:, par, half, 0, :], ALU.subtract).then_inc(yT_lo, 1)
                        if s.maxima:
                            h, me = s.g + 2, s.k % 2
                            dve.wait_ge(mx_red, NS * (h + 1))
                            if not s.first:
                                dve.wait_ge(mxT_ps, h - 1)
                            if s.first:
                                dve.wait_ge(ones_set, 3)
                            dve.tensor_tensor(row_max_all[:, me, :], row_max[:, me, 0, :], row_max[:, me, 1, :],
                                              ALU.max).then_inc(mx_comb, 1)

                    slots(dve, slot)

                @block.tensor
                def _(pe):
                    def score_step(s, st):
                        c, kt = STEPS[st]
                        r = s.k % 4
                        keys = slice(P * kt, P * (kt + 1))
                        qs = slice(q_from[st], q_from[st] + width[st])
                        dst = ps[:, S_BANK + st % 2, 0:width[st]]
                        if st == 0:
                            pe.wait_ge(mx_row, 16 * (s.g + 1))
                        if not (s.zero and s.k == 0 and st < 2):
                            pe.wait_ge(sc_exp, NS * s.g + st - 1)
                        pe.matmul(dst, k1[:, r, keys], q1[:, r, qs], start=True, stop=False)
                        pe.matmul(dst, k2[0:HD + 1, r, keys], q2[0:HD + 1, r, qs], start=False,
                                  stop=True).then_inc(sc_ps, 1)

                    def max_step(s, st):
                        h, r = s.g + 2, (s.k + 2) % 4
                        t, half = MSTEPS[st]
                        w = min(BANK, P * (t + 1) - BANK * half)
                        dst = ps[:, M_BANK + st % 2, 0:w]
                        if st == 0:
                            pe.wait_ge(laid[s.k % 2], 96 * (2 * s.it + (s.k + 2) // 2 + 1))
                        if not (s.first and s.k == 2 and st < 2):
                            pe.wait_ge(mx_red, NS * h + st - 1)
                        pe.matmul(dst, q1[:, r, P * t:P * (t + 1)], k1[:, r, BANK * half:BANK * half + w],
                                  start=True, stop=True).then_inc(mx_ps, 1)

                    def pv_blocks(s, st):
                        kk = (s.k - 1) % 4
                        it = s.it + (s.k - 1) // 4
                        h = 4 * it + kk
                        e, par, a = kk % 2, (kk // 2) % 2, kk % 2
                        tri = [(t, kt) for t in range(TT) for kt in range(t + 1)]
                        for t, kt in tri[3 * st:3 * st + 3]:
                            if t == 0:
                                pe.wait_ge(v_lo_done, 2 * (2 * it + kk // 2) + 2)
                            if kt == 0:
                                pe.wait_ge(lo_pool, NPL * h + POOL_LO.index(DIAG[t]) + 1)
                                if t == 4:
                                    pe.wait_ge(lo_dve, NVL * (h + 1))
                                if t % 4 == 0 and not (s.zero and s.k == 1):
                                    pe.wait_ge(y_norm, 2 * (h - 1) + t // 4 + 1)
                            b = STEPS.index((t // 4, kt))
                            o = at[b] + P * t - q_from[b]
                            dst = ps[:, O_BANK + t // 4, (HD + 1) * (t % 4):(HD + 1) * (t % 4 + 1)]
                            p_hi = prob[:, e, :].bitcast(BF16)[:, 2 * o + 1:2 * (o + P):2]
                            pe.matmul(dst, p_hi, v_hi[:, par, kt, a, :], start=(kt == 0), stop=False)
                            pe.matmul(dst[:, 0:HD], p_hi, v_lo[:, par, kt, a, :], start=False, stop=False)
                            ins = pe.matmul(dst, prob_lo[:, e, o:o + P], v_hi[:, par, kt, a, :], start=False,
                                            stop=(kt == t))
                            if kt == t:
                                ins.then_inc(pv_ps, 1)

                    QK_PARTS = {0: (0, 0, 3), 1: (0, 3, 6), 4: (1, 0, 3), 5: (1, 3, 6),
                                6: (2, 0, 2), 7: (2, 2, 3), 9: (3, 0, 2), 10: (3, 2, 3)}
                    V_PARTS = {0: (0, 0, 2), 1: (0, 2, 4), 4: (1, 0, 2), 5: (1, 2, 4)}

                    def job(s, st):
                        if st == JOB[1]:
                            if s.row:
                                h = s.g + 1
                                pe.wait_ge(mx_comb, h + 1)
                                if s.even and not s.first and not (s.zero and s.k <= 2):
                                    pe.wait_ge(yT_lo, 2 * (2 * s.it + s.k // 2 - 2) + 2)
                                elif s.even:
                                    pe.wait_ge(v_lo_done, 2 * (2 * s.it + s.k // 2) + 2)
                                elif s.qk_before:
                                    pe.wait_ge(qk_lo, 4 * (2 * s.it + s.k // 2 + 2) + 4)
                                else:
                                    pe.wait_ge(mxT_out, h)
                                pe.transpose(ps[0:TT, J_BANK, 0:P], row_max_all[:, (s.k + 1) % 2, :],
                                             ident[:, :]).then_inc(mxT_ps, 1)
                        if s.even and s.qk and st in QK_PARTS:
                            j, first, last = QK_PARTS[st]
                            pr = 2 * s.it + s.k // 2 + 2
                            if j == 0 and first == 0:
                                if s.first:
                                    pe.wait_ge(qk_lo, 4)
                                elif s.zero and s.k <= 2:
                                    pe.wait_ge(v_lo_done, 2 * (2 * s.it + s.k // 2) + 1)
                                else:
                                    pe.wait_ge(yT_lo, 2 * (2 * s.it + s.k // 2 - 2) + 1)
                            if j == 1 and first == 0 and s.row:
                                pe.wait_ge(mxT_out, s.g + 2)
                            if j >= 2 and first == 0:
                                pe.wait_ge(qk_lo, 4 * pr + j - 1)
                            project(pe, pr, j, first, last)
                        if not s.even and s.v and st in V_PARTS:
                            j, first, last = V_PARTS[st]
                            pr = 2 * s.it + s.k // 2 + 1
                            b_, hp = batch_and_pair(pr)
                            if j == 0 and first == 0:
                                if s.qk_before:
                                    pe.wait_ge(qk_lo, 4 * (2 * s.it + s.k // 2 + 2) + 3)
                                else:
                                    pe.wait_ge(yT_lo, 2 * (2 * s.it + s.k // 2 - 2) + 1)
                            if j == 1 and first == 0:
                                pe.wait_ge(mxT_out, s.g + 2)
                            lat_half = [latT[:, ll, bass.ds(b_ * T + BANK * j, BANK)] for ll in range(2)]
                            w_v = [wkvu[:, vl, bass.ds(hp * P + NH * HD, P)] for vl in range(2)]
                            for t in range(first, last):
                                n = 0
                                for vl, ll in PASSES:
                                    ins = pe.matmul(ps[:, JOB_BANK[j], P * t:P * (t + 1)],
                                                    lat_half[ll][:, P * t:P * (t + 1)], w_v[vl],
                                                    start=(n == 0), stop=(n == 2))
                                    n += 1
                            if last == 4:
                                ins.then_inc(v_ps, 1)
                        if not s.even and st in JOB[3:] and s.y:
                            pr, par = 2 * s.it + s.k // 2 - 1, (s.k // 2 - 1) % 2
                            half = JOB.index(st) - 3
                            pe.wait_ge(y_norm, 4 * pr + 4)
                            if s.v:
                                pe.wait_ge(v_lo_done, 2 * (2 * s.it + s.k // 2 + 1) + 1 + half)
                            else:
                                pe.wait_ge(yT_lo, 2 * pr - 1 + half)
                                if half:
                                    pe.wait_ge(mxT_out, NHEADS)
                            for t in range(4):
                                ins = pe.transpose(ps[:, JOB_BANK[2 + half], P * t:P * (t + 1)],
                                                   y_st[:, par, 4 * half + t, :], ident[:, :])
                            ins.then_inc(yT_ps, 1)

                    def slot(s):
                        s.qk_before = not s.even and not s.last and not s.tail
                        for st in range(NS):
                            if s.score:
                                score_step(s, st)
                            job(s, st)
                            if s.maxima:
                                max_step(s, st)
                            if s.pv:
                                pv_blocks(s, st)

                    slots(pe, slot)

        with ExitStack() as fin:
            wo_s = wo.rearrange("p (l k n) -> p l k n", l=2, k=KH)
            wf_s = wq[:, :, :, :]
            wp_s = wkvu[:, :, :].rearrange("p l (k n) -> p l k n", k=KH)
            resid = sb(fin, "resid", [P, 2, 4, C], F32)
            h2 = sb(fin, "h2", [P, 2, 4, C], F32)
            st2 = sb(fin, "st2", [P, 2, 4, 6], F32)
            mv2 = sb(fin, "mv2", [P, 2, 4, 2], F32)
            var2 = sb(fin, "var2", [P, 2, 4], F32)
            std2 = sb(fin, "std2", [P, 2, 4], F32)
            rstd2 = sb(fin, "rstd2", [P, 2, 4], F32)
            tmp2 = sb(fin, "tmp2", [P, 2, 4], F32)
            xn2 = sb(fin, "xn2", [P, 2, 4, C], F32)
            x2T = sb(fin, "x2T", [P, 2, 2, KC, BANK], F16)
            relu = sb(fin, "relu", [P, 2, BANK], F32)
            r_sq = sb(fin, "r_sq", [P, 2, BANK], F32)
            rT = sb(fin, "rT", [P, 2, 2, KH, BANK], F16)
            row_scale = sb(fin, "row_scale", [P, KH + KC], F32)
            half_scale = sb(fin, "half_scale", [P, KH + KC], F32)
            minus_half = sb(fin, "minus_half", [P, KH + KC], F32)
            top2 = sb(fin, "top2", [P, 2], F32)
            top2_all = sb(fin, "top2_all", [P, 2], F32)
            spare = rT[:, :, :, :, :].rearrange("p a l k n -> p (a l k n)").bitcast(F32)
            fc_above, fc_t, pr_above, pr_t = (spare[:, n * KH * C:(n + 1) * KH * C] for n in range(4))
            FC_ROWS, PR_ROWS = slice(0, KH), slice(KH, KH + KC)

            resid_in = [sem("resid_in_even"), sem("resid_in_odd")]
            w_step = sem("w_step")
            pr_tern = sem("pr_tern")
            pr_step = sem("pr_step")
            pr_whole = sem("pr_whole")
            pr_scaled = sem("pr_scaled")
            prT_ps = sem("prT_ps")
            prT_hi = sem("prT_hi")
            prT_lo = sem("prT_lo")
            pr_top = sem("pr_top")
            fc_top = sem("fc_top")
            top2_shared = sem("top2_shared")
            low_rank = sem("low_rank")
            fc_full = sem("fc_full")
            pr_winv = sem("pr_winv")
            fc_winv = sem("fc_winv")
            fcT_ps = sem("fcT_ps")
            fcT_hi = sem("fcT_hi")
            fcT_lo = sem("fcT_lo")
            att_ps = sem("att_ps")
            h2_done = sem("h2_done")
            ln_step = sem("ln_step")
            stats_seen = sem("stats_seen")
            var2_ready = sem("var2_ready")
            std2_ready = sem("std2_ready")
            xn2_ready = sem("xn2_ready")
            ln_last = sem("ln_last")
            x2T_ps = sem("x2T_ps")
            x2T_hi = sem("x2T_hi")
            x2T_lo = sem("x2T_lo")
            fc_ps = sem("fc_ps")
            relu_done = sem("relu_done")
            sq_done = sem("sq_done")
            r_hi = sem("r_hi")
            r_lo = sem("r_lo")
            out_ps = sem("out_ps")
            res_done = sem("res_done")
            out_sent = [sem("out_sent_even"), sem("out_sent_odd")]
            FC_BANK, AT_BANK, PR_BANK, XT_BANK = 0, 2, 4, 6

            def half_of(i):
                return i // 2 if isinstance(i, int) else i >> 1

            def groups(eng, start, run):
                start()
                for par in range(2):
                    run(par, 0, par, par == 0, False)
                with eng.Fori(1, GROUPS // 2 - 1) as it:
                    for par in range(2):
                        run(2 * it + par, it, par, False, False)
                for par in range(2):
                    run(GROUPS - 2 + par, GROUPS // 2 - 1, par, False, par == 1)

            with nc.Block() as block:
                @block.sync
                def _(sp):
                    def load_resid(i, par):
                        e_src = embed_scr.rearrange("(g j p) c -> g p j c", j=4, p=P)
                        e_src = e_src[i] if isinstance(i, int) else \
                            e_src[bass.ds(i, 1)].rearrange("a p j c -> p (a j) c")
                        sp.dma_start(resid[:, par, :, :], e_src).then_inc(resid_in[par], 16)

                    def load(i, par):
                        sp.wait_ge(att_ps, 4 * (i - 1))
                        sp.wait_ge(h2_done, 4 * (i - 1))
                        src = y_scr.rearrange("b h p k n -> (b h) p k n")[bass.ds(i, 1)] \
                            .rearrange("a p k n -> p (a k) n")
                        sp.dma_start(yT[par].rearrange("p k l n -> p k (l n)"), src).then_inc(yT_in[par], 16)
                        load_resid(i, par)

                    def start():
                        load_resid(0, 0)
                        load_resid(1, 1)
                        sp.wait_ge(y_out[0], 32 * (NHEADS // 4))
                        sp.wait_ge(y_out[1], 32 * (NHEADS // 4))

                    def run(i, half, par, first, last):
                        if not isinstance(i, int) or i + 2 < GROUPS:
                            load(i + 2, par)
                        sp.wait_ge(res_done, 4 * (i + 1))
                        o_dst = out.rearrange("b (h j p) c -> (b h) p j c", j=4, p=P)
                        o_dst = o_dst[i] if isinstance(i, int) else \
                            o_dst[bass.ds(i, 1)].rearrange("a p j c -> p (a j) c")
                        sp.dma_start(o_dst, res[:, par, :, :]).then_inc(out_sent[par], 16)

                    groups(sp, start, run)
                    sp.wait_ge(out_sent[0], 16 * (GROUPS // 2))
                    sp.wait_ge(out_sent[1], 16 * (GROUPS // 2))

                @block.gpsimd
                def _(pool):
                    def start():
                        pool.wait_ge(pr_top, 1)
                        pool.partition_all_reduce(top2_all[:, 1:2], top2[:, 1:2], P,
                                                  bass.bass_isa.ReduceOp.max).then_inc(top2_shared, 1)
                        w = wpr_f.rearrange("p k n -> p (k n)")
                        pool.wait_ge(pr_tern, 1)
                        pool.tensor_tensor(pr_t, w, pr_t, ALU.add).then_inc(pr_step, 1)
                        pool.wait_ge(pr_step, 1)
                        pool.tensor_tensor(pr_t, w, pr_t, ALU.subtract).then_inc(pr_whole, 1)
                        pool.wait_ge(fc_top, 1)
                        pool.partition_all_reduce(top2_all[:, 0:1], top2[:, 0:1], P,
                                                  bass.bass_isa.ReduceOp.max).then_inc(top2_shared, 1)

                    def run(i, half, par, first, last):
                        for jt in range(KH):
                            pool.wait_ge(relu_done, KH * i + jt + 1)
                            if not (first and jt < 2):
                                pool.wait_ge(r_hi, KH * i + jt - 1)
                                pool.wait_ge(r_lo, KH * i + jt - 1)
                            pool.tensor_tensor(r_sq[:, jt % 2, :], relu[:, jt % 2, :], relu[:, jt % 2, :],
                                               ALU.mult).then_inc(sq_done, 1)

                    groups(pool, start, run)

                @block.scalar
                def _(act):
                    def high(i, par, first):
                        for k in range(KC):
                            act.wait_ge(x2T_ps, KC * i + k + 1)
                            if k == 0 and not first:
                                act.wait_ge(fc_ps, KH * (i - 1))
                            act.activation(x2T[:, par, 0, k, :], ps[:, XT_BANK + k, :], ACT.Copy).then_inc(x2T_hi, 1)

                    def root(i, par):
                        act.wait_ge(var2_ready, i + 1)
                        act.activation(std2[:, par, :], var2[:, par, :], ACT.Sqrt).then_inc(std2_ready, 1)

                    def start():
                        act.wait_ge(pr_whole, 1)
                        for k in range(KC):
                            act.activation(wpr_f[:, k, :], pr_t[:, HID * k:HID * (k + 1)], ACT.Copy,
                                           scale=row_scale[:, KH + k:KH + k + 1]).then_inc(pr_scaled, 1)
                        act.wait_ge(pr_winv, 1)
                        for n in range(2):
                            act.wait_ge(prT_ps, n + 1)
                            act.activation(wp_s[:, 0, 4 * n:4 * n + 4, :].rearrange("p (b h) n -> p b (h n)", b=2),
                                           ps[:, XT_BANK:XT_BANK + 2, :], ACT.Copy,
                                           scale=winv[:, WP:WP + 1]).then_inc(prT_hi, 1)
                        root(0, 0)
                        act.wait_ge(fc_winv, 1)
                        for k, bank in enumerate((FC_BANK, PR_BANK)):
                            act.wait_ge(fcT_ps, k + 1)
                            act.activation(wf_s[:, 0, k, :].rearrange("p (b n) -> p b n", b=2), ps[:, bank:bank + 2, :],
                                           ACT.Copy, scale=winv[:, WF:WF + 1]).then_inc(fcT_hi, 1)
                        high(0, 0, True)

                    def run(i, half, par, first, last):
                        def r_high(jt):
                            act.wait_ge(sq_done, KH * i + jt + 1)
                            if jt == 0 and not (isinstance(i, int) and i < 2):
                                act.wait_ge(out_ps, 4 * (i - 1))
                            act.activation(rT[:, par, 0, jt, :], r_sq[:, jt % 2, :], ACT.Copy).then_inc(r_hi, 1)

                        for jt in range(KH):
                            act.wait_ge(fc_ps, KH * i + jt + 1)
                            if not (first and jt < 2):
                                act.wait_ge(sq_done, KH * i + jt - 1)
                            act.activation(relu[:, jt % 2, :], ps[:, FC_BANK + jt % 2, :], ACT.Relu,
                                           scale=H_SHIFT).then_inc(relu_done, 1)
                            if jt:
                                r_high(jt - 1)
                        r_high(KH - 1)
                        if not last:
                            root(i + 1, 1 - par)
                            high(i + 1, 1 - par, first)

                    groups(act, start, run)

                @block.vector
                def _(dve):
                    LN = 6
                    w_steps = [0]

                    def then(ins):
                        w_steps[0] += 1
                        ins.then_inc(w_step, 1)
                        dve.wait_ge(w_step, w_steps[0])

                    def residual(i, j, par, first):
                        dve.wait_ge(att_ps, 4 * i + j + 1)
                        if j == 0:
                            dve.wait_ge(resid_in[par], 16 * (half_of(i) + 1))
                            if not first:
                                dve.wait_ge(res_done, 4 * (i - 1))
                        dve.scalar_tensor_tensor(h2[:, par, j, :], ps[:, AT_BANK + j % 2, 0:C], coef[:, 1:2],
                                                 resid[:, par, j, :], ALU.mult, ALU.add).then_inc(h2_done, 1)

                    def norm2(i, par):
                        dve.wait_ge(h2_done, 4 * i + 4)
                        for j in range(4):
                            ins = dve.bn_stats(st2[:, par, j, :], h2[:, par, j, :])
                        ins.then_inc(ln_step, 1)
                        dve.wait_ge(ln_step, LN * i + 1)
                        dve.sem_inc(stats_seen, 1)
                        for j in range(4):
                            ins = dve.bn_aggr(mv2[:, par, j, :], st2[:, par, j, :])
                        ins.then_inc(ln_step, 1)
                        dve.wait_ge(ln_step, LN * i + 2)
                        dve.tensor_scalar(var2[:, par, :], mv2[:, par, :, 1], EPS, None, ALU.add).then_inc(var2_ready, 1)
                        dve.wait_ge(std2_ready, i + 1)
                        dve.reciprocal(rstd2[:, par, :], std2[:, par, :]).then_inc(ln_step, 1)
                        dve.wait_ge(ln_step, LN * i + 3)
                        dve.tensor_tensor(tmp2[:, par, :], rstd2[:, par, :], rstd2[:, par, :], ALU.mult) \
                            .then_inc(ln_step, 1)
                        dve.wait_ge(ln_step, LN * i + 4)
                        dve.tensor_tensor(tmp2[:, par, :], tmp2[:, par, :], var2[:, par, :], ALU.mult) \
                            .then_inc(ln_step, 1)
                        dve.wait_ge(ln_step, LN * i + 5)
                        dve.tensor_scalar(tmp2[:, par, :], tmp2[:, par, :], -0.5 * X_SCALE, 1.5 * X_SCALE, ALU.mult,
                                          ALU.add).then_inc(ln_step, 1)
                        dve.wait_ge(ln_step, LN * i + 6)
                        dve.tensor_tensor(rstd2[:, par, :], rstd2[:, par, :], tmp2[:, par, :], ALU.mult) \
                            .then_inc(ln_last, 1)
                        dve.wait_ge(ln_last, i + 1)
                        for j in range(4):
                            if j == 0 and not (isinstance(i, int) and i < 2):
                                dve.wait_ge(x2T_ps, KC * (i - 1))
                            ins = dve.tensor_scalar(xn2[:, par, j, :], h2[:, par, j, :], mv2[:, par, j, 0:1],
                                                    rstd2[:, par, j:j + 1], ALU.subtract, ALU.mult)
                        ins.then_inc(xn2_ready, 1)

                    def low(i, par):
                        for k in range(KC):
                            dve.wait_ge(x2T_hi, KC * i + k + 1)
                            dve.tensor_tensor(x2T[:, par, 1, k, :], ps[:, XT_BANK + k, :], x2T[:, par, 0, k, :],
                                              ALU.subtract).then_inc(x2T_lo, 1)

                    def row_scales(w, rows):
                        s = row_scale[:, rows]
                        then(dve.tensor_reduce(s, w, AX_X, ALU.add, apply_absolute_value=True))
                        then(dve.tensor_scalar(s, s, 1.0 / w.shape[2], EPS, ALU.mult, ALU.max))
                        dve.tensor_scalar(half_scale[:, rows], s, 0.5, None, ALU.mult)
                        then(dve.tensor_scalar(minus_half[:, rows], s, -0.5, None, ALU.mult))

                    def is_above(w, rows, above):
                        n, row = w.shape[1], w.shape[2]
                        then(dve.tensor_tensor(above.rearrange("p (n r) -> p n r", n=n), w,
                                               half_scale[:, rows].unsqueeze(2).broadcast_to([P, n, row]), ALU.is_gt))

                    def minus_ternary(w, rows, above, t):
                        n, row = w.shape[1], w.shape[2]
                        for k in range(n):
                            r = rows.start + k
                            ins = dve.scalar_tensor_tensor(t[:, row * k:row * (k + 1)], w[:, k, :], minus_half[:, r:r + 1],
                                                           above[:, row * k:row * (k + 1)], ALU.is_lt, ALU.subtract)
                        return ins

                    def exponent(m, col):
                        c, m_ = slice(m, m + 1), slice(col, col + 1)
                        then(dve.tensor_single_scalar(pow2[:, c].bitcast(I32), top2_all[:, m_].bitcast(I32),
                                                      EXP_BITS, ALU.bitwise_and))
                        then(dve.tensor_scalar(pow2[:, c], pow2[:, c], 2.0 ** -30, None, ALU.max))
                        then(dve.reciprocal(winv[:, c], pow2[:, c]))
                        return dve.tensor_scalar(winv[:, c], winv[:, c], W_TOP, None, ALU.mult)

                    def proj_low(n):
                        dve.wait_ge(prT_hi, n + 1)
                        dve.scalar_tensor_tensor(wp_s[:, 1, 4 * n:4 * n + 4, :].rearrange("p (b h) n -> p b (h n)", b=2),
                                                 ps[:, XT_BANK:XT_BANK + 2, :], winv[:, WP:WP + 1],
                                                 wp_s[:, 0, 4 * n:4 * n + 4, :].rearrange("p (b h) n -> p b (h n)", b=2),
                                                 ALU.mult, ALU.subtract).then_inc(prT_lo, 1)

                    def fc_low(k):
                        bank = (FC_BANK, PR_BANK)[k]
                        dve.wait_ge(fcT_hi, k + 1)
                        dve.scalar_tensor_tensor(wf_s[:, 1, k, :].rearrange("p (b n) -> p b n", b=2),
                                                 ps[:, bank:bank + 2, :], winv[:, WF:WF + 1],
                                                 wf_s[:, 0, k, :].rearrange("p (b n) -> p b n", b=2),
                                                 ALU.mult, ALU.subtract).then_inc(fcT_lo, 1)

                    def start():
                        dve.wait_ge(ffn_w, 48)
                        row_scales(wpr_f, PR_ROWS)
                        dve.tensor_reduce(top2[:, 1:2], row_scale[:, PR_ROWS], AX_X, ALU.max).then_inc(pr_top, 1)
                        is_above(wpr_f, PR_ROWS, pr_above)
                        minus_ternary(wpr_f, PR_ROWS, pr_above, pr_t).then_inc(pr_tern, 1)
                        dve.wait_ge(top2_shared, 1)
                        exponent(WP, 1).then_inc(pr_winv, 1)
                        row_scales(wfc_f, FC_ROWS)
                        residual(0, 0, 0, True)
                        is_above(wfc_f, FC_ROWS, fc_above)
                        residual(0, 1, 0, True)
                        then(minus_ternary(wfc_f, FC_ROWS, fc_above, fc_t))
                        residual(0, 2, 0, True)
                        w_all = wfc_f.rearrange("p k c -> p (k c)")
                        then(dve.tensor_tensor(fc_t, w_all, fc_t, ALU.add))
                        residual(0, 3, 0, True)
                        then(dve.tensor_tensor(fc_t, w_all, fc_t, ALU.subtract))
                        dve.wait_ge(low_rank, 1)
                        for k in range(KH):
                            bank = (FC_BANK, PR_BANK)[k // 4] + (k % 4) // 2
                            ins = dve.scalar_tensor_tensor(wfc_f[:, k, :], fc_t[:, C * k:C * (k + 1)],
                                                           row_scale[:, k:k + 1],
                                                           ps[:, bank, C * (k % 2):C * (k % 2 + 1)],
                                                           ALU.mult, ALU.add)
                        ins.then_inc(fc_full, 1)
                        dve.wait_ge(pr_winv, 1)
                        proj_low(0)
                        residual(1, 0, 1, True)
                        dve.wait_ge(fc_full, 1)
                        dve.tensor_reduce(top2[:, 0:1], wfc_f, mybir.AxisListType.XY, ALU.max,
                                          apply_absolute_value=True).then_inc(fc_top, 1)
                        residual(1, 1, 1, True)
                        proj_low(1)
                        dve.wait_ge(top2_shared, 2)
                        exponent(WF, 0).then_inc(fc_winv, 1)
                        dve.wait_ge(fc_winv, 1)
                        norm2(0, 0)
                        residual(1, 2, 1, True)
                        residual(1, 3, 1, True)
                        fc_low(0)
                        fc_low(1)
                        then(dve.tensor_tensor(coef[:, 2:3], pow2[:, WF:WF + 1], pow2[:, WF:WF + 1], ALU.mult))
                        then(dve.scalar_tensor_tensor(coef[:, 2:3], pow2[:, WP:WP + 1], 0.25, coef[:, 2:3],
                                                      ALU.mult, ALU.mult))
                        low(0, 0)

                    def run(i, half, par, first, last):
                        for jt in range(KH):
                            dve.wait_ge(r_hi, KH * i + jt + 1)
                            dve.tensor_tensor(rT[:, par, 1, jt, :], r_sq[:, jt % 2, :], rT[:, par, 0, jt, :],
                                              ALU.subtract).then_inc(r_lo, 1)
                        if not last:
                            if not first:
                                for j in range(4):
                                    residual(i + 1, j, 1 - par, False)
                            norm2(i + 1, 1 - par)
                        for j in range(4):
                            dve.wait_ge(out_ps, 4 * i + j + 1)
                            if j == 0 and not (isinstance(i, int) and i < 2):
                                dve.wait_ge(out_sent[par], 16 * half)
                            dve.scalar_tensor_tensor(res[:, par, j, :], ps[:, PR_BANK + j % 2, 0:C], coef[:, 2:3],
                                                     h2[:, par, j, :], ALU.mult, ALU.add).then_inc(res_done, 1)
                            if j == 1 and not last:
                                low(i + 1, 1 - par)

                    groups(dve, start, run)

                @block.tensor
                def _(pe):
                    def attention_out(i, par, j, first):
                        if j == 0:
                            pe.wait_ge(yT_in[par], 16 * (half_of(i) + 1))
                        if not (first and j < 2):
                            pe.wait_ge(h2_done, 4 * i + j - 1)
                        n = 0
                        for k in range(KH):
                            for yl, wl in ((0, 0), (0, 1), (1, 0)):
                                ins = pe.matmul(ps[:, AT_BANK + j % 2, 0:C], yT[par][:, k, yl, P * j:P * (j + 1)],
                                                wo_s[:, wl, k, :], start=(n == 0), stop=(n == 3 * KH - 1))
                                n += 1
                        ins.then_inc(att_ps, 1)

                    def turn(i, par, first):
                        pe.wait_ge(xn2_ready, i + 1)
                        for k in range(KC):
                            if not first:
                                pe.wait_ge(x2T_lo, KC * (i - 1) + k + 1)
                            for j in range(4):
                                ins = pe.transpose(ps[:, XT_BANK + k, P * j:P * (j + 1)],
                                                   xn2[:, par, j, P * k:P * (k + 1)], ident[:, :])
                            ins.then_inc(x2T_ps, 1)

                    def proj_turn(n):
                        pe.wait_ge(pr_scaled, KC)
                        if n:
                            pe.wait_ge(prT_lo, n)
                        for h in range(4 * n, 4 * n + 4):
                            for k in range(KC):
                                c = C * (h % 2) + P * k
                                ins = pe.transpose(ps[:, XT_BANK + (h % 4) // 2, c:c + P],
                                                   wpr_f[:, k, P * h:P * (h + 1)], ident[:, :])
                        ins.then_inc(prT_ps, 1)

                    def start():
                        for k in range(KH):
                            bank = (FC_BANK, PR_BANK)[k // 4] + (k % 4) // 2
                            ins = pe.matmul(ps[:, bank, C * (k % 2):C * (k % 2 + 1)], uT[:, P * k:P * (k + 1)],
                                            fbv[:, :], start=True, stop=True)
                        ins.then_inc(low_rank, 1)
                        pe.wait_ge(ffn_w, 48)
                        for j in range(4):
                            attention_out(0, 0, j, True)
                        proj_turn(0)
                        attention_out(1, 1, 0, False)
                        attention_out(1, 1, 1, False)
                        proj_turn(1)
                        attention_out(1, 1, 2, False)
                        attention_out(1, 1, 3, False)
                        pe.wait_ge(fc_full, 1)
                        for k, bank in enumerate((FC_BANK, PR_BANK)):
                            for h in range(KH):
                                ins = pe.transpose(ps[:, bank + h // 4, P * (h % 4):P * (h % 4 + 1)],
                                                   wfc_f[:, h, P * k:P * (k + 1)], ident[:, :])
                            ins.then_inc(fcT_ps, 1)
                        pe.wait_ge(prT_lo, 2)
                        turn(0, 0, True)
                        pe.wait_ge(fcT_hi, 2)
                        pe.wait_ge(fcT_lo, 2)

                    def run(i, half, par, first, last):
                        pe.wait_ge(x2T_hi, KC * (i + 1))
                        pe.wait_ge(x2T_lo, KC * (i + 1))
                        for jt in range(KH):
                            if not (first and jt < 2):
                                pe.wait_ge(relu_done, KH * i + jt - 1)
                            n = 0
                            for k in range(KC):
                                for wl, xl in ((0, 0), (0, 1), (1, 0)):
                                    ins = pe.matmul(ps[:, FC_BANK + jt % 2, :], wf_s[:, wl, k, P * jt:P * (jt + 1)],
                                                    x2T[:, par, xl, k, :], start=(n == 0), stop=(n == 3 * KC - 1))
                                    n += 1
                            ins.then_inc(fc_ps, 1)
                        if not last and not first:
                            for j in range(4):
                                attention_out(i + 1, 1 - par, j, False)
                        for j in range(4):
                            if not (first and j < 2):
                                pe.wait_ge(res_done, 4 * i + j - 1)
                            n = 0
                            for jt in range(KH):
                                if j == 0:
                                    pe.wait_ge(r_hi, KH * i + jt + 1)
                                    pe.wait_ge(r_lo, KH * i + jt + 1)
                                for rl, wl in ((0, 0), (0, 1), (1, 0)):
                                    ins = pe.matmul(ps[:, PR_BANK + j % 2, 0:C], rT[:, par, rl, jt, P * j:P * (j + 1)],
                                                    wp_s[:, wl, jt, :], start=(n == 0), stop=(n == 3 * KH - 1))
                                    n += 1
                            ins.then_inc(out_ps, 1)
                            if j == 1 and not last:
                                turn(i + 1, 1 - par, False)

                    groups(pe, start, run)


_INS = ['x', 'L0_tok_weights', 'L0_attn_w_kv_down', 'L0_attn_w_kv_up', 'L0_attn_w_q', 'L0_attn_w_out',
        'L0_ffn_fast_b', 'L0_ffn_w_fc', 'L0_ffn_w_proj', 'L0_ffn_u', 'L0_ffn_v', 'L0_ffn_gate']


def kernel(**inputs):
    import numpy as _np
    import concourse.bacc as _bacc
    from concourse import mybir as _mybir
    from concourse.bass_utils import run_bass_kernel_spmd as _run

    nc = _bacc.Bacc("TRN2", target_bir_lowering=False, num_devices=1)
    arrays, args = {}, []
    for name in _INS:
        a = _np.ascontiguousarray(inputs[name])
        if a.ndim == 0:
            a = a.reshape(1)
        arrays[f"in_{name}_dram"] = a
        args.append(nc.dram_tensor(f"in_{name}_dram", a.shape, _mybir.dt.from_np(a.dtype), kind="ExternalInput").ap())
    shape = tuple(inputs['x'].shape) + (inputs['L0_tok_weights'].shape[1],)
    args.append(nc.dram_tensor("out_0_dram", shape, F32, kind="ExternalOutput").ap())
    layer_kernel(nc, *args)
    r = _run(nc, [arrays], core_ids=[0])
    return r.results[0]["out_0_dram"]
```
